# Optimizing a Trainium2 kernel written in Bass

```python
import numpy as np
import jax
import jax.numpy as jnp

def _softmax(x, axis=-1):
    return jax.nn.softmax(x, axis=axis)

def _gelu(x):
    return jax.nn.gelu(x, approximate=True)

def _silu(x):
    return jax.nn.silu(x)

def _sigmoid(x):
    return jax.nn.sigmoid(x)

def _layernorm(x, axis=-1, eps=1e-05):
    m = jnp.mean(x, axis=axis, keepdims=True)
    v = jnp.var(x, axis=axis, keepdims=True)
    return (x - m) / jnp.sqrt(v + eps)

def _scatter_add(tgt, idx, src, axis=0):
    return tgt.at[idx].add(src)

def _segment_sum(src, seg, n):
    return jax.ops.segment_sum(src, seg, n)
kernel_name = 'mk_cond_resid_d4_seqx_r2_c32cd9'

def setup_inputs(seed: int=0):
    np.random.seed(seed)
    _w = jnp.asarray

    def _rec_inputs():
        import jax
        import jax.numpy as jnp
        _rk = jax.random.key(seed)
        x = 7.22e-05 + 1 * jax.random.normal(jax.random.fold_in(_rk, 1), (2, 2048, 512), jnp.float32)
        _lenS = 2048 - jax.random.randint(jax.random.fold_in(_rk, 7), (2,), 0, max(1, 2048 // 4) + 1, jnp.int32)
        _lenS2 = 2048 - jax.random.randint(jax.random.fold_in(_rk, 8), (2,), 0, max(1, 2048 // 4) + 1, jnp.int32)
        cond_512 = 0.0061147 + 1.02565 * jax.random.normal(jax.random.fold_in(_rk, 11), (2, 256), jnp.float32)
        itok_BxS_0_999 = jax.random.randint(jax.random.fold_in(_rk, 12), (2, 2048), 0, 500, jnp.int32)
        itok_BxS_0_4 = jax.random.randint(jax.random.fold_in(_rk, 13), (2, 2048), 0, 5, jnp.int32)
        cond_64 = 0.0990542 + 1.04422 * jax.random.normal(jax.random.fold_in(_rk, 15), (2, 64), jnp.float32)
        fside_Bx32_0 = -0.136436 + 0.990155 * jax.random.normal(jax.random.fold_in(_rk, 16), (2, 32), jnp.float32)
        _validS = jnp.arange(2048)[None, :] < _lenS[:, None]
        _validS2 = jnp.arange(2048)[None, :] < _lenS2[:, None]
        _causal = jnp.tril(jnp.ones((2048, 2048), dtype=bool))
        mask_BxS_ik0 = jnp.where(jnp.broadcast_to(_validS[:, :], (2, 2048)), 0, 1).astype(jnp.int32)
        return (x, cond_512, itok_BxS_0_999, itok_BxS_0_4, cond_64, fside_Bx32_0, mask_BxS_ik0)
    x, cond_512, itok_BxS_0_999, itok_BxS_0_4, cond_64, fside_Bx32_0, mask_BxS_ik0 = _rec_inputs()

    def _L0_cond_setup():
        import jax, jax.numpy as jnp
        import numpy as np
        import math
        HEAD_NUM = 16
        EPS = 1e-08

        def modulated_linear(x, s, aff_w, aff_b, w, b):
            style = s @ aff_w.T + aff_b
            w_mod = w[None, :, :] * style[:, None, :]
            demod = jax.lax.rsqrt(jnp.sum(w_mod * w_mod, axis=2) + EPS)
            w_mod = w_mod * demod[:, :, None]
            return jnp.einsum('bni,boi->bno', x, w_mod) + b
        key = jax.random.key(seed)
        ks = jax.random.split(key, 6)
        B, N, F, S = (8, 512, 512, 256)
        return {'x': jax.random.normal(ks[0], (B, N, F), dtype=jnp.float32), 's': jax.random.normal(ks[1], (B, S), dtype=jnp.float32), 'k_aff_w': jax.random.normal(ks[2], (F, S), dtype=jnp.float32) * 0.02, 'k_aff_b': jnp.ones((F,), dtype=jnp.float32), 'k_w': jax.random.normal(ks[3], (F, F), dtype=jnp.float32) * 0.02, 'k_b': jnp.zeros((F,), dtype=jnp.float32), 'o_aff_w': jax.random.normal(ks[4], (F, S), dtype=jnp.float32) * 0.02, 'o_aff_b': jnp.ones((F,), dtype=jnp.float32), 'o_w': jax.random.normal(ks[5], (F, F), dtype=jnp.float32) * 0.02, 'o_b': jnp.zeros((F,), dtype=jnp.float32)}
    _L0_cond_all = _L0_cond_setup()
    _L0_cond_in = {k: v for k, v in _L0_cond_all.items() if k in ('k_aff_w', 'k_aff_b', 'k_w', 'k_b', 'o_aff_w', 'o_aff_b', 'o_w', 'o_b')}
    del _L0_cond_all

    def _L1_cond_setup():
        import jax, jax.numpy as jnp
        import numpy as np
        IN_DIM = 512
        OUT_DIM = 512
        MU_DIM = 256
        K = 30
        key = jax.random.key(seed)
        k1, k2, k3, k4, k5 = jax.random.split(key, 5)
        B, S = (16, 1024)
        x = jax.random.normal(k1, (B, S, IN_DIM), dtype=jnp.float32)
        mu = jax.random.normal(k2, (B, MU_DIM), dtype=jnp.float32)
        W_dec = jax.random.normal(k3, (MU_DIM, (IN_DIM + 1) * K), dtype=jnp.float32) / np.sqrt(MU_DIM)
        b_dec = jax.random.normal(k4, ((IN_DIM + 1) * K,), dtype=jnp.float32) * 0.01
        V = jax.random.normal(k5, (K, OUT_DIM), dtype=jnp.float32) / np.sqrt(K)
        return {'x': x, 'mu': mu, 'W_dec': W_dec, 'b_dec': b_dec, 'V': V}
    _L1_cond_all = _L1_cond_setup()
    _L1_cond_in = {k: v for k, v in _L1_cond_all.items() if k in ('W_dec', 'b_dec', 'V')}
    del _L1_cond_all

    def _L2_cond_setup():
        import jax, jax.numpy as jnp
        import numpy as np
        W_DIM = 256
        CLAMP = 256.0
        key = jax.random.key(seed)
        ks = jax.random.split(key, 6)
        B, L, C = (8, 4096, 512)
        return {'x': jax.random.normal(ks[0], (B, L, C), dtype=jnp.float32), 'w': jax.random.normal(ks[1], (B, W_DIM), dtype=jnp.float32), 'weight': jax.random.normal(ks[2], (C, C), dtype=jnp.float32), 'bias': jax.random.normal(ks[3], (C,), dtype=jnp.float32), 'affine_w': jax.random.normal(ks[4], (C, W_DIM), dtype=jnp.float32), 'affine_b': jnp.ones((C,), dtype=jnp.float32)}
    _L2_cond_all = _L2_cond_setup()
    _L2_cond_in = {k: v for k, v in _L2_cond_all.items() if k in ('weight', 'bias', 'affine_w', 'affine_b')}
    del _L2_cond_all

    def _L3_cond_setup():
        import jax, jax.numpy as jnp
        import numpy as np
        EPS = 1e-05

        def _ln(x, g, b):
            m = jnp.mean(x, axis=-1, keepdims=True)
            v = jnp.mean((x - m) ** 2, axis=-1, keepdims=True)
            return (x - m) * jax.lax.rsqrt(v + EPS) * g + b

        def _mlp_ln(s, W1, b1, W2, b2, g, b):
            h = jax.nn.silu(s @ W1 + b1) @ W2 + b2
            return _ln(h, g, b)
        key = jax.random.key(seed)
        B, S, D = (4, 1024, 512)
        MEM, NOI, RES = (256, 64, 32)
        ks = jax.random.split(key, 40)
        ki = iter(range(40))

        def nrm(shape, scale=0.02):
            return jax.random.normal(ks[next(ki)], shape, jnp.float32) * scale

        def gamma(shape):
            return jnp.ones(shape, jnp.float32) + nrm(shape)
        inp = {'x': jax.random.normal(ks[next(ki)], (B, S, D), jnp.float32), 'pathway_ids': jax.random.randint(ks[next(ki)], (B, S), 0, 500), 'compartment_ids': jax.random.randint(ks[next(ki)], (B, S), 0, 5), 'time_steps': jax.random.randint(ks[next(ki)], (B, S), 0, 5), 'scale_type': jax.random.randint(ks[next(ki)], (B, S), 0, 3), 'memory_state': jax.random.normal(ks[next(ki)], (B, MEM), jnp.float32), 'noise_state': jax.random.normal(ks[next(ki)], (B, NOI), jnp.float32), 'resource_state': jax.random.normal(ks[next(ki)], (B, RES), jnp.float32), 'pw_g': gamma((500, D)), 'pw_b': nrm((500, D)), 'cp_g': gamma((5, D)), 'cp_b': nrm((5, D)), 'tm_g': gamma((5, D)), 'tm_b': nrm((5, D)), 'ms_g': gamma((3, D)), 'ms_b': nrm((3, D)), 'mem_W1': nrm((MEM, D)), 'mem_b1': jnp.zeros((D,)), 'mem_W2': nrm((D, D)), 'mem_b2': jnp.zeros((D,)), 'mem_g': gamma((D,)), 'mem_be': jnp.zeros((D,)), 'noi_W1': nrm((NOI, D)), 'noi_b1': jnp.zeros((D,)), 'noi_W2': nrm((D, D)), 'noi_b2': jnp.zeros((D,)), 'noi_g': gamma((D,)), 'noi_be': jnp.zeros((D,)), 'res_W1': nrm((RES, D)), 'res_b1': jnp.zeros((D,)), 'res_W2': nrm((D, D)), 'res_b2': jnp.zeros((D,)), 'res_g': gamma((D,)), 'res_be': jnp.zeros((D,)), 'int_W1': nrm((6 * D, D)), 'int_b1': jnp.zeros((D,)), 'int_W2': nrm((D, D)), 'int_b2': jnp.zeros((D,)), 'int_g': gamma((D,)), 'int_be': jnp.zeros((D,)), 'aw': jnp.ones((6,), jnp.float32) / 6.0}
        return inp
    _L3_cond_all = _L3_cond_setup()
    _L3_cond_in = {k: v for k, v in _L3_cond_all.items() if k in ('pw_g', 'pw_b', 'cp_g', 'cp_b', 'tm_g', 'tm_b', 'ms_g', 'ms_b', 'mem_W1', 'mem_b1', 'mem_W2', 'mem_b2', 'mem_g', 'mem_be', 'noi_W1', 'noi_b1', 'noi_W2', 'noi_b2', 'noi_g', 'noi_be', 'res_W1', 'res_b1', 'res_W2', 'res_b2', 'res_g', 'res_be', 'int_W1', 'int_b1', 'int_W2', 'int_b2', 'int_g', 'int_be', 'aw')}
    del _L3_cond_all
    return {'x': x, 'cond_512': cond_512, 'itok_BxS_0_999': itok_BxS_0_999, 'itok_BxS_0_4': itok_BxS_0_4, 'cond_64': cond_64, 'fside_Bx32_0': fside_Bx32_0, 'mask_BxS_ik0': mask_BxS_ik0, 'L0_cond_k_aff_w': _L0_cond_in['k_aff_w'], 'L0_cond_k_aff_b': _L0_cond_in['k_aff_b'], 'L0_cond_k_w': _L0_cond_in['k_w'], 'L0_cond_k_b': _L0_cond_in['k_b'], 'L0_cond_o_aff_w': _L0_cond_in['o_aff_w'], 'L0_cond_o_aff_b': _L0_cond_in['o_aff_b'], 'L0_cond_o_w': _L0_cond_in['o_w'], 'L0_cond_o_b': _L0_cond_in['o_b'], 'L1_cond_W_dec': _L1_cond_in['W_dec'], 'L1_cond_b_dec': _L1_cond_in['b_dec'], 'L1_cond_V': _L1_cond_in['V'], 'L2_cond_weight': _L2_cond_in['weight'], 'L2_cond_bias': _L2_cond_in['bias'], 'L2_cond_affine_w': _L2_cond_in['affine_w'], 'L2_cond_affine_b': _L2_cond_in['affine_b'], 'L3_cond_pw_g': _L3_cond_in['pw_g'], 'L3_cond_pw_b': _L3_cond_in['pw_b'], 'L3_cond_cp_g': _L3_cond_in['cp_g'], 'L3_cond_cp_b': _L3_cond_in['cp_b'], 'L3_cond_tm_g': _L3_cond_in['tm_g'], 'L3_cond_tm_b': _L3_cond_in['tm_b'], 'L3_cond_ms_g': _L3_cond_in['ms_g'], 'L3_cond_ms_b': _L3_cond_in['ms_b'], 'L3_cond_mem_W1': _L3_cond_in['mem_W1'], 'L3_cond_mem_b1': _L3_cond_in['mem_b1'], 'L3_cond_mem_W2': _L3_cond_in['mem_W2'], 'L3_cond_mem_b2': _L3_cond_in['mem_b2'], 'L3_cond_mem_g': _L3_cond_in['mem_g'], 'L3_cond_mem_be': _L3_cond_in['mem_be'], 'L3_cond_noi_W1': _L3_cond_in['noi_W1'], 'L3_cond_noi_b1': _L3_cond_in['noi_b1'], 'L3_cond_noi_W2': _L3_cond_in['noi_W2'], 'L3_cond_noi_b2': _L3_cond_in['noi_b2'], 'L3_cond_noi_g': _L3_cond_in['noi_g'], 'L3_cond_noi_be': _L3_cond_in['noi_be'], 'L3_cond_res_W1': _L3_cond_in['res_W1'], 'L3_cond_res_b1': _L3_cond_in['res_b1'], 'L3_cond_res_W2': _L3_cond_in['res_W2'], 'L3_cond_res_b2': _L3_cond_in['res_b2'], 'L3_cond_res_g': _L3_cond_in['res_g'], 'L3_cond_res_be': _L3_cond_in['res_be'], 'L3_cond_int_W1': _L3_cond_in['int_W1'], 'L3_cond_int_b1': _L3_cond_in['int_b1'], 'L3_cond_int_W2': _L3_cond_in['int_W2'], 'L3_cond_int_b2': _L3_cond_in['int_b2'], 'L3_cond_int_g': _L3_cond_in['int_g'], 'L3_cond_int_be': _L3_cond_in['int_be'], 'L3_cond_aw': _L3_cond_in['aw']}

def reference(x, cond_512, itok_BxS_0_999, itok_BxS_0_4, cond_64, fside_Bx32_0, mask_BxS_ik0, L0_cond_k_aff_w, L0_cond_k_aff_b, L0_cond_k_w, L0_cond_k_b, L0_cond_o_aff_w, L0_cond_o_aff_b, L0_cond_o_w, L0_cond_o_b, L1_cond_W_dec, L1_cond_b_dec, L1_cond_V, L2_cond_weight, L2_cond_bias, L2_cond_affine_w, L2_cond_affine_b, L3_cond_pw_g, L3_cond_pw_b, L3_cond_cp_g, L3_cond_cp_b, L3_cond_tm_g, L3_cond_tm_b, L3_cond_ms_g, L3_cond_ms_b, L3_cond_mem_W1, L3_cond_mem_b1, L3_cond_mem_W2, L3_cond_mem_b2, L3_cond_mem_g, L3_cond_mem_be, L3_cond_noi_W1, L3_cond_noi_b1, L3_cond_noi_W2, L3_cond_noi_b2, L3_cond_noi_g, L3_cond_noi_be, L3_cond_res_W1, L3_cond_res_b1, L3_cond_res_W2, L3_cond_res_b2, L3_cond_res_g, L3_cond_res_be, L3_cond_int_W1, L3_cond_int_b1, L3_cond_int_W2, L3_cond_int_b2, L3_cond_int_g, L3_cond_int_be, L3_cond_aw):
    import jax
    import jax.numpy as jnp

    def _L0_cond_ref(x, s, k_aff_w, k_aff_b, k_w, k_b, o_aff_w, o_aff_b, o_w, o_b):
        import jax, jax.numpy as jnp
        import numpy as np
        import math
        HEAD_NUM = 16
        EPS = 1e-08

        def modulated_linear(x, s, aff_w, aff_b, w, b):
            style = s @ aff_w.T + aff_b
            w_mod = w[None, :, :] * style[:, None, :]
            demod = jax.lax.rsqrt(jnp.sum(w_mod * w_mod, axis=2) + EPS)
            w_mod = w_mod * demod[:, :, None]
            return jnp.einsum('bni,boi->bno', x, w_mod) + b
        B, N, F = x.shape
        H = HEAD_NUM
        D = F // H
        kx = modulated_linear(x, s, k_aff_w, k_aff_b, k_w, k_b)
        kx = kx.reshape(B, N, H, D)
        q = k = v = kx
        scores = jnp.einsum('bnhd,bnjd->bnhj', q, k) / math.sqrt(D)
        A = jax.nn.softmax(scores, axis=-1)
        out = jnp.einsum('bnhj,bnjd->bnhd', A, v).reshape(B, N, F)
        out = modulated_linear(out, s, o_aff_w, o_aff_b, o_w, o_b)
        return out

    def _L1_cond_ref(x, mu, W_dec, b_dec, V):
        import jax, jax.numpy as jnp
        import numpy as np
        IN_DIM = 512
        OUT_DIM = 512
        MU_DIM = 256
        K = 30
        B = mu.shape[0]
        U = (mu @ W_dec + b_dec).reshape(B, IN_DIM + 1, K)
        param = jnp.einsum('bik,kj->bij', U, V)
        weight = param[:, :-1, :]
        bias = param[:, -1, :]
        out = jnp.einsum('bsd,bde->bse', x, weight)
        out = out + bias[:, None, :]
        return out

    def _L2_cond_ref(x, w, weight, bias, affine_w, affine_b):
        import jax, jax.numpy as jnp
        import numpy as np
        W_DIM = 256
        CLAMP = 256.0
        B, L, C = x.shape
        gain = 1.0 / np.sqrt(W_DIM).astype(np.float32)
        styles = w @ (affine_w * gain).T + affine_b
        ws = weight[None, :, :] * styles[:, None, :]
        dcoefs = jax.lax.rsqrt(jnp.sum(ws * ws, axis=2) + 1e-08)
        xm = x * styles[:, None, :]
        y = jnp.einsum('blc,oc->blo', xm, weight)
        y = y * dcoefs[:, None, :]
        y = jnp.clip(y + bias, -CLAMP, CLAMP)
        return y

    def _L3_cond_ref(x, pathway_ids, compartment_ids, time_steps, scale_type, memory_state, noise_state, resource_state, pw_g, pw_b, cp_g, cp_b, tm_g, tm_b, ms_g, ms_b, mem_W1, mem_b1, mem_W2, mem_b2, mem_g, mem_be, noi_W1, noi_b1, noi_W2, noi_b2, noi_g, noi_be, res_W1, res_b1, res_W2, res_b2, res_g, res_be, int_W1, int_b1, int_W2, int_b2, int_g, int_be, aw):
        import jax, jax.numpy as jnp
        import numpy as np
        EPS = 1e-05

        def _ln(x, g, b):
            m = jnp.mean(x, axis=-1, keepdims=True)
            v = jnp.mean((x - m) ** 2, axis=-1, keepdims=True)
            return (x - m) * jax.lax.rsqrt(v + EPS) * g + b

        def _mlp_ln(s, W1, b1, W2, b2, g, b):
            h = jax.nn.silu(s @ W1 + b1) @ W2 + b2
            return _ln(h, g, b)
        h = _ln(x, pw_g[pathway_ids], pw_b[pathway_ids])
        h = _ln(h, cp_g[compartment_ids], cp_b[compartment_ids])
        t = _ln(x, tm_g[time_steps], tm_b[time_steps])
        m = x + _mlp_ln(memory_state, mem_W1, mem_b1, mem_W2, mem_b2, mem_g, mem_be)[:, None, :]
        n = x + _mlp_ln(noise_state, noi_W1, noi_b1, noi_W2, noi_b2, noi_g, noi_be)[:, None, :]
        r = x + _mlp_ln(resource_state, res_W1, res_b1, res_W2, res_b2, res_g, res_be)[:, None, :]
        s = _ln(x, ms_g[scale_type], ms_b[scale_type])
        w = jax.nn.softmax(aw)
        cat = jnp.concatenate([w[0] * h, w[1] * t, w[2] * m, w[3] * n, w[4] * r, w[5] * s], axis=-1)
        return _mlp_ln(cat, int_W1, int_b1, int_W2, int_b2, int_g, int_be)
    x = x + _L0_cond_ref(x, cond_512, L0_cond_k_aff_w, L0_cond_k_aff_b, L0_cond_k_w, L0_cond_k_b, L0_cond_o_aff_w, L0_cond_o_aff_b, L0_cond_o_w, L0_cond_o_b)
    x = x + _L1_cond_ref(x, cond_512, L1_cond_W_dec, L1_cond_b_dec, L1_cond_V)
    x = x + _L2_cond_ref(x, cond_512, L2_cond_weight, L2_cond_bias, L2_cond_affine_w, L2_cond_affine_b)
    x = x + _L3_cond_ref(x, itok_BxS_0_999, itok_BxS_0_4, itok_BxS_0_4, mask_BxS_ik0, cond_512, cond_64, fside_Bx32_0, L3_cond_pw_g, L3_cond_pw_b, L3_cond_cp_g, L3_cond_cp_b, L3_cond_tm_g, L3_cond_tm_b, L3_cond_ms_g, L3_cond_ms_b, L3_cond_mem_W1, L3_cond_mem_b1, L3_cond_mem_W2, L3_cond_mem_b2, L3_cond_mem_g, L3_cond_mem_be, L3_cond_noi_W1, L3_cond_noi_b1, L3_cond_noi_W2, L3_cond_noi_b2, L3_cond_noi_g, L3_cond_noi_be, L3_cond_res_W1, L3_cond_res_b1, L3_cond_res_W2, L3_cond_res_b2, L3_cond_res_g, L3_cond_res_be, L3_cond_int_W1, L3_cond_int_b1, L3_cond_int_W2, L3_cond_int_b2, L3_cond_int_g, L3_cond_int_be, L3_cond_aw)
    return x

_drawn_inputs = setup_inputs


def setup_inputs(seed=0):
    import zlib

    import numpy as np

    out = dict(_drawn_inputs(seed))
    spreads = {'L0_cond_k_aff_b': (1.0, 0.2),
     'L0_cond_k_b': (0.0, 0.1),
     'L0_cond_o_aff_b': (1.0, 0.2),
     'L0_cond_o_b': (0.0, 0.1),
     'L2_cond_affine_b': (1.0, 0.2),
     'L3_cond_mem_b1': (0.0, 2.0),
     'L3_cond_mem_b2': (0.0, 2.0),
     'L3_cond_mem_be': (0.0, 2.0),
     'L3_cond_noi_b1': (0.0, 2.0),
     'L3_cond_noi_b2': (0.0, 2.0),
     'L3_cond_noi_be': (0.0, 2.0),
     'L3_cond_res_b1': (0.0, 2.0),
     'L3_cond_res_b2': (0.0, 2.0),
     'L3_cond_res_be': (0.0, 2.0),
     'L3_cond_int_b1': (0.0, 2.0),
     'L3_cond_int_b2': (0.0, 2.0),
     'L3_cond_int_be': (0.0, 2.0),
     'L3_cond_aw': (0.1666666716337204, 0.6)}
    factors = {'cond_64': 28.695,
     'fside_Bx32_0': 36.327,
     'L1_cond_b_dec': 5.988,
     'L2_cond_bias': 2.777,
     'L3_cond_pw_g': 64.0,
     'L3_cond_pw_b': 64.0,
     'L3_cond_cp_g': 64.0,
     'L3_cond_cp_b': 64.0,
     'L3_cond_tm_g': 64.0,
     'L3_cond_tm_b': 64.0,
     'L3_cond_ms_g': 64.0,
     'L3_cond_ms_b': 64.0,
     'L3_cond_mem_W1': 30.277,
     'L3_cond_mem_W2': 26.813,
     'L3_cond_mem_g': 64.0,
     'L3_cond_noi_W1': 28.343,
     'L3_cond_noi_W2': 26.055,
     'L3_cond_noi_g': 64.0,
     'L3_cond_res_W1': 36.913,
     'L3_cond_res_W2': 29.871,
     'L3_cond_res_g': 64.0,
     'L3_cond_int_W1': 3.147,
     'L3_cond_int_g': 64.0}
    for name, (base, spread) in spreads.items():
        noise = np.random.default_rng([zlib.crc32(name.encode()), seed]).standard_normal(out[name].shape)
        drawn = base * np.exp(spread * noise) if base else spread * noise
        out[name] = jnp.asarray(drawn.astype(out[name].dtype))
    for name, factor in factors.items():
        out[name] = (out[name] * factor).astype(out[name].dtype)
    return out
```

```python
import numpy as np
import concourse.bass as bass
from concourse import mybir
from contextlib import ExitStack

F32 = mybir.dt.float32
F32R = mybir.dt.float32r
I32 = mybir.dt.int32
ALU = mybir.AluOpType
ACT = mybir.ActivationFunctionType
AX = mybir.AxisListType.X

B, N, F = 2, 2048, 512
P = 128
T = B * N // P
TB = N // P
C = F // P
H = 16
D = F // H
Q = P // D
PR = D // 2
S = 256
BIG = 2.0 ** 98

STYLE_K, DEMOD_K, STYLE_O, DEMOD_O, STYLE_2, DEMOD_2, BIAS_1 = range(7)
ROWS = 7


TABLE_BATCH, TABLE_COMP, TABLE_SCALE = 0, B, B + 5
TABLE = B + 5 + 3
LOW = 32
RANK = 30
MLPS = ("mem", "noi", "res")
BLOCKS = ("h", "t", "m", "n", "r", "s")
CHUNK = 6


def allocator(nc, ctx, sems):
    def sb(name, shape, dt=F32):
        return ctx.enter_context(nc.sbuf_tensor(name, shape, dt))

    def ps(name, shape):
        return ctx.enter_context(nc.psum_tensor(name, shape, F32))

    def sem(name):
        sems.append(nc.alloc_semaphore(name=name))
        return sems[-1]

    return sb, ps, sem


def staged(nc, stage, *args):
    sems = []
    stage(nc, sems, *args)
    nc.clear_and_free_semaphores(sems)
    nc.all_engine_barrier()


def later(t, n):
    return not isinstance(t, int) or t >= n


def steps(engine, body, last, peel, by, first=0, end=T):
    for s in range(first, peel):
        body(s, s % 2, lambda o, s=s: 0 <= s - o < T)
    with engine.Fori(peel // by, end // by) as i:
        for u in range(by):
            body(i * by + u, u % 2, lambda o: True)
    for s in range(end, last):
        body(s, s % 2, lambda o, s=s: 0 <= s - o < T)


def modulation(nc, sems, I, rows, W, ident):
    with ExitStack() as ctx:
        sb, ps, sem = allocator(nc, ctx, sems)
        cond = sb("cond", [P, S // P, B])
        aff = sb("aff", [P, 3, S // P, F])
        affb = sb("affb", [B, 3, F])
        w = sb("w", [P, 3, C, F])
        wsq = sb("wsq", [P, 3, C, F])
        style = sb("style", [B, 3, F])
        stsq = sb("stsq", [P, 3, C, B])
        vareps = sb("vareps", [P, 3, C, B])
        demod_t = sb("demod_t", [P, 3, C, B])
        demod = sb("demod", [C * B, 3, P])
        minus_half = sb("minus_half", [P, 3, C, B])
        ps_style = ps("ps_style", [B, 3, 512])
        ps_demod = ps("ps_demod", [P, 3, C, B])
        ps_back = ps("ps_back", [C * B, 3, P])
        ps_turn = ps("ps_turn", [P, 3, C, B])

        small_in = sem("small_in")
        w_in = [sem(f"w_in{j}") for j in range(3)]
        style_mm = sem("style_mm")
        style_ready = sem("style_ready")
        turned = sem("turned")
        stsq_ready = sem("stsq_ready")
        wsq_ready = sem("wsq_ready")
        demod_mm = sem("demod_mm")
        vareps_ready = sem("vareps_ready")
        half_ready = sem("half_ready")
        demod_t_ready = sem("demod_t_ready")
        demod_back = sem("demod_back")
        demod_ready = sem("demod_ready")
        rows_out = sem("rows_out")
        hi_ready = sem("prep_hi_ready")
        block = ctx.enter_context(nc.Block())

        @block.sync
        def _(sp):
            sp.dma_start(ident[:, :], I["ident"]).then_inc(small_in, 16)
            sp.dma_start(cond[:, :, :], I["cond_t"].rearrange("(c p) b -> p c b", p=P)).then_inc(small_in, 16)
            for j, n in enumerate(("k", "o", "2")):
                sp.dma_start(aff[:, j, :, :], I[f"aff_{n}_t"].rearrange("(c p) f -> p c f", p=P)).then_inc(small_in, 16)
                sp.dma_start(affb[:, j, :], I[f"aff_{n}_b"].rearrange("(a f) -> a f", a=1).to_broadcast((B, F))).then_inc(small_in, 16)
            for j, n in enumerate(("k", "o", "2")):
                sp.dma_start(w[:, j, :, :], I[f"w_{n}_t"].rearrange("(c p) f -> p c f", p=P)).then_inc(w_in[j], 16)
            sp.wait_ge(style_ready, 3)
            for j in range(3):
                sp.dma_start(rows[2 * j], style[:, j, :]).then_inc(rows_out, 16)
            sp.wait_ge(demod_ready, 1)
            for j in range(3):
                for c in range(C):
                    sp.dma_start(rows[2 * j + 1, :, c * P:(c + 1) * P], demod[c * B:(c + 1) * B, j, :]).then_inc(rows_out, 16)
            sp.wait_ge(rows_out, 16 * (3 + 3 * C))

        @block.tensor
        def _(pe):
            pe.wait_ge(small_in, 16 * 8)
            for j in range(3):
                for c in range(S // P):
                    mm = nc.tensor.matmul(ps_style[:, j, :], cond[:, c, :], aff[:, j, c, :], start=c == 0, stop=c == S // P - 1)
                mm.then_inc(style_mm, 1)
            for j in range(3):
                pe.wait_ge(style_ready, j + 1)
                for c in range(C):
                    mm = nc.tensor.transpose(ps_turn[:, j, c, :], style[:, j, c * P:(c + 1) * P], ident[0:B, 0:B])
                mm.then_inc(turned, 1)
            for j in range(3):
                pe.wait_ge(stsq_ready, j + 1)
                pe.wait_ge(wsq_ready, j + 1)
                for o in range(C):
                    for c in range(C):
                        mm = nc.tensor.matmul(ps_demod[:, j, o, :], wsq[:, j, c, o * P:(o + 1) * P], stsq[:, j, c, :],
                                              start=c == 0, stop=c == C - 1)
            mm.then_inc(demod_mm, 1)
            pe.wait_ge(demod_t_ready, 1)
            for j in range(3):
                mm = nc.tensor.transpose(ps_back[:, j, :], demod_t[:, j, :, :].rearrange("p c b -> p (c b)"), ident[:, :])
            mm.then_inc(demod_back, 1)

        @block.vector
        def _(dve):
            nc.vector.memset(minus_half[:, :, :, :], -0.5).then_inc(half_ready, 1)
            dve.wait_ge(small_in, 16 * 8)
            for j in range(3):
                dve.wait_ge(style_mm, j + 1)
                gain = 1.0 if j < 2 else 1.0 / float(np.sqrt(S))
                nc.vector.scalar_tensor_tensor(style[:, j, :], ps_style[:, j, :], gain, affb[:, j, :],
                                               ALU.mult, ALU.add).then_inc(style_ready, 1)
            dve.wait_ge(demod_mm, 1)
            nc.vector.tensor_scalar(vareps[:, :, :, :], ps_demod[:, :, :, :], 1e-8, None, ALU.add).then_inc(vareps_ready, 1)
            dve.wait_ge(demod_back, 1)
            nc.vector.tensor_copy(demod[:, :, :], ps_back[:, :, :]).then_inc(demod_ready, 1)
            for j in range(2):
                dve.wait_ge(hi_ready, j + 1)
                nc.vector.tensor_tensor(W[j][1][:, :, :], w[:, j, :, :], W[j][0][:, :, :].bitcast(F32), ALU.subtract)

        @block.scalar
        def _(act):
            act.wait_ge(turned, 3)
            for j in range(3):
                nc.scalar.activation(stsq[:, j, :, :], ps_turn[:, j, :, :], ACT.Square).then_inc(stsq_ready, 1)
            for j in range(2):
                act.wait_ge(w_in[j], 16)
                nc.scalar.activation(W[j][0][:, :, :], w[:, j, :, :], ACT.Copy).then_inc(hi_ready, 1)

        @block.gpsimd
        def _(pool):
            for j in range(3):
                pool.wait_ge(w_in[j], 16)
                nc.gpsimd.tensor_tensor(wsq[:, j, :, :], w[:, j, :, :], w[:, j, :, :], ALU.mult).then_inc(wsq_ready, 1)
            pool.wait_ge(half_ready, 1)
            pool.wait_ge(vareps_ready, 1)
            nc.gpsimd.tensor_tensor(demod_t[:, :, :, :], vareps[:, :, :, :], minus_half[:, :, :, :], ALU.pow).then_inc(demod_t_ready, 1)


def attention(nc, sems, I, rows, W, ident, x1_dram):
    (wk_hi, wk_lo), (wo_hi, wo_lo) = W[0], W[1]
    x_dram = I["x"].rearrange("(t p) f -> t p f", p=P)
    x1_tiles = x1_dram.rearrange("(t p) f -> t p f", p=P)
    with ExitStack() as ctx:
        sb, ps, sem = allocator(nc, ctx, sems)
        bc = sb("bc", [P, 4, B, F])
        bias_k = sb("bias_k", [P, F])
        bias_o = sb("bias_o", [P, F])
        mask_l = sb("mask_l", [2, P])
        mask_r = sb("mask_r", [2, F])
        mask_lr = sb("mask_lr", [2, P], F32R)
        mask_rr = sb("mask_rr", [2, F], F32R)
        x_in = sb("x_in", [P, F])
        xm = sb("xm", [P, F])
        xh = sb("xh", [P, C, P], F32R)
        xl = sb("xl", [P, C, P], F32R)
        kd = sb("kd", [P, F])
        kb = sb("kb", [P, F])
        kt = [sb(f"kt{i}", [P, PR, H, 2]) for i in range(2)]
        v = [sb(f"v{i}", [P, PR, D]) for i in range(2)]
        mx = sb("mx", [P, PR])
        low = sb("low", [P, PR, D])
        e = sb("e", [P, PR, D])
        total = sb("total", [P, PR])
        rinv = sb("rinv", [P, PR])
        a = sb("a", [P, PR, D])
        at = [sb(f"at{i}", [P, PR, D]) for i in range(2)]
        ot = sb("ot", [P, F])
        om = sb("om", [P, F])
        oh = sb("oh", [P, C, P], F32R)
        ol = sb("ol", [P, C, P], F32R)
        od = sb("od", [P, F])
        x_res = sb("x_res", [P, F])
        xb = sb("xb", [P, F])
        x1 = [sb(f"x1o{i}", [P, F]) for i in range(2)]

        ps_x = ps("ps_x", [P, C, P])
        ps_k = ps("ps_k", [P, F])
        ps_s = [ps(f"ps_s{i}", [P, PR, D]) for i in range(2)]
        ps_v = ps("ps_v", [P, PR, H, 2])
        ps_t = ps("ps_t", [P, C, P])
        ps_o = ps("ps_o", [P, F])

        consts_in = sem("consts_in")
        mask_ready = sem("mask_ready")
        x_landed = sem("x_landed")
        xm_ready = sem("xm_ready")
        x_turned = sem("x_turned")
        xh_ready = sem("xh_ready")
        xl_ready = sem("xl_ready")
        k_done = sem("k_done")
        kd_ready = sem("kd_ready")
        kb_ready = sem("kb_ready")
        kt_ready = sem("kt_ready")
        v_ready = sem("v_ready")
        scores_done = sem("scores_done")
        mx_ready = sem("mx_ready")
        low_ready = sem("low_ready")
        e_ready = sem("e_ready")
        total_ready = sem("total_ready")
        rinv_ready = sem("rinv_ready")
        a_ready = sem("a_ready")
        at_ready = sem("at_ready")
        mixed = sem("mixed")
        ot_ready = sem("ot_ready")
        om_ready = sem("om_ready")
        o_turned = sem("o_turned")
        oh_ready = sem("oh_ready")
        ol_ready = sem("ol_ready")
        o_done = sem("o_done")
        od_ready = sem("od_ready")
        res_landed = sem("res_landed")
        xb_ready = sem("xb_ready")
        x1_ready = sem("x1_ready")
        x1_stored = [sem(f"x1_stored{i}") for i in range(2)]
        block = ctx.enter_context(nc.Block())

        @block.sync
        def _(sp):
            for j in range(4):
                for b in range(B):
                    sp.dma_start(bc[:, j, b, :], rows[j, b:b + 1, :].to_broadcast((P, F))).then_inc(consts_in, 16)
            sp.dma_start(bias_k[:, :], I["k_b"].rearrange("(a f) -> a f", a=1).to_broadcast((P, F))).then_inc(consts_in, 16)
            sp.dma_start(bias_o[:, :], I["o_b"].rearrange("(a f) -> a f", a=1).to_broadcast((P, F))).then_inc(consts_in, 16)
            sp.dma_start(mask_l[:, :], I["mask_l"]).then_inc(consts_in, 16)
            sp.dma_start(mask_r[:, :], I["mask_r"]).then_inc(consts_in, 16)

            def step(s, u, has):
                if has(0):
                    if later(s, 1):
                        sp.wait_ge(xm_ready, s)
                    sp.dma_start(x_in[:, :], x_dram[s]).then_inc(x_landed, 16)
                if has(4):
                    t = s - 4
                    if later(t, 1):
                        sp.wait_ge(xb_ready, t)
                    sp.dma_start(x_res[:, :], x_dram[t]).then_inc(res_landed, 16)
                if has(5):
                    t = s - 5
                    p = (u + 1) % 2
                    sp.wait_ge(x1_ready, t + 1)
                    sp.dma_start(x1_tiles[t], x1[p][:, :]).then_inc(x1_stored[p], 16)

            steps(sp, step, T + 5, 6, 2)
            for p in range(2):
                sp.wait_ge(x1_stored[p], 16 * (T // 2))

        @block.tensor
        def _(pe):
            pe.wait_ge(mask_ready, 2)

            def step(s, u, has):
                if has(4):
                    t = s - 4
                    pe.wait_ge(ol_ready, t + 1)
                    if later(t, 1):
                        pe.wait_ge(od_ready, t)
                    terms = [(o, w, c) for c in range(C) for o, w in ((oh, wo_hi), (oh, wo_lo), (ol, wo_hi))]
                    for n, (o, w, c) in enumerate(terms):
                        mm = nc.tensor.matmul(ps_o[:, :], o[:, c, :], w[:, c, :], start=n == 0, stop=n == len(terms) - 1)
                    mm.then_inc(o_done, 1)
                if has(0):
                    pe.wait_ge(xm_ready, s + 1)
                    if later(s, 1):
                        pe.wait_ge(xl_ready, s)
                    for c in range(C):
                        mm = nc.tensor.transpose(ps_x[:, c, :], xm[:, c * P:(c + 1) * P], ident[:, :])
                    mm.then_inc(x_turned, 1)
                if has(1):
                    t, p = s - 1, (u + 1) % 2
                    pe.wait_ge(kt_ready, t + 1)
                    if later(t, 2):
                        pe.wait_ge(low_ready, t - 1)
                    nc.tensor.matmul(ps_s[p][:, :, :], mask_lr[:, :], mask_rr[:, :], start=True, stop=False, skip_group_check=True)
                    for j in range(PR):
                        for q in range(Q):
                            g = slice(D * q, D * q + D)
                            pair = kt[p][g, j, :, :]
                            mm = nc.tensor.matmul(ps_s[p][g, j, :], pair, pair, start=False, stop=True, skip_group_check=True)
                    mm.then_inc(scores_done, 1)
                if has(0):
                    pe.wait_ge(xl_ready, s + 1)
                    if later(s, 1):
                        pe.wait_ge(kd_ready, s)
                    terms = [(x, w, c) for c in range(C) for x, w in ((xh, wk_hi), (xh, wk_lo), (xl, wk_hi))]
                    for n, (x, w, c) in enumerate(terms):
                        mm = nc.tensor.matmul(ps_k[:, :], x[:, c, :], w[:, c, :], start=n == 0, stop=n == len(terms) - 1)
                    mm.then_inc(k_done, 1)
                if has(3):
                    t = s - 3
                    pe.wait_ge(om_ready, t + 1)
                    if later(t, 1):
                        pe.wait_ge(ol_ready, t)
                if has(2):
                    pe.wait_ge(at_ready, s - 1)
                    pe.wait_ge(v_ready, s - 1)
                    if later(s, 3):
                        pe.wait_ge(ot_ready, s - 2)
                if has(3):
                    for c in range(C):
                        mm = nc.tensor.transpose(ps_t[:, c, :], om[:, c * P:(c + 1) * P], ident[:, :])
                    mm.then_inc(o_turned, 1)
                if has(2):
                    for j in range(PR):
                        for q in range(Q):
                            g = slice(D * q, D * q + D)
                            mm = nc.tensor.matmul(ps_v[g, j, :, :], v[u][g, j, :], at[u][g, j, :], start=True, stop=True)
                    mm.then_inc(mixed, 1)

            steps(pe, step, T + 4, 6, 2)

        @block.scalar
        def _(act):
            def step(s, u, has):
                if has(0):
                    act.wait_ge(x_turned, s + 1)
                    if later(s, 1):
                        act.wait_ge(k_done, s)
                    nc.scalar.activation(xh[:, :, :], ps_x[:, :, :], ACT.Copy).then_inc(xh_ready, 1)
                if has(1):
                    t = s - 1
                    act.wait_ge(low_ready, t + 1)
                    if later(t, 1):
                        act.wait_ge(a_ready, t)
                    nc.scalar.activation(e[:, :, :], low[:, :, :], ACT.Exp, scale=float(D) ** -0.5).then_inc(e_ready, 1)
                if has(3):
                    t = s - 3
                    act.wait_ge(o_turned, t + 1)
                    if later(t, 1):
                        act.wait_ge(o_done, t)
                    nc.scalar.activation(oh[:, :, :], ps_t[:, :, :], ACT.Copy).then_inc(oh_ready, 1)

            steps(act, step, T + 3, 6, 2)

        @block.vector
        def _(dve):
            dve.wait_ge(consts_in, 16 * 12)
            nc.vector.tensor_copy(mask_lr[:, :], mask_l[:, :]).then_inc(mask_ready, 1)
            nc.vector.tensor_copy(mask_rr[:, :], mask_r[:, :]).then_inc(mask_ready, 1)

            def step(s, u, has):
                if has(4):
                    t = s - 4
                    dve.wait_ge(o_done, t + 1)
                    if later(t, 1):
                        dve.wait_ge(x1_ready, t)
                    nc.vector.tensor_tensor(od[:, :], ps_o[:, :], bc[:, DEMOD_O, t // TB, :], ALU.mult).then_inc(od_ready, 1)
                if has(0):
                    dve.wait_ge(xh_ready, s + 1)
                    nc.vector.tensor_tensor(xl[:, :, :], ps_x[:, :, :], xh[:, :, :].bitcast(F32), ALU.subtract).then_inc(xl_ready, 1)
                if has(1):
                    t, p = s - 1, (u + 1) % 2
                    dve.wait_ge(scores_done, t + 1)
                    if later(t, 1):
                        dve.wait_ge(low_ready, t)
                    nc.vector.reduce_max(mx[:, :], ps_s[p][:, :, :], axis=AX).then_inc(mx_ready, 1)
                    dve.wait_ge(mx_ready, t + 1)
                    if later(t, 1):
                        dve.wait_ge(e_ready, t)
                    nc.vector.tensor_tensor(low[:, :, :], ps_s[p][:, :, :], mx[:, :].unsqueeze(2).to_broadcast((P, PR, D)),
                                            ALU.subtract).then_inc(low_ready, 1)
                if has(0):
                    dve.wait_ge(k_done, s + 1)
                    if later(s, 1):
                        dve.wait_ge(kb_ready, s)
                    nc.vector.tensor_tensor(kd[:, :], ps_k[:, :], bc[:, DEMOD_K, s // TB, :], ALU.mult).then_inc(kd_ready, 1)
                if has(1):
                    t, p = s - 1, (u + 1) % 2
                    dve.wait_ge(e_ready, t + 1)
                    if later(t, 1):
                        dve.wait_ge(rinv_ready, t)
                    nc.vector.reduce_sum(total[:, :], e[:, :, :], axis=AX).then_inc(total_ready, 1)
                    dve.wait_ge(total_ready, t + 1)
                    if later(t, 1):
                        dve.wait_ge(a_ready, t)
                    nc.vector.reciprocal(rinv[:, :], total[:, :]).then_inc(rinv_ready, 1)
                if has(2):
                    t = s - 2
                    dve.wait_ge(mixed, t + 1)
                    if later(t, 1):
                        dve.wait_ge(om_ready, t)
                    nc.vector.transpose(ot[:, :].rearrange("p (h a c) -> p h a c", h=H, c=2),
                                        ps_v[:, :, :, :].rearrange("p a h c -> p h a c")).then_inc(ot_ready, 1)
                if has(1):
                    t, p = s - 1, (u + 1) % 2
                    dve.wait_ge(a_ready, t + 1)
                    if later(t, 2):
                        dve.wait_ge(mixed, t - 1)
                    nc.vector.transpose(at[p][:, :, :], a[:, :, :]).then_inc(at_ready, 1)
                if has(3):
                    t = s - 3
                    dve.wait_ge(oh_ready, t + 1)
                    nc.vector.tensor_tensor(ol[:, :, :], ps_t[:, :, :], oh[:, :, :].bitcast(F32), ALU.subtract).then_inc(ol_ready, 1)
                if has(0):
                    dve.wait_ge(kb_ready, s + 1)
                    if later(s, 2):
                        dve.wait_ge(scores_done, s - 1)
                    nc.vector.transpose(kt[u][:, :, :, :].rearrange("p a h c -> p h a c"),
                                        kb[:, :].rearrange("p (h a c) -> p h a c", h=H, c=2)).then_inc(kt_ready, 1)
                    dve.wait_ge(kt_ready, s + 1)
                    if later(s, 2):
                        dve.wait_ge(mixed, s - 1)
                    nc.vector.transpose(v[u][:, :, :], kt[u][:, :, :, :].rearrange("p a h c -> p a (h c)")).then_inc(v_ready, 1)

            steps(dve, step, T + 4, 6, 2)

        @block.gpsimd
        def _(pool):
            pool.wait_ge(consts_in, 16 * 12)

            def step(s, u, has):
                if has(4):
                    t, p = s - 4, u
                    pool.wait_ge(res_landed, 16 * (t + 1))
                    if later(t, 1):
                        pool.wait_ge(x1_ready, t)
                    nc.gpsimd.tensor_tensor(xb[:, :], x_res[:, :], bias_o[:, :], ALU.add).then_inc(xb_ready, 1)
                    pool.wait_ge(od_ready, t + 1)
                    pool.wait_ge(xb_ready, t + 1)
                    if later(t, 2):
                        pool.wait_ge(x1_stored[p], 8 * (t - p))
                    nc.gpsimd.tensor_tensor(x1[p][:, :], od[:, :], xb[:, :], ALU.add).then_inc(x1_ready, 1)
                if has(0):
                    pool.wait_ge(kd_ready, s + 1)
                    if later(s, 1):
                        pool.wait_ge(kt_ready, s)
                    nc.gpsimd.tensor_tensor(kb[:, :], kd[:, :], bias_k[:, :], ALU.add).then_inc(kb_ready, 1)
                if has(1):
                    t = s - 1
                    pool.wait_ge(rinv_ready, t + 1)
                    if later(t, 1):
                        pool.wait_ge(at_ready, t)
                    nc.gpsimd.tensor_tensor(a[:, :, :], e[:, :, :], rinv[:, :].unsqueeze(2).to_broadcast((P, PR, D)),
                                            ALU.mult).then_inc(a_ready, 1)
                if has(2):
                    t = s - 2
                    pool.wait_ge(ot_ready, t + 1)
                    if later(t, 1):
                        pool.wait_ge(o_turned, t)
                    nc.gpsimd.tensor_tensor(om[:, :], ot[:, :], bc[:, STYLE_O, t // TB, :], ALU.mult).then_inc(om_ready, 1)
                if has(-1):
                    t = s + 1
                    pool.wait_ge(x_landed, 16 * (t + 1))
                    if later(t, 1):
                        pool.wait_ge(x_turned, t)
                    nc.gpsimd.tensor_tensor(xm[:, :], x_in[:, :], bc[:, STYLE_K, t // TB, :], ALU.mult).then_inc(xm_ready, 1)

            steps(pool, step, T + 4, 6, 2, first=-1, end=T - 2)




def conditions(nc, sems, I, rows, ident, wv, table_t, u_hi_lo, v_hi, v_lo):
    with ExitStack() as ctx:
        sb, ps, sem = allocator(nc, ctx, sems)
        cond = sb("c_cond", [P, S // P, B])
        c64 = sb("c64", [64, B])
        c32 = sb("c32", [32, B])
        aw = sb("aw", [P, 6])
        aw_max = sb("aw_max", [P, 1])
        aw_low = sb("aw_low", [P, 6])
        aw_exp = sb("aw_exp", [P, 6])
        aw_sum = sb("aw_sum", [P, 1])
        aw_inv = sb("aw_inv", [P, 1])
        w1 = [sb("w1_mem", [P, S // P, F]), sb("w1_noi", [64, 1, F]), sb("w1_res", [32, 1, F])]
        w2 = [sb(f"w2_{n}", [P, C, F]) for n in MLPS]
        vec = sb("vec", [B, 4, 3, F])
        hb = sb("hb", [B, 3, F])
        hs = sb("hs", [B, 3, F])
        hs_t = sb("hs_t", [P, 3, C, B])
        h2 = sb("h2", [B, 3, F])
        stats = sb("c_stats", [B, 3, 6])
        mean_var = sb("c_mean_var", [B, 3, 2])
        var_eps = sb("c_var_eps", [B, 3])
        half = sb("c_half", [B, 3])
        rstd = sb("c_rstd", [B, 3])
        hn = sb("c_hn", [B, 3, F])
        table = sb("table", [TABLE, 6, F])
        dec = [sb(f"dec{i}", [P, S // P, CHUNK, F]) for i in range(2)]
        dec_b = sb("dec_b", [P, C, RANK])
        last_w = sb("last_w", [P, S // P, RANK])
        last_b = sb("last_b", [RANK, 1])
        last_u = sb("last_u", [RANK, B])
        u = sb("u", [P, C, RANK, B])
        v = sb("v_rows", [P, F])
        bias1 = sb("bias1", [B, F])

        ps_h = ps("ps_h", [B, 3, 512])
        ps_turn = ps("c_ps_turn", [P, 3, C, B])
        ps_table = ps("ps_table_t", [P, 6, C, TABLE])
        ps_u = ps("ps_u", [P, C, RANK, B])
        ps_last = ps("ps_last", [RANK, B])
        ps_bias = ps("ps_bias", [B, F])

        in_first = sem("in_first")
        in_mlp = sem("in_mlp")
        in_table = sem("in_table")
        in_v = sem("in_v")
        dec_in = [sem(f"dec_in{i}") for i in range(2)]
        dec_used = sem("dec_used")
        zeroed = sem("zeroed")
        aw_step = sem("aw_step")
        aw_exp_ready = sem("aw_exp_ready")
        wv_ready = sem("wv_ready")
        h_mm = sem("h_mm")
        hb_ready = sem("hb_ready")
        hs_ready = sem("hs_ready")
        hs_turned = sem("hs_turned")
        hs_t_ready = sem("hs_t_ready")
        h2_mm = sem("h2_mm")
        h2_ready = sem("h2_ready")
        stats_ready = sem("c_stats_ready")
        mv_ready = sem("c_mv_ready")
        var_ready = sem("c_var_ready")
        rstd_ready = sem("c_rstd_ready")
        ln_step = sem("ln_step")
        table_ready = sem("table_ready")
        table_turned = sem("table_turned")
        last_mm = sem("last_mm")
        last_ready = sem("last_ready")
        bias_mm = sem("bias_mm")
        bias_ready = sem("bias_ready")
        bias_out = sem("bias_out")
        u_ready = sem("u_ready")
        u_hi_ready = sem("u_hi_ready")
        v_hi_ready = sem("v_hi_ready")
        block = ctx.enter_context(nc.Block())
        chunks = RANK // CHUNK

        @block.sync
        def _(sp):
            sp.dma_start(cond[:, :, :], I["cond_t"].rearrange("(c p) b -> p c b", p=P)).then_inc(in_first, 16)
            sp.dma_start(aw[:, :], I["aw"].rearrange("(a f) -> a f", a=1).to_broadcast((P, 6))).then_inc(in_first, 16)
            sp.dma_start(last_w[:, :, :], I["dec_last_w"].rearrange("(c p) k -> p c k", p=P)).then_inc(in_first, 16)
            sp.dma_start(last_b[:, :], I["dec_last_b"]).then_inc(in_first, 16)
            sp.dma_start(dec_b[:, :, :], I["dec_b"].rearrange("(c p) k -> p c k", p=P)).then_inc(in_first, 16)
            sp.dma_start(c64[:, :], I["cond64_t"]).then_inc(in_mlp, 16)
            sp.dma_start(c32[:, :], I["fside_t"]).then_inc(in_mlp, 16)
            sp.dma_start(w1[0][:, :, :], I["mem_W1"].rearrange("(c p) f -> p c f", p=P)).then_inc(in_mlp, 16)
            sp.dma_start(w1[1][:, 0, :], I["noi_W1"]).then_inc(in_mlp, 16)
            sp.dma_start(w1[2][:, 0, :], I["res_W1"]).then_inc(in_mlp, 16)
            for j, n in enumerate(MLPS):
                for i, m in enumerate(("b1", "b2", "g", "be")):
                    sp.dma_start(vec[:, i, j, :], I[f"{n}_{m}"].rearrange("(a f) -> a f", a=1).to_broadcast((B, F))).then_inc(in_mlp, 16)
                sp.dma_start(w2[j][:, :, :], I[f"{n}_W2"].rearrange("(c p) f -> p c f", p=P)).then_inc(in_mlp, 16)
            sp.wait_ge(zeroed, 2)
            sp.dma_start(table[TABLE_COMP:TABLE_COMP + 5, 0, :], I["cp_b"]).then_inc(in_table, 16)
            sp.dma_start(table[TABLE_COMP:TABLE_COMP + 5, 1, :], I["tm_b"]).then_inc(in_table, 16)
            sp.dma_start(table[TABLE_SCALE:TABLE_SCALE + 3, 5, :], I["ms_b"]).then_inc(in_table, 16)
            for q in range(Q):
                sp.dma_start(v[32 * q:32 * q + RANK, :], I["V"]).then_inc(in_v, 16)
            for n in range(chunks):
                if n >= 2:
                    sp.wait_ge(dec_used, n - 1)
                for c in range(S // P):
                    sp.dma_start(dec[n % 2][:, c, :, :], I["dec_w"][c * P:(c + 1) * P, n * CHUNK:(n + 1) * CHUNK, :]).then_inc(dec_in[n % 2], 16)
            sp.wait_ge(bias_ready, 1)
            sp.dma_start(rows[BIAS_1], bias1[:, :]).then_inc(bias_out, 16)
            sp.wait_ge(bias_out, 16)

        @block.tensor
        def _(pe):
            pe.wait_ge(in_first, 16 * 5)
            for c in range(S // P):
                mm = nc.tensor.matmul(ps_last[:, :], last_w[:, c, :], cond[:, c, :], start=c == 0, stop=c == S // P - 1)
            mm.then_inc(last_mm, 1)
            pe.wait_ge(in_mlp, 16 * 20)
            for c in range(S // P):
                nc.tensor.matmul(ps_h[:, 0, :], cond[:, c, :], w1[0][:, c, :], start=c == 0, stop=c == S // P - 1)
            nc.tensor.matmul(ps_h[:, 1, :], c64[:, :], w1[1][:, 0, :], start=True, stop=True)
            nc.tensor.matmul(ps_h[:, 2, :], c32[:, :], w1[2][:, 0, :], start=True, stop=True).then_inc(h_mm, 1)
            pe.wait_ge(hs_ready, 1)
            for j in range(3):
                for c in range(C):
                    mm = nc.tensor.transpose(ps_turn[:, j, c, :], hs[:, j, c * P:(c + 1) * P], ident[0:B, 0:B])
            mm.then_inc(hs_turned, 1)
            pe.wait_ge(hs_t_ready, 1)
            for j in range(3):
                for c in range(C):
                    mm = nc.tensor.matmul(ps_h[:, j, :], hs_t[:, j, c, :], w2[j][:, c, :], start=c == 0, stop=c == C - 1)
            mm.then_inc(h2_mm, 1)
            pe.wait_ge(last_ready, 1)
            pe.wait_ge(in_v, 16 * Q)
            nc.tensor.matmul(ps_bias[:, :], last_u[:, :], v[0:RANK, :], start=True, stop=True).then_inc(bias_mm, 1)
            for n in range(chunks):
                pe.wait_ge(dec_in[n % 2], 16 * 2 * (n // 2 + 1))
                for k in range(CHUNK):
                    for i in range(C):
                        for c in range(S // P):
                            mm = nc.tensor.matmul(ps_u[:, i, n * CHUNK + k, :], dec[n % 2][:, c, k, i * P:(i + 1) * P], cond[:, c, :],
                                                  start=c == 0, stop=c == S // P - 1)
                mm.then_inc(dec_used, 1)
            pe.wait_ge(table_ready, 1)
            pe.wait_ge(in_table, 16 * 3)
            for j in range(6):
                for c in range(C):
                    mm = nc.tensor.transpose(ps_table[:, j, c, :], table[:, j, c * P:(c + 1) * P], ident[0:TABLE, 0:TABLE])
            mm.then_inc(table_turned, 1)

        @block.scalar
        def _(act):
            act.wait_ge(aw_step, 2)
            nc.scalar.activation(aw_exp[:, :], aw_low[:, :], ACT.Exp).then_inc(aw_exp_ready, 1)
            act.wait_ge(hb_ready, 1)
            nc.scalar.activation(hs[:, :, :], hb[:, :, :], ACT.Silu).then_inc(hs_ready, 1)

        @block.vector
        def _(dve):
            nc.vector.memset(table[:, :, :], 0.0).then_inc(zeroed, 1)
            nc.vector.memset(v[:, :], 0.0).then_inc(zeroed, 1)
            nc.vector.memset(u_hi_lo[:, :, :, :].bitcast(F32), 0.0).then_inc(zeroed, 1)
            nc.vector.memset(half[:, :], -0.5).then_inc(zeroed, 1)
            dve.wait_ge(in_first, 16 * 5)
            nc.vector.reduce_max(aw_max[:, :], aw[:, :], axis=AX).then_inc(aw_step, 1)
            dve.wait_ge(aw_step, 1)
            nc.vector.tensor_scalar(aw_low[:, :], aw[:, :], aw_max[:, 0:1], None, ALU.subtract).then_inc(aw_step, 1)
            dve.wait_ge(aw_exp_ready, 1)
            nc.vector.reduce_sum(aw_sum[:, :], aw_exp[:, :], axis=AX).then_inc(aw_step, 1)
            dve.wait_ge(aw_step, 3)
            nc.vector.reciprocal(aw_inv[:, :], aw_sum[:, :]).then_inc(aw_step, 1)
            dve.wait_ge(aw_step, 4)
            nc.vector.tensor_scalar(wv[:, :], aw_exp[:, :], aw_inv[:, 0:1], None, ALU.mult).then_inc(wv_ready, 1)
            dve.wait_ge(last_mm, 1)
            nc.vector.tensor_scalar(last_u[:, :], ps_last[:, :], last_b[:, 0:1], None, ALU.add).then_inc(last_ready, 1)
            dve.wait_ge(h_mm, 1)
            nc.vector.tensor_tensor(hb[:, :, :], ps_h[:, :, :], vec[:, 0, :, :], ALU.add).then_inc(hb_ready, 1)
            dve.wait_ge(hs_turned, 1)
            nc.vector.tensor_copy(hs_t[:, :, :, :], ps_turn[:, :, :, :]).then_inc(hs_t_ready, 1)
            dve.wait_ge(h2_mm, 1)
            nc.vector.tensor_tensor(h2[:, :, :], ps_h[:, :, :], vec[:, 1, :, :], ALU.add).then_inc(h2_ready, 1)
            dve.wait_ge(h2_ready, 1)
            for j in range(3):
                nc.vector.bn_stats(stats[:, j, :], h2[:, j, :]).then_inc(stats_ready, 1)
            dve.wait_ge(stats_ready, 3)
            for j in range(3):
                nc.vector.bn_aggr(mean_var[:, j, :], stats[:, j, :]).then_inc(mv_ready, 1)
            dve.wait_ge(mv_ready, 3)
            nc.vector.tensor_scalar(var_eps[:, :], mean_var[:, :, 1], 1e-5, None, ALU.add).then_inc(var_ready, 1)
            dve.wait_ge(rstd_ready, 1)
            for j in range(3):
                nc.vector.tensor_scalar(hn[:, j, :], h2[:, j, :], mean_var[:, j, 0:1], rstd[:, j:j + 1],
                                        ALU.subtract, ALU.mult).then_inc(ln_step, 1)
            dve.wait_ge(ln_step, 3)
            nc.vector.tensor_tensor(h2[:, :, :], hn[:, :, :], vec[:, 2, :, :], ALU.mult).then_inc(ln_step, 1)
            dve.wait_ge(ln_step, 4)
            nc.vector.tensor_tensor(table[0:B, 2:5, :], h2[:, :, :], vec[:, 3, :, :], ALU.add).then_inc(table_ready, 1)
            dve.wait_ge(bias_mm, 1)
            nc.vector.tensor_copy(bias1[:, :], ps_bias[:, :]).then_inc(bias_ready, 1)
            dve.wait_ge(in_v, 16 * Q)
            nc.vector.tensor_copy(v_hi[:, :], v[:, :]).then_inc(v_hi_ready, 1)
            dve.wait_ge(v_hi_ready, 1)
            nc.vector.tensor_tensor(v_lo[:, :], v[:, :], v_hi[:, :].bitcast(F32), ALU.subtract)
            dve.wait_ge(dec_used, chunks)
            nc.vector.tensor_tensor(u[:, :, :, :], ps_u[:, :, :, :], dec_b[:, :, :].unsqueeze(3).to_broadcast((P, C, RANK, B)),
                                    ALU.add).then_inc(u_ready, 1)
            dve.wait_ge(u_ready, 1)
            dve.wait_ge(zeroed, 4)
            for b in range(B):
                for k in (0, 64):
                    nc.vector.tensor_copy(u_hi_lo[:, b, :, k:k + RANK], u[:, :, :, b]).then_inc(u_hi_ready, 1)
            dve.wait_ge(u_hi_ready, 2 * B)
            for b in range(B):
                for k in (0, 64):
                    nc.vector.tensor_tensor(u_hi_lo[:, b, :, k + 32:k + 32 + RANK], u[:, :, :, b],
                                            u_hi_lo[:, b, :, k:k + RANK].bitcast(F32), ALU.subtract)
            dve.wait_ge(table_turned, 1)
            dve.wait_ge(wv_ready, 1)
            for j in range(6):
                nc.vector.tensor_scalar(table_t[:, j, :, :], ps_table[:, j, :, :], wv[:, j:j + 1], None, ALU.mult)

        @block.gpsimd
        def _(pool):
            pool.wait_ge(var_ready, 1)
            pool.wait_ge(zeroed, 4)
            nc.gpsimd.tensor_tensor(rstd[:, :], var_eps[:, :], half[:, :], ALU.pow).then_inc(rstd_ready, 1)


LOADS = ("w_2_t", "int_W2", 2, 3, 4, 0, 1, 5)
PARTS = ("2", "out", "h", "t", "x", "s")


def weights(nc, sems, I, wv, table_t, Wt, tab):
    raw_n = 4
    with ExitStack() as ctx:
        sb, ps, sem = allocator(nc, ctx, sems)
        raw = [sb(f"raw{i}", [P, C, F]) for i in range(raw_n)]
        acc = [sb(f"acc{i}", [P, C, F]) for i in range(2)]
        tab_bias = sb("tab_bias", [TABLE, F])
        tab_sum = sb("tab_sum", [TABLE, F])
        ps_tab = ps("ps_tab", [TABLE, F])
        raw_in = [sem(f"raw_in{i}") for i in range(raw_n)]
        hi_ready = sem("w_hi_ready")
        item_done = sem("item_done")
        tab_used = sem("tab_used")
        acc_ready = sem("acc_ready")
        acc_hi = sem("acc_hi")
        bias_zero = sem("bias_zero")
        bias_in = sem("bias_in")
        tab_sum_ready = sem("tab_sum_ready")
        tab_hi_ready = sem("tab_hi_ready")
        tab_zero = sem("tab_zero")
        block = ctx.enter_context(nc.Block())
        dest = {"w_2_t": "2", "int_W2": "out", 0: "h", 1: "t", 5: "s"}

        @block.sync
        def _(sp):
            for i, item in enumerate(LOADS):
                if i >= raw_n:
                    sp.wait_ge(item_done, i - raw_n + 1)
                    if i - raw_n >= 2:
                        sp.wait_ge(tab_used, i - raw_n - 1)
                src = I[item] if isinstance(item, str) else I["int_W1"][item * F:(item + 1) * F, :]
                sp.dma_start(raw[i % raw_n][:, :, :], src.rearrange("(c p) f -> p c f", p=P)).then_inc(raw_in[i % raw_n], 16)
                if i == 1:
                    sp.wait_ge(bias_zero, 1)
                    sp.dma_start(tab_bias[0:B, :], I["int_b1"].rearrange("(a f) -> a f", a=1).to_broadcast((B, F))).then_inc(bias_in, 16)

        @block.tensor
        def _(pe):
            for i, item in enumerate(LOADS[2:]):
                pe.wait_ge(raw_in[(i + 2) % raw_n], 16 * ((i + 2) // raw_n + 1))
                for c in range(C):
                    mm = nc.tensor.matmul(ps_tab[:, :], table_t[:, item, c, :], raw[(i + 2) % raw_n][:, c, :],
                                          start=i == 0 and c == 0, stop=i == 5 and c == C - 1)
                mm.then_inc(tab_used, 1)

        @block.scalar
        def _(act):
            n = 0
            for i, item in enumerate(LOADS):
                if item in dest:
                    act.wait_ge(raw_in[i % raw_n], 16 * (i // raw_n + 1))
                    scale = wv[:, item:item + 1] if isinstance(item, int) else 1.0
                    nc.scalar.activation(Wt[dest[item]][0][:, :, :], raw[i % raw_n][:, :, :], ACT.Copy, scale=scale).then_inc(hi_ready, 1)
                elif item == 4:
                    act.wait_ge(acc_ready, 3)
                    nc.scalar.activation(Wt["x"][0][:, :, :], acc[0][:, :, :], ACT.Copy).then_inc(hi_ready, 1)

        @block.vector
        def _(dve):
            nc.vector.memset(tab_bias[:, :], 0.0).then_inc(bias_zero, 1)
            nc.vector.memset(tab[:, :].bitcast(F32), 0.0).then_inc(tab_zero, 1)
            hi = 0
            for i, item in enumerate(LOADS):
                r = raw[i % raw_n]
                dve.wait_ge(raw_in[i % raw_n], 16 * (i // raw_n + 1))
                if item in dest:
                    hi += 1
                    dve.wait_ge(hi_ready, hi)
                    w_hi, w_lo = Wt[dest[item]]
                    if isinstance(item, str):
                        nc.vector.tensor_tensor(w_lo[:, :, :], r[:, :, :], w_hi[:, :, :].bitcast(F32), ALU.subtract).then_inc(item_done, 1)
                    else:
                        nc.vector.scalar_tensor_tensor(w_lo[:, :, :].rearrange("p c f -> p (c f)"), r[:, :, :].rearrange("p c f -> p (c f)"), wv[:, item:item + 1],
                                                       w_hi[:, :, :].bitcast(F32).rearrange("p c f -> p (c f)"), ALU.mult, ALU.subtract).then_inc(item_done, 1)
                elif item == 2:
                    nc.vector.tensor_scalar(acc[0][:, :, :], r[:, :, :], wv[:, 2:3], None, ALU.mult).then_inc(item_done, 1)
                    dve.wait_ge(item_done, 3)
                    nc.vector.tensor_copy(tab_sum[:, :], tab_bias[:, :]).then_inc(acc_ready, 1)
                elif item == 3:
                    nc.vector.scalar_tensor_tensor(acc[1][:, :, :], r[:, :, :], wv[:, 3:4], acc[0][:, :, :], ALU.mult, ALU.add).then_inc(item_done, 1)
                    dve.wait_ge(item_done, 4)
                else:
                    nc.vector.scalar_tensor_tensor(acc[0][:, :, :], r[:, :, :], wv[:, 4:5], acc[1][:, :, :], ALU.mult, ALU.add).then_inc(item_done, 1)
                    dve.wait_ge(item_done, 5)
                    nc.vector.engine_nop().then_inc(acc_ready, 2)
                    hi += 1
                    dve.wait_ge(hi_ready, hi)
                    nc.vector.tensor_tensor(Wt["x"][1][:, :, :], acc[0][:, :, :], Wt["x"][0][:, :, :].bitcast(F32), ALU.subtract)
            dve.wait_ge(tab_used, 6)
            dve.wait_ge(bias_in, 16)
            nc.vector.tensor_tensor(tab_sum[:, :], ps_tab[:, :], tab_bias[:, :], ALU.add).then_inc(tab_sum_ready, 1)
            dve.wait_ge(tab_sum_ready, 1)
            dve.wait_ge(tab_zero, 1)
            nc.vector.tensor_copy(tab[0:TABLE, :], tab_sum[:, :]).then_inc(tab_hi_ready, 1)
            dve.wait_ge(tab_hi_ready, 1)
            nc.vector.tensor_tensor(tab[LOW:LOW + TABLE, :], tab_sum[:, :], tab[0:TABLE, :].bitcast(F32), ALU.subtract)


def cascade(nc, sems, I, rows, ident, Wt, tab, u_hi_lo, v_hi, v_lo, x1_dram, out):
    x1_tiles = x1_dram.rearrange("(t p) f -> t p f", p=P)
    out_tiles = out.rearrange("(t p) f -> t p f", p=P)
    with ExitStack() as ctx:
        sb, ps, sem = allocator(nc, ctx, sems)
        style2 = sb("style2", [P, B, F])
        demod2 = sb("demod2", [P, B, F])
        bias1 = sb("bias1_bc", [P, B, F])
        bias2 = sb("bias2", [P, F])
        b2 = sb("b2", [P, F])
        gain = sb("gain", [P, F])
        shift = sb("shift", [P, F])
        half = sb("half", [P, 1])
        codes = sb("codes", [2 * LOW, 1])
        ids = sb("ids", [P, 3, T], I32)
        x1 = sb("x1", [P, F])
        x1b = sb("x1b", [P, F])
        u_now = sb("u_now", [P, C, P], F32R)
        z = sb("z", [P, P], F32R)
        x2 = sb("x2", [P, F])
        xm2 = sb("xm2", [P, F])
        yd = sb("yd", [P, F])
        x3 = sb("x3", [P, F])
        x3s = sb("x3s", [P, 4, F])
        stats = sb("stats", [P, 3, 6])
        mean_var = sb("mean_var", [P, 3, 2])
        var_eps = sb("var_eps", [P, 3])
        rstd = sb("rstd", [P, 3])
        shift_n = sb("shift_n", [P, 3])
        xn = sb("xn", [P, F])
        tt = sb("tt", [P, F])
        ss = sb("ss", [P, F])
        h1 = sb("h1", [P, F])
        h = sb("h", [P, F])
        g = sb("act_g", [P, F])
        f2 = sb("f2", [P, F])
        o = sb("o", [P, F])
        names = ("x1", "x2", "x3", "t", "s", "h", "g")
        own = ("x1", "x2", "x3", "t", "g")
        hi = {n: sb(f"{n}_hi", [P, C, P], F32R) for n in own}
        lo = {n: sb(f"{n}_lo", [P, C, P], F32R) for n in own}
        for n, m in (("s", "x1"), ("h", "x2")):
            hi[n], lo[n] = hi[m], lo[m]
        pid = sb("pid", [P, 3], I32)
        path = sb("path", [P, 2 * F])
        comp = sb("comp", [P, 2 * F])
        scal = sb("scal", [P, F])
        id_rows = sb("id_rows", [2 * LOW, P], I32)
        one_hot = sb("one_hot", [2 * LOW, P], F32R)

        tp = [ps(f"tp{i}", [P, C, P]) for i in range(3)]
        ps_z = ps("ps_z", [P, P])
        ps_1 = ps("ps_1", [P, F])
        ps_2 = ps("ps_2", [P, F])
        ps_3 = ps("ps_3", [P, F])
        ps_4 = ps("ps_4", [P, F])

        consts_in = sem("c2_in")
        half_ready = sem("half_ready2")
        x1_in = sem("x1_in")
        rows_in = sem("id_rows_in")
        pid_ready = sem("pid_ready")
        path_in = sem("path_in")
        comp_in = sem("comp_in")
        scal_in = sem("scal_in")
        u_now_ready = sem("u_now_ready")
        x1b_ready = sem("x1b_ready")
        turned = {n: sem(f"{n}_turned") for n in names}
        hi_ready = {n: sem(f"{n}_hi_ready") for n in names}
        lo_ready = {n: sem(f"{n}_lo_ready") for n in names}
        u_done = sem("u_done")
        z_hi_ready = sem("z_hi_ready")
        z_ready = sem("z_ready")
        v_done = sem("v_done")
        x2_ready = sem("x2_ready")
        xm2_ready = sem("xm2_ready")
        l2_done = sem("l2_done")
        yd_ready = sem("yd_ready")
        yb_ready = sem("yb_ready")
        yc_ready = sem("yc_ready")
        x3_ready = sem("x3_ready")
        x3s_ready = sem("x3s_ready")
        st_ready = [sem(f"st_ready{i}") for i in range(3)]
        mv_ready = [sem(f"mv_ready{i}") for i in range(3)]
        var_ready = [sem(f"var_ready{i}") for i in range(3)]
        rstd_ready = [sem(f"rstd_ready{i}") for i in range(3)]
        shift_ready = [sem(f"shift_ready{i}") for i in range(3)]
        xn_ready = sem("xn_ready")
        t_ready = sem("t_ready")
        s_ready = sem("s_ready")
        h1_ready = sem("h1_ready")
        h1b_ready = sem("h1b_ready")
        hn_ready = sem("hn_ready")
        h_ready = sem("h_ready")
        hot_ready = sem("hot_ready")
        l3x_done = sem("l3x_done")
        l3t_done = sem("l3t_done")
        l3s_done = sem("l3s_done")
        l3_done = sem("l3_done")
        g_ready = sem("act_g_ready")
        l4_done = sem("l4_done")
        f2_ready = sem("f2_ready")
        fn_ready = sem("fn_ready")
        fg_ready = sem("fg_ready")
        o_ready = sem("o_ready")
        stored = sem("stored")
        dve_passed = sem("dve_passed")
        pool_passed = sem("pool_passed")
        block = ctx.enter_context(nc.Block())
        LN1, LN2, LN3 = range(3)

        def row(name):
            return I[name].rearrange("(a f) -> a f", a=1).to_broadcast((P, F))

        @block.sync
        def _(sp):
            for b in range(B):
                sp.dma_start(style2[:, b, :], rows[STYLE_2, b:b + 1, :].to_broadcast((P, F))).then_inc(consts_in, 16)
                sp.dma_start(demod2[:, b, :], rows[DEMOD_2, b:b + 1, :].to_broadcast((P, F))).then_inc(consts_in, 16)
                sp.dma_start(bias1[:, b, :], rows[BIAS_1, b:b + 1, :].to_broadcast((P, F))).then_inc(consts_in, 16)
            for dst, name in ((bias2, "bias_2"), (b2, "int_b2"), (gain, "int_g"), (shift, "int_be")):
                sp.dma_start(dst[:, :], row(name)).then_inc(consts_in, 16)
            sp.dma_start(codes[:, :], I["codes"]).then_inc(consts_in, 16)
            sp.dma_start(ids[:, :, :], I["ids"]).then_inc(consts_in, 16)

            def step(s, u, has):
                if has(5):
                    t = s - 5
                    sp.wait_ge(o_ready, t + 1)
                    sp.dma_start(out_tiles[t], o[:, :]).then_inc(stored, 16)
                if has(0):
                    if later(s, 1):
                        sp.wait_ge(turned["x1"], s)
                        sp.wait_ge(x1b_ready, s)
                    sp.dma_start(x1[:, :], x1_tiles[s]).then_inc(x1_in, 16)
                if has(2):
                    t = s - 2
                    if later(t, 1):
                        sp.wait_ge(hot_ready, t)
                    sp.dma_start(id_rows[:, :], I["id_rows"][t]).then_inc(rows_in, 16)

            steps(sp, step, T + 5, 5, 1)
            sp.wait_ge(stored, 16 * T)

        def product(out_ps, a, w, first=True, last=True):
            terms = [(x, y, c) for c in range(C) for x, y in ((hi[a], w[0]), (hi[a], w[1]), (lo[a], w[0]))]
            for n, (x, y, c) in enumerate(terms):
                mm = nc.tensor.matmul(out_ps[:, :], x[:, c, :], y[:, c, :], start=first and n == 0, stop=last and n == len(terms) - 1)
            return mm

        def turn(src, bank):
            for c in range(C):
                mm = nc.tensor.transpose(bank[:, c, :], src[:, c * P:(c + 1) * P], ident[:, :])
            return mm

        @block.tensor
        def _(pe):
            def step(s, u, has):
                a, b, c, d = s, s - 1, s - 2, s - 3
                if has(0):
                    pe.wait_ge(x1_in, 16 * (a + 1))
                    if later(a, 3):
                        pe.wait_ge(lo_ready["h"], a - 2)
                    turn(x1, tp[0]).then_inc(turned["x1"], 1)
                if has(1):
                    pe.wait_ge(xm2_ready, b + 1)
                    if later(b, 2):
                        pe.wait_ge(lo_ready["s"], b - 1)
                    turn(xm2, tp[1]).then_inc(turned["x2"], 1)
                if has(2):
                    pe.wait_ge(x3_ready, c + 1)
                    if later(c, 2):
                        pe.wait_ge(lo_ready["g"], c - 1)
                    turn(x3, tp[2]).then_inc(turned["x3"], 1)
                    pe.wait_ge(t_ready, c + 1)
                    if has(0):
                        pe.wait_ge(lo_ready["x1"], a + 1)
                    turn(tt, tp[0]).then_inc(turned["t"], 1)
                if has(0):
                    pe.wait_ge(lo_ready["x1"], a + 1)
                    pe.wait_ge(u_now_ready, a + 1)
                    if later(a, 1):
                        pe.wait_ge(z_ready, a)
                    for n, x in enumerate((hi["x1"], lo["x1"])):
                        for k in range(C):
                            mm = nc.tensor.matmul(ps_z[:, :], u_now[:, k, :], x[:, k, :], start=n == 0 and k == 0, stop=n == 1 and k == C - 1)
                    mm.then_inc(u_done, 1)
                if has(1):
                    pe.wait_ge(lo_ready["x2"], b + 1)
                    if later(b, 1):
                        pe.wait_ge(yd_ready, b)
                    product(ps_2, "x2", Wt["2"]).then_inc(l2_done, 1)
                if has(3):
                    pe.wait_ge(g_ready, d + 1)
                    if has(2):
                        pe.wait_ge(lo_ready["x3"], c + 1)
                    turn(g, tp[2]).then_inc(turned["g"], 1)
                if has(0):
                    pe.wait_ge(z_ready, a + 1)
                    if later(a, 1):
                        pe.wait_ge(x2_ready, a)
                    nc.tensor.matmul(ps_1[:, :], z[:, :], v_hi[:, :], start=True, stop=False)
                    nc.tensor.matmul(ps_1[:, :], z[:, :], v_lo[:, :], start=False, stop=True).then_inc(v_done, 1)
                if has(2):
                    pe.wait_ge(lo_ready["x3"], c + 1)
                    if later(c, 1):
                        pe.wait_ge(g_ready, c)
                    product(ps_3, "x3", Wt["x"], last=False).then_inc(l3x_done, 1)
                    pe.wait_ge(s_ready, c + 1)
                    if has(1):
                        pe.wait_ge(lo_ready["x2"], b + 1)
                    turn(ss, tp[1]).then_inc(turned["s"], 1)
                    pe.wait_ge(lo_ready["t"], c + 1)
                    product(ps_3, "t", Wt["t"], first=False, last=False).then_inc(l3t_done, 1)
                if has(3):
                    pe.wait_ge(lo_ready["g"], d + 1)
                    if later(d, 1):
                        pe.wait_ge(f2_ready, d)
                    product(ps_4, "g", Wt["out"]).then_inc(l4_done, 1)
                if has(2):
                    pe.wait_ge(h_ready, c + 1)
                    turn(h, tp[0]).then_inc(turned["h"], 1)
                    pe.wait_ge(lo_ready["s"], c + 1)
                    product(ps_3, "s", Wt["s"], first=False, last=False).then_inc(l3s_done, 1)
                    pe.wait_ge(lo_ready["h"], c + 1)
                    pe.wait_ge(hot_ready, c + 1)
                    product(ps_3, "h", Wt["h"], first=False, last=False)
                    nc.tensor.matmul(ps_3[:, :], one_hot[:, :], tab[:, :], start=False, stop=True).then_inc(l3_done, 1)

            steps(pe, step, T + 3, 5, 1)

        @block.scalar
        def _(act):
            def high(n, t, bank, used):
                act.wait_ge(turned[n], t + 1)
                if later(t, 1):
                    act.wait_ge(used, t)
                nc.scalar.activation(hi[n][:, :, :], bank[:, :, :], ACT.Copy).then_inc(hi_ready[n], 1)

            def normalize(k, t, dst, src, ready, used):
                act.wait_ge(shift_ready[k], t + 1)
                if later(t, 1):
                    act.wait_ge(used, t)
                nc.scalar.activation(dst[:, :], src[:, :], ACT.Identity, bias=shift_n[:, k:k + 1], scale=rstd[:, k:k + 1]).then_inc(ready, 1)

            def step(s, u, has):
                a, b, c, d = s, s - 1, s - 2, s - 3
                if has(3):
                    act.wait_ge(l3_done, d + 1)
                    if later(d, 1):
                        act.wait_ge(turned["g"], d)
                    nc.scalar.activation(g[:, :], ps_3[:, :], ACT.Silu).then_inc(g_ready, 1)
                if has(0):
                    high("x1", a, tp[0], u_done)
                if has(1):
                    high("x2", b, tp[1], l2_done)
                if has(2):
                    high("x3", c, tp[2], l3x_done)
                    high("t", c, tp[0], l3t_done)
                if has(0):
                    act.wait_ge(u_done, a + 1)
                    if later(a, 1):
                        act.wait_ge(v_done, a)
                    nc.scalar.activation(z[:, :], ps_z[:, :], ACT.Copy).then_inc(z_hi_ready, 1)
                if has(2):
                    normalize(LN2, c, h1, h1, hn_ready, h_ready)
                if has(3):
                    high("g", d, tp[2], l4_done)
                if has(2):
                    high("s", c, tp[1], l3s_done)
                if has(1):
                    normalize(LN1, b, xn, x3, xn_ready, h1_ready)
                if has(2):
                    high("h", c, tp[0], l3_done)
                if has(3):
                    normalize(LN3, d, f2, f2, fn_ready, o_ready)

            steps(act, step, T + 3, 5, 1)

        @block.vector
        def _(dve):
            nc.vector.memset(half[:, :], -0.5).then_inc(half_ready, 1)
            dve.wait_ge(consts_in, 16 * 12)

            def low(n, t, bank):
                dve.wait_ge(hi_ready[n], t + 1)
                nc.vector.tensor_tensor(lo[n][:, :, :], bank[:, :, :], hi[n][:, :, :].bitcast(F32), ALU.subtract).then_inc(lo_ready[n], 1)

            def moments(k, t, src):
                if later(t, 1):
                    dve.wait_ge(mv_ready[k], t)
                nc.vector.bn_stats(stats[:, k, :], src[:, :]).then_inc(st_ready[k], 1)
                dve.wait_ge(st_ready[k], t + 1)
                if later(t, 1):
                    dve.wait_ge(shift_ready[k], t)
                dve.sem_inc(dve_passed, 1)
                nc.vector.bn_aggr(mean_var[:, k, :], stats[:, k, :]).then_inc(mv_ready[k], 1)
                dve.wait_ge(mv_ready[k], t + 1)
                if later(t, 1):
                    dve.wait_ge(rstd_ready[k], t)
                nc.vector.tensor_scalar(var_eps[:, k:k + 1], mean_var[:, k, 1:2], 1e-5, None, ALU.add).then_inc(var_ready[k], 1)

            def shifts(k, t, applied):
                dve.wait_ge(rstd_ready[k], t + 1)
                if later(t, 1):
                    dve.wait_ge(applied, t)
                nc.vector.tensor_scalar(shift_n[:, k:k + 1], mean_var[:, k, 0:1], rstd[:, k:k + 1], -1.0, ALU.mult, ALU.mult).then_inc(shift_ready[k], 1)

            def step(s, u, has):
                a, b, c, d = s, s - 1, s - 2, s - 3
                if has(0):
                    low("x1", a, tp[0])
                if has(1):
                    low("x2", b, tp[1])
                if has(2):
                    low("x3", c, tp[2])
                    low("t", c, tp[0])
                if has(0):
                    dve.wait_ge(z_hi_ready, a + 1)
                    nc.vector.tensor_tensor(z[64:P, :], ps_z[64:P, :], z[64:P, :].bitcast(F32), ALU.subtract).then_inc(z_ready, 1)
                if has(2):
                    dve.wait_ge(h1b_ready, c + 1)
                    moments(LN2, c, h1)
                if has(1):
                    dve.wait_ge(l2_done, b + 1)
                    if later(b, 1):
                        dve.wait_ge(x3_ready, b)
                    nc.vector.tensor_tensor(yd[:, :], ps_2[:, :], demod2[:, b // TB, :], ALU.mult).then_inc(yd_ready, 1)
                if has(2):
                    shifts(LN2, c, hn_ready)
                if has(3):
                    low("g", d, tp[2])
                if has(0):
                    dve.wait_ge(v_done, a + 1)
                    dve.wait_ge(x1b_ready, a + 1)
                    if later(a, 1):
                        dve.wait_ge(x3_ready, a)
                        dve.wait_ge(xm2_ready, a)
                    nc.vector.tensor_tensor(x2[:, :], ps_1[:, :], x1b[:, :], ALU.add).then_inc(x2_ready, 1)
                if has(2):
                    low("s", c, tp[1])
                    dve.wait_ge(rows_in, 16 * (c + 1))
                    if later(c, 1):
                        dve.wait_ge(l3_done, c)
                    nc.vector.tensor_scalar(one_hot[:, :], id_rows[:, :], codes[:, 0:1], None, ALU.is_equal).then_inc(hot_ready, 1)
                if has(1):
                    dve.wait_ge(x3_ready, b + 1)
                    moments(LN1, b, x3)
                    shifts(LN1, b, xn_ready)
                if has(3):
                    dve.wait_ge(l4_done, d + 1)
                    if later(d, 1):
                        dve.wait_ge(o_ready, d)
                    nc.vector.tensor_tensor(f2[:, :], ps_4[:, :], b2[:, :], ALU.add).then_inc(f2_ready, 1)
                    dve.wait_ge(f2_ready, d + 1)
                    moments(LN3, d, f2)
                if has(2):
                    low("h", c, tp[0])
                if has(3):
                    shifts(LN3, d, fn_ready)

            steps(dve, step, T + 3, 5, 1)

        @block.gpsimd
        def _(pool):
            pool.wait_ge(consts_in, 16 * 12)
            pool.wait_ge(half_ready, 1)

            def power(k, t):
                pool.wait_ge(var_ready[k], t + 1)
                if later(t, 1):
                    pool.wait_ge(shift_ready[k], t)
                nc.gpsimd.tensor_tensor(rstd[:, k:k + 1], var_eps[:, k:k + 1], half[:, :], ALU.pow).then_inc(rstd_ready[k], 1)

            def step(s, u, has):
                a, b, c, d, f = s, s - 1, s - 2, s - 3, s - 4
                if has(2):
                    pool.wait_ge(xn_ready, c + 1)
                    pool.wait_ge(path_in, 16 * (c + 1))
                    if later(c, 1):
                        pool.wait_ge(h_ready, c)
                    nc.gpsimd.tensor_tensor(h1[:, :], xn[:, :], path[:, 0:F], ALU.mult).then_inc(h1_ready, 1)
                    pool.wait_ge(h1_ready, c + 1)
                    nc.gpsimd.tensor_tensor(h1[:, :], h1[:, :], path[:, F:2 * F], ALU.add).then_inc(h1b_ready, 1)
                if has(0):
                    if later(a, 1):
                        pool.wait_ge(u_done, a)
                    nc.gpsimd.tensor_copy(u_now[:, :, :], u_hi_lo[:, a // TB, :, :]).then_inc(u_now_ready, 1)
                    pool.wait_ge(x1_in, 16 * (a + 1))
                    if later(a, 1):
                        pool.wait_ge(x2_ready, a)
                    nc.gpsimd.tensor_tensor(x1b[:, :], x1[:, :], bias1[:, a // TB, :], ALU.add).then_inc(x1b_ready, 1)
                if has(2):
                    power(LN2, c)
                if has(4):
                    pool.wait_ge(fn_ready, f + 1)
                    nc.gpsimd.tensor_tensor(f2[:, :], f2[:, :], gain[:, :], ALU.mult).then_inc(fg_ready, 1)
                    pool.wait_ge(fg_ready, f + 1)
                    if later(f, 1):
                        pool.wait_ge(stored, 16 * f)
                    nc.gpsimd.tensor_tensor(o[:, :], f2[:, :], x3s[:, f % 4, :], ALU.add).then_inc(o_ready, 1)
                if has(2):
                    pool.wait_ge(hn_ready, c + 1)
                    pool.wait_ge(comp_in, 16 * (c + 1))
                    if later(c, 1):
                        pool.wait_ge(turned["h"], c)
                    nc.gpsimd.tensor_tensor(h[:, :], h1[:, :], comp[:, 0:F], ALU.mult).then_inc(h_ready, 1)
                if has(1):
                    if later(b, 1):
                        pool.wait_ge(path_in, 16 * b)
                        pool.wait_ge(comp_in, 16 * b)
                        pool.wait_ge(scal_in, 16 * b)
                    nc.gpsimd.tensor_copy(pid[:, :], ids[:, :, b]).then_inc(pid_ready, 1)
                    pool.wait_ge(pid_ready, b + 1)
                    if later(b, 1):
                        pool.wait_ge(h1b_ready, b)
                        pool.wait_ge(h_ready, b)
                        pool.wait_ge(t_ready, b)
                        pool.wait_ge(s_ready, b)
                    pool.sem_inc(pool_passed, 1)
                    for dst, table, k, landed in ((path, "path", 0, path_in), (comp, "comp", 1, comp_in), (scal, "scale", 2, scal_in)):
                        nc.gpsimd.indirect_dma_start(dst[:, :], None, I[table], bass.IndirectOffsetOnAxis(pid[:, k:k + 1], 0)).then_inc(landed, 16)
                    pool.wait_ge(yd_ready, b + 1)
                    nc.gpsimd.tensor_tensor(yd[:, :], yd[:, :], bias2[:, :], ALU.add).then_inc(yb_ready, 1)
                    pool.wait_ge(yb_ready, b + 1)
                    pool.sem_inc(pool_passed, 1)
                    nc.gpsimd.tensor_scalar(yd[:, :], yd[:, :], 256.0, -256.0, ALU.min, ALU.max).then_inc(yc_ready, 1)
                    pool.wait_ge(yc_ready, b + 1)
                    if later(b, 1):
                        pool.wait_ge(xn_ready, b)
                        pool.wait_ge(turned["x3"], b)
                        pool.wait_ge(x3s_ready, b)
                    nc.gpsimd.tensor_tensor(x3[:, :], yd[:, :], x2[:, :], ALU.add).then_inc(x3_ready, 1)
                if has(0):
                    pool.wait_ge(x2_ready, a + 1)
                    if later(a, 1):
                        pool.wait_ge(turned["x2"], a)
                    nc.gpsimd.tensor_tensor(xm2[:, :], x2[:, :], style2[:, a // TB, :], ALU.mult).then_inc(xm2_ready, 1)
                if has(1):
                    power(LN1, b)
                    pool.wait_ge(x3_ready, b + 1)
                    if later(b, 4):
                        pool.wait_ge(o_ready, b - 3)
                    nc.gpsimd.tensor_tensor(x3s[:, b % 4, :], x3[:, :], shift[:, :], ALU.add).then_inc(x3s_ready, 1)
                    pool.wait_ge(xn_ready, b + 1)
                    pool.wait_ge(comp_in, 16 * (b + 1))
                    if later(b, 1):
                        pool.wait_ge(turned["t"], b)
                    nc.gpsimd.tensor_tensor(tt[:, :], xn[:, :], comp[:, F:2 * F], ALU.mult).then_inc(t_ready, 1)
                    pool.wait_ge(scal_in, 16 * (b + 1))
                    if later(b, 1):
                        pool.wait_ge(turned["s"], b)
                    nc.gpsimd.tensor_tensor(ss[:, :], xn[:, :], scal[:, :], ALU.mult).then_inc(s_ready, 1)
                if has(3):
                    power(LN3, d)

            steps(pool, step, T + 4, 5, 1)


def program(nc, I, out):
    rows = nc.dram_tensor("rows", (ROWS, B, F), F32, kind="Internal").ap()
    x1_dram = nc.dram_tensor("x1_dram", (B * N, F), F32, kind="Internal").ap()
    with ExitStack() as ctx:
        sb, _, _ = allocator(nc, ctx, [])
        ident = sb("ident", [P, P])
        with ExitStack() as first:
            sb1, _, _ = allocator(nc, first, [])
            W = [[sb1(f"w{n}_{part}", [P, C, F], F32R) for part in ("hi", "lo")] for n in "ko"]
            staged(nc, modulation, I, rows, W, ident)
            staged(nc, attention, I, rows, W, ident, x1_dram)
        wv = sb("wv", [P, 6])
        table_t = sb("table_t", [P, 6, C, TABLE])
        u_hi_lo = sb("u_hi_lo", [P, B, C, P], F32R)
        v_hi = sb("v_hi", [P, F], F32R)
        v_lo = sb("v_lo", [P, F], F32R)
        tab = sb("tab", [2 * LOW, F], F32R)
        staged(nc, conditions, I, rows, ident, wv, table_t, u_hi_lo, v_hi, v_lo)
        Wt = {n: [sb(f"w{n}_{part}", [P, C, F], F32R) for part in ("high", "low")] for n in PARTS}
        staged(nc, weights, I, wv, table_t, Wt, tab)
        staged(nc, cascade, I, rows, ident, Wt, tab, u_hi_lo, v_hi, v_lo, x1_dram, out)


def kernel(x, cond_512, itok_BxS_0_999, itok_BxS_0_4, cond_64, fside_Bx32_0, mask_BxS_ik0, **w):
    import concourse.bacc as bacc
    from concourse.bass_utils import run_bass_kernel_spmd as run

    token = np.arange(P) % 2
    sign = np.where(token, 1.0, -1.0).astype(np.float32)
    columns = np.tile(sign, F // P)
    paths, comps, scales = (np.asarray(a).reshape(T, P) for a in (itok_BxS_0_999, itok_BxS_0_4, mask_BxS_ik0))
    batch = np.repeat(np.arange(B, dtype=np.int32), TB * P).reshape(T, P)
    id_rows = np.zeros((T, 2 * LOW, P), np.int32)
    codes = np.full((2 * LOW, 1), -1.0, np.float32)
    for at in (0, LOW):
        for first, count, what in ((TABLE_BATCH, B, batch), (TABLE_COMP, 5, comps), (TABLE_SCALE, 3, scales)):
            id_rows[:, at + first:at + first + count, :] = what[:, None, :]
            codes[at + first:at + first + count, 0] = np.arange(count)
    dec = np.asarray(w["L1_cond_W_dec"])
    dec_b = np.asarray(w["L1_cond_b_dec"])
    arrays = {
        "x": np.asarray(x).reshape(B * N, F),
        "cond_t": np.asarray(cond_512).T,
        "cond64_t": np.asarray(cond_64).T,
        "fside_t": np.asarray(fside_Bx32_0).T,
        "ids": np.stack([paths, comps, scales]).transpose(2, 0, 1),
        "id_rows": id_rows,
        "aff_k_t": np.asarray(w["L0_cond_k_aff_w"]).T, "aff_k_b": w["L0_cond_k_aff_b"],
        "aff_o_t": np.asarray(w["L0_cond_o_aff_w"]).T, "aff_o_b": w["L0_cond_o_aff_b"],
        "aff_2_t": np.asarray(w["L2_cond_affine_w"]).T, "aff_2_b": w["L2_cond_affine_b"],
        "w_k_t": np.asarray(w["L0_cond_k_w"]).T, "k_b": w["L0_cond_k_b"],
        "w_o_t": np.asarray(w["L0_cond_o_w"]).T, "o_b": w["L0_cond_o_b"],
        "w_2_t": np.asarray(w["L2_cond_weight"]).T, "bias_2": w["L2_cond_bias"],
        "dec_w": dec[:, :F * RANK].reshape(S, F, RANK).transpose(0, 2, 1),
        "dec_b": dec_b[:F * RANK].reshape(F, RANK),
        "dec_last_w": dec[:, F * RANK:], "dec_last_b": dec_b[F * RANK:].reshape(RANK, 1),
        "V": w["L1_cond_V"],
        "path": np.concatenate([w["L3_cond_pw_g"], w["L3_cond_pw_b"]], axis=1),
        "comp": np.concatenate([w["L3_cond_cp_g"], w["L3_cond_tm_g"]], axis=1),
        "scale": w["L3_cond_ms_g"],
        "codes": codes,
        "ident": np.eye(P, dtype=np.float32),
        "mask_l": np.stack([np.ones(P, np.float32), sign]),
        "mask_r": np.stack([np.full(F, -BIG, np.float32), (BIG * columns).astype(np.float32)]),
    }
    for name in ("cp_b", "tm_b", "ms_b", "int_W1", "int_b1", "int_W2", "int_b2", "int_g", "int_be", "aw",
                 *(f"{m}_{v}" for m in MLPS for v in ("W1", "b1", "W2", "b2", "g", "be"))):
        arrays[name] = w[f"L3_cond_{name}"]
    arrays = {k: np.ascontiguousarray(a) for k, a in arrays.items()}
    nc = bacc.Bacc("TRN2", target_bir_lowering=False, num_devices=1)
    I = {k: nc.dram_tensor(f"in_{k}", a.shape, mybir.dt.from_np(a.dtype), kind="ExternalInput").ap() for k, a in arrays.items()}
    out = nc.dram_tensor("out", (B * N, F), F32, kind="ExternalOutput").ap()
    program(nc, I, out)
    got = run(nc, [{f"in_{k}": a for k, a in arrays.items()}], core_ids=[0]).results[0]["out"]
    return got.reshape(B, N, F)
```

```python
import numpy as np
import concourse.bass as bass
from concourse import mybir
from contextlib import ExitStack

F32 = mybir.dt.float32
F32R = mybir.dt.float32r
I32 = mybir.dt.int32
ALU = mybir.AluOpType
ACT = mybir.ActivationFunctionType
AX = mybir.AxisListType.X

B, N, F = 2, 2048, 512
P = 128
T = B * N // P
TB = N // P
C = F // P
H = 16
D = F // H
Q = P // D
PR = D // 2
S = 256
BIG = 2.0 ** 98

STYLE_K, DEMOD_K, STYLE_O, DEMOD_O, STYLE_2, DEMOD_2, BIAS_1 = range(7)
ROWS = 7


TABLE_BATCH, TABLE_COMP, TABLE_SCALE = 0, B, B + 5
TABLE = B + 5 + 3
LOW = 32
RANK = 30
MLPS = ("mem", "noi", "res")
BLOCKS = ("h", "t", "m", "n", "r", "s")


def allocator(nc, ctx, sems):
    def sb(name, shape, dt=F32):
        return ctx.enter_context(nc.sbuf_tensor(name, shape, dt))

    def ps(name, shape):
        return ctx.enter_context(nc.psum_tensor(name, shape, F32))

    def sem(name):
        sems.append(nc.alloc_semaphore(name=name))
        return sems[-1]

    return sb, ps, sem


def staged(nc, stage, *args):
    sems = []
    stage(nc, sems, *args)
    nc.clear_and_free_semaphores(sems)
    nc.all_engine_barrier()


def later(t, n):
    return not isinstance(t, int) or t >= n


def steps(engine, body, last, peel, by, first=0, end=T):
    for s in range(first, peel):
        body(s, s % 2, lambda o, s=s: 0 <= s - o < T)
    with engine.Fori(peel // by, end // by) as i:
        for u in range(by):
            body(i * by + u, u % 2, lambda o: True)
    for s in range(end, last):
        body(s, s % 2, lambda o, s=s: 0 <= s - o < T)


def modulation(nc, sems, I, rows, W, ident, cond):
    with ExitStack() as ctx:
        sb, ps, sem = allocator(nc, ctx, sems)
        aff = sb("aff", [P, 3, S // P, F])
        affb = sb("affb", [B, 3, F])
        w = sb("w", [P, 3, C, F])
        wsq = sb("wsq", [P, 3, C, F])
        style = sb("style", [B, 3, F])
        stsq = sb("stsq", [P, 3, C, B])
        vareps = sb("vareps", [P, 3, C, B])
        demod_t = sb("demod_t", [P, 3, C, B])
        demod = sb("demod", [C * B, 3, P])
        minus_half = sb("minus_half", [P, 3, C, B])
        ps_style = ps("ps_style", [B, 3, 512])
        ps_demod = ps("ps_demod", [P, 3, C, B])
        ps_back = ps("ps_back", [C * B, 3, P])
        ps_turn = ps("ps_turn", [P, 3, C, B])

        small_in = sem("small_in")
        w_in = [sem(f"w_in{j}") for j in range(3)]
        style_mm = sem("style_mm")
        style_ready = sem("style_ready")
        turned = sem("turned")
        stsq_ready = sem("stsq_ready")
        wsq_ready = sem("wsq_ready")
        demod_mm = sem("demod_mm")
        vareps_ready = sem("vareps_ready")
        half_ready = sem("half_ready")
        demod_t_ready = sem("demod_t_ready")
        demod_back = sem("demod_back")
        demod_ready = sem("demod_ready")
        rows_out = sem("rows_out")
        hi_ready = sem("prep_hi_ready")
        block = ctx.enter_context(nc.Block())

        @block.sync
        def _(sp):
            sp.dma_start(ident[:, :], I["ident"]).then_inc(small_in, 16)
            sp.dma_start(cond[:, :, :], I["cond_t"].rearrange("(c p) b -> p c b", p=P)).then_inc(small_in, 16)
            for j, n in enumerate(("k", "o", "2")):
                sp.dma_start(aff[:, j, :, :], I[f"aff_{n}_t"].rearrange("(c p) f -> p c f", p=P)).then_inc(small_in, 16)
                sp.dma_start(affb[:, j, :], I[f"aff_{n}_b"].rearrange("(a f) -> a f", a=1).to_broadcast((B, F))).then_inc(small_in, 16)
            for j, n in enumerate(("k", "o", "2")):
                sp.dma_start(w[:, j, :, :], I[f"w_{n}_t"].rearrange("(c p) f -> p c f", p=P)).then_inc(w_in[j], 16)
            sp.wait_ge(style_ready, 3)
            for j in range(3):
                sp.dma_start(rows[2 * j], style[:, j, :]).then_inc(rows_out, 16)
            sp.wait_ge(demod_ready, 1)
            for j in range(3):
                for c in range(C):
                    sp.dma_start(rows[2 * j + 1, :, c * P:(c + 1) * P], demod[c * B:(c + 1) * B, j, :]).then_inc(rows_out, 16)
            sp.wait_ge(rows_out, 16 * (3 + 3 * C))

        @block.tensor
        def _(pe):
            pe.wait_ge(small_in, 16 * 8)
            for j in range(3):
                for c in range(S // P):
                    mm = nc.tensor.matmul(ps_style[:, j, :], cond[:, c, :], aff[:, j, c, :], start=c == 0, stop=c == S // P - 1)
                mm.then_inc(style_mm, 1)
            for j in range(3):
                pe.wait_ge(style_ready, j + 1)
                for c in range(C):
                    mm = nc.tensor.transpose(ps_turn[:, j, c, :], style[:, j, c * P:(c + 1) * P], ident[0:B, 0:B])
                mm.then_inc(turned, 1)
            for j in range(3):
                pe.wait_ge(stsq_ready, j + 1)
                pe.wait_ge(wsq_ready, j + 1)
                for o in range(C):
                    for c in range(C):
                        mm = nc.tensor.matmul(ps_demod[:, j, o, :], wsq[:, j, c, o * P:(o + 1) * P], stsq[:, j, c, :],
                                              start=c == 0, stop=c == C - 1)
            mm.then_inc(demod_mm, 1)
            pe.wait_ge(demod_t_ready, 1)
            for j in range(3):
                mm = nc.tensor.transpose(ps_back[:, j, :], demod_t[:, j, :, :].rearrange("p c b -> p (c b)"), ident[:, :])
            mm.then_inc(demod_back, 1)

        @block.vector
        def _(dve):
            nc.vector.memset(minus_half[:, :, :, :], -0.5).then_inc(half_ready, 1)
            dve.wait_ge(small_in, 16 * 8)
            for j in range(3):
                dve.wait_ge(style_mm, j + 1)
                gain = 1.0 if j < 2 else 1.0 / float(np.sqrt(S))
                nc.vector.scalar_tensor_tensor(style[:, j, :], ps_style[:, j, :], gain, affb[:, j, :],
                                               ALU.mult, ALU.add).then_inc(style_ready, 1)
            dve.wait_ge(demod_mm, 1)
            nc.vector.tensor_scalar(vareps[:, :, :, :], ps_demod[:, :, :, :], 1e-8, None, ALU.add).then_inc(vareps_ready, 1)
            dve.wait_ge(demod_back, 1)
            nc.vector.tensor_copy(demod[:, :, :], ps_back[:, :, :]).then_inc(demod_ready, 1)
            for j in range(2):
                dve.wait_ge(hi_ready, j + 1)
                nc.vector.tensor_tensor(W[j][1][:, :, :], w[:, j, :, :], W[j][0][:, :, :].bitcast(F32), ALU.subtract)

        @block.scalar
        def _(act):
            act.wait_ge(turned, 3)
            for j in range(3):
                nc.scalar.activation(stsq[:, j, :, :], ps_turn[:, j, :, :], ACT.Square).then_inc(stsq_ready, 1)
            for j in range(2):
                act.wait_ge(w_in[j], 16)
                nc.scalar.activation(W[j][0][:, :, :], w[:, j, :, :], ACT.Copy).then_inc(hi_ready, 1)

        @block.gpsimd
        def _(pool):
            for j in range(3):
                pool.wait_ge(w_in[j], 16)
                nc.gpsimd.tensor_tensor(wsq[:, j, :, :], w[:, j, :, :], w[:, j, :, :], ALU.mult).then_inc(wsq_ready, 1)
            pool.wait_ge(half_ready, 1)
            pool.wait_ge(vareps_ready, 1)
            nc.gpsimd.tensor_tensor(demod_t[:, :, :, :], vareps[:, :, :, :], minus_half[:, :, :, :], ALU.pow).then_inc(demod_t_ready, 1)


def attention(nc, sems, I, rows, W, ident, cond, u_dram, prefetch, x1_dram):
    (wk_hi, wk_lo), (wo_hi, wo_lo) = W[0], W[1]
    x_dram = I["x"].rearrange("(t p) f -> t p f", p=P)
    x1_tiles = x1_dram.rearrange("(t p) f -> t p f", p=P)
    U_AT = 4
    PEEL, LAST = 8, T + 5
    with ExitStack() as ctx:
        sb, ps, sem = allocator(nc, ctx, sems)
        bc = sb("bc", [P, 4, B, F])
        bias_k = sb("bias_k", [P, F])
        bias_o = sb("bias_o", [P, F])
        mask_l = sb("mask_l", [2, P])
        mask_r = sb("mask_r", [2, F])
        mask_lr = sb("mask_lr", [2, P], F32R)
        mask_rr = sb("mask_rr", [2, F], F32R)
        x_in = sb("x_in", [P, F])
        xm = sb("xm", [P, F])
        xh = sb("xh", [P, C, P], F32R)
        xl = sb("xl", [P, C, P], F32R)
        kb = sb("kb", [P, F])
        kt = [sb(f"kt{i}", [P, PR, H * 2]) for i in range(2)]
        k_diag = [sb(f"k_diag{i}", [P, PR, Q, H * 2]) for i in range(2)]
        v = [sb(f"v{i}", [P, PR // Q, P]) for i in range(2)]
        mx = sb("mx", [P, PR])
        low = sb("low", [P, PR, D])
        e = sb("e", [P, PR, D])
        total = sb("total", [P, PR])
        rinv = sb("rinv", [P, PR])
        at = sb("at", [P, PR, D])
        at_diag = sb("at_diag", [P, PR, Q, D])
        om = sb("om", [P, F])
        oh = sb("oh", [P, C, P], F32R)
        ol = sb("ol", [P, C, P], F32R)
        od = sb("od", [P, F])
        xb = sb("xb", [P, F])
        x1 = [sb(f"x1o{i}", [P, F]) for i in range(2)]
        dec = [sb(f"dec{i}", [P, S // P, F]) for i in range(2)]
        u_row = sb("u_row", [B, F])

        ps_x = ps("ps_x", [P, C, P])
        ps_k = ps("ps_k", [P, F])
        ps_s = ps("ps_s", [P, PR, D])
        ps_vt = ps("ps_vt", [P, PR // Q, P])
        ps_v = ps("ps_v", [P, PR, H, 2])
        ps_t = ps("ps_t", [P, C, P])
        ps_o = ps("ps_o", [P, F])
        ps_u = ps("ps_u", [B, F])

        consts_in = sem("consts_in")
        mask_ready = sem("mask_ready")
        diag_zero = sem("diag_zero")
        x_landed = sem("x_landed")
        xm_ready = sem("xm_ready")
        x_turned = sem("x_turned")
        xh_ready = sem("xh_ready")
        xl_ready = sem("xl_ready")
        k_done = sem("k_done")
        kd_ready = sem("kd_ready")
        kb_ready = sem("kb_ready")
        kt_ready = sem("kt_ready")
        k_diag_ready = sem("k_diag_ready")
        v_ready = sem("v_ready")
        v_turned = sem("v_turned")
        at_diag_ready = sem("at_diag_ready")
        scores_done = sem("scores_done")
        mx_ready = sem("mx_ready")
        low_ready = sem("low_ready")
        e_ready = sem("e_ready")
        total_ready = sem("total_ready")
        rinv_ready = sem("rinv_ready")
        a_ready = sem("a_ready")
        at_ready = sem("at_ready")
        mixed = sem("mixed")
        ot_ready = sem("ot_ready")
        om_ready = sem("om_ready")
        o_turned = sem("o_turned")
        oh_ready = sem("oh_ready")
        ol_ready = sem("ol_ready")
        o_done = sem("o_done")
        od_ready = sem("od_ready")
        res_landed = sem("res_landed")
        xb_ready = sem("xb_ready")
        x1_ready = sem("x1_ready")
        x1_stored = [sem(f"x1_stored{i}") for i in range(2)]
        ahead = sem("ahead")
        dec_in = [sem(f"dec_in{i}") for i in range(2)]
        dec_used = sem("dec_used")
        u_row_ready = sem("u_row_ready")
        u_stored = sem("u_stored")
        block = ctx.enter_context(nc.Block())

        def has_u(s):
            return not isinstance(s, int) or 0 <= s - U_AT < RANK

        @block.sync
        def _(sp):
            for j in range(4):
                for b in range(B):
                    sp.dma_start(bc[:, j, b, :], rows[j, b:b + 1, :].to_broadcast((P, F))).then_inc(consts_in, 16)
            sp.dma_start(bias_k[:, :], I["k_b"].rearrange("(a f) -> a f", a=1).to_broadcast((P, F))).then_inc(consts_in, 16)
            sp.dma_start(bias_o[:, :], I["o_b"].rearrange("(a f) -> a f", a=1).to_broadcast((P, F))).then_inc(consts_in, 16)
            sp.dma_start(mask_l[:, :], I["mask_l"]).then_inc(consts_in, 16)
            sp.dma_start(mask_r[:, :], I["mask_r"]).then_inc(consts_in, 16)

            def step(s, u_, has):
                if has_u(s - 2):
                    k = s - 2 - U_AT
                    sp.wait_ge(u_row_ready, k + 1)
                    sp.dma_start(u_dram[k], u_row[:, :]).then_inc(u_stored, 16)
                if has(6):
                    t, p = s - 6, u_
                    sp.wait_ge(x1_ready, t + 1)
                    sp.dma_start(x1_tiles[t], x1[p][:, :]).then_inc(x1_stored[p], 16)
                if has(-1):
                    t = s + 1
                    if later(t, 1):
                        sp.wait_ge(xm_ready, t)
                    sp.dma_start(x_in[:, :], x_dram[t]).then_inc(x_landed, 16)
                if has_u(s + 1):
                    k, p = s + 1 - U_AT, (u_ + 1) % 2
                    if later(k, 2):
                        sp.wait_ge(dec_used, k - 1)
                    sp.dma_start(dec[p][:, :, :], I["dec_w"][k].rearrange("(c p) f -> p c f", p=P)).then_inc(dec_in[p], 16)
                if has(4):
                    t = s - 4
                    if later(t, 1):
                        sp.wait_ge(x1_ready, t)
                    sp.dma_start(xb[:, :], x_dram[t]).then_inc(res_landed, 16)
                if isinstance(s, int) and s >= 4 and prefetch:
                    dst, src = prefetch.pop(0)
                    sp.dma_start(dst, src).then_inc(ahead, 16)

            count = len(prefetch)
            steps(sp, step, T + 6, PEEL, 2, first=-1, end=T - 2)
            assert not prefetch
            sp.wait_ge(ahead, 16 * count)
            sp.wait_ge(u_stored, 16 * RANK)
            for p in range(2):
                sp.wait_ge(x1_stored[p], 16 * (T // 2))

        @block.tensor
        def _(pe):
            pe.wait_ge(mask_ready, 2)
            pe.wait_ge(diag_zero, 3)

            def project(out_ps, hi, lo, w_hi, w_lo):
                terms = [(x, w, c) for c in range(C) for x, w in ((hi, w_hi), (hi, w_lo), (lo, w_hi))]
                for n, (x, w, c) in enumerate(terms):
                    mm = nc.tensor.matmul(out_ps[:, :], x[:, c, :], w[:, c, :], start=n == 0, stop=n == len(terms) - 1)
                return mm

            def step(s, u_, has):
                if has(0):
                    pe.wait_ge(xm_ready, s + 1)
                    if later(s, 1):
                        pe.wait_ge(xl_ready, s)
                    for c in range(C):
                        mm = nc.tensor.transpose(ps_x[:, c, :], xm[:, c * P:(c + 1) * P], ident[:, :])
                    mm.then_inc(x_turned, 1)
                if has(2):
                    t, p = s - 2, u_
                    pe.wait_ge(kt_ready, t + 1)
                    if later(t, 1):
                        pe.wait_ge(v_ready, t)
                    for m in range(PR // Q):
                        mm = nc.tensor.transpose(ps_vt[:, m, :], kt[p][:, Q * m:Q * m + Q, :].rearrange("p g h -> p (g h)"), ident[:, :])
                    mm.then_inc(v_turned, 1)
                    pe.wait_ge(k_diag_ready, t + 1)
                    if later(t, 1):
                        pe.wait_ge(low_ready, t)
                    nc.tensor.matmul(ps_s[:, :, :], mask_lr[:, :], mask_rr[:, :], start=True, stop=False, skip_group_check=True)
                    for j in range(PR):
                        m, g = divmod(j, Q)
                        mm = nc.tensor.matmul(ps_s[D * g:D * g + D, Q * m:Q * m + Q, :], kt[p][:, j, :], k_diag[p][:, j, :, :],
                                              start=False, stop=True, skip_group_check=True)
                    mm.then_inc(scores_done, 1)
                if has(5):
                    t = s - 5
                    pe.wait_ge(ol_ready, t + 1)
                    if later(t, 1):
                        pe.wait_ge(od_ready, t)
                    project(ps_o, oh, ol, wo_hi, wo_lo).then_inc(o_done, 1)
                if has(0):
                    pe.wait_ge(xl_ready, s + 1)
                    if later(s, 1):
                        pe.wait_ge(kd_ready, s)
                    project(ps_k, xh, xl, wk_hi, wk_lo).then_inc(k_done, 1)
                if has_u(s):
                    pe.wait_ge(dec_in[u_], 8 * (s - U_AT - u_) + 16)
                    if later(s, U_AT + 1):
                        pe.wait_ge(u_row_ready, s - U_AT)
                    for c in range(S // P):
                        mm = nc.tensor.matmul(ps_u[:, :], cond[:, c, :], dec[u_][:, c, :], start=c == 0, stop=c == S // P - 1)
                    mm.then_inc(dec_used, 1)
                if has(3):
                    t, p = s - 3, (u_ + 1) % 2
                    pe.wait_ge(at_diag_ready, t + 1)
                    pe.wait_ge(v_ready, t + 1)
                    if later(t, 1):
                        pe.wait_ge(ot_ready, t)
                    for j in range(PR):
                        m, q = divmod(j, Q)
                        mm = nc.tensor.matmul(ps_v[D * q:D * q + D, Q * m:Q * m + Q, :, :], v[p][:, m, D * q:D * q + D], at_diag[:, j, :, :],
                                              start=True, stop=True)
                    mm.then_inc(mixed, 1)
                if has(4):
                    t = s - 4
                    pe.wait_ge(om_ready, t + 1)
                    if later(t, 1):
                        pe.wait_ge(ol_ready, t)
                    for c in range(C):
                        mm = nc.tensor.transpose(ps_t[:, c, :], om[:, c * P:(c + 1) * P], ident[:, :])
                    mm.then_inc(o_turned, 1)

            steps(pe, step, LAST, PEEL, 2)

        @block.scalar
        def _(act):
            act.wait_ge(diag_zero, 3)

            def diagonal(dst, src):
                for q in range(Q):
                    g = slice(D * q, D * q + D)
                    last = nc.scalar.activation(dst[g, :, q, :], src[g, :, :], ACT.Copy)
                return last

            def step(s, u_, has):
                if has(5):
                    t = s - 5
                    act.wait_ge(o_turned, t + 1)
                    if later(t, 1):
                        act.wait_ge(o_done, t)
                    nc.scalar.activation(oh[:, :, :], ps_t[:, :, :], ACT.Copy).then_inc(oh_ready, 1)
                if has(3):
                    t = s - 3
                    act.wait_ge(at_ready, t + 1)
                    if later(t, 1):
                        act.wait_ge(mixed, t)
                    diagonal(at_diag, at).then_inc(at_diag_ready, 1)
                if has(0):
                    act.wait_ge(x_turned, s + 1)
                    if later(s, 1):
                        act.wait_ge(k_done, s)
                    nc.scalar.activation(xh[:, :, :], ps_x[:, :, :], ACT.Copy).then_inc(xh_ready, 1)
                if has_u(s - 1):
                    k = s - 1 - U_AT
                    act.wait_ge(dec_used, k + 1)
                    if later(k, 1):
                        act.wait_ge(u_stored, 16 * k)
                    nc.scalar.activation(u_row[:, :], ps_u[:, :], ACT.Copy).then_inc(u_row_ready, 1)
                if has(2):
                    t, p = s - 2, u_
                    act.wait_ge(v_turned, t + 1)
                    if later(t, 2):
                        act.wait_ge(mixed, t - 1)
                    nc.scalar.activation(v[p][:, :, :], ps_vt[:, :, :], ACT.Copy).then_inc(v_ready, 1)
                if has(1):
                    t, p = s - 1, (u_ + 1) % 2
                    act.wait_ge(kt_ready, t + 1)
                    if later(t, 2):
                        act.wait_ge(scores_done, t - 1)
                    diagonal(k_diag[p], kt[p]).then_inc(k_diag_ready, 1)
                if has(2):
                    t = s - 2
                    act.wait_ge(low_ready, t + 1)
                    if later(t, 1):
                        act.wait_ge(at_ready, t)
                    nc.scalar.activation(e[:, :, :], low[:, :, :], ACT.Exp, scale=float(D) ** -0.5).then_inc(e_ready, 1)

            steps(act, step, LAST, PEEL, 2)

        @block.vector
        def _(dve):
            for d in (*k_diag, at_diag):
                nc.vector.memset(d[:, :, :, :], 0.0).then_inc(diag_zero, 1)
            dve.wait_ge(consts_in, 16 * 12)
            nc.vector.tensor_copy(mask_lr[:, :], mask_l[:, :]).then_inc(mask_ready, 1)
            nc.vector.tensor_copy(mask_rr[:, :], mask_r[:, :]).then_inc(mask_ready, 1)

            def step(s, u_, has):
                if has(5):
                    t = s - 5
                    dve.wait_ge(oh_ready, t + 1)
                    nc.vector.tensor_tensor(ol[:, :, :], ps_t[:, :, :], oh[:, :, :].bitcast(F32), ALU.subtract).then_inc(ol_ready, 1)
                if has(4):
                    t = s - 4
                    dve.wait_ge(mixed, t + 1)
                    if later(t, 1):
                        dve.wait_ge(o_turned, t)
                    nc.vector.transpose(om[:, :].rearrange("p (h a c) -> p h a c", h=H, c=2),
                                        ps_v[:, :, :, :].rearrange("p a h c -> p h a c")).then_inc(ot_ready, 1)
                if has(0):
                    dve.wait_ge(xh_ready, s + 1)
                    nc.vector.tensor_tensor(xl[:, :, :], ps_x[:, :, :], xh[:, :, :].bitcast(F32), ALU.subtract).then_inc(xl_ready, 1)
                if has(5):
                    t = s - 5
                    dve.wait_ge(o_done, t + 1)
                    if later(t, 1):
                        dve.wait_ge(x1_ready, t)
                    nc.vector.tensor_tensor(od[:, :], ps_o[:, :], bc[:, DEMOD_O, t // TB, :], ALU.mult).then_inc(od_ready, 1)
                if has(2):
                    t = s - 2
                    dve.wait_ge(scores_done, t + 1)
                    if later(t, 1):
                        dve.wait_ge(low_ready, t)
                    nc.vector.reduce_max(mx[:, :], ps_s[:, :, :], axis=AX).then_inc(mx_ready, 1)
                    dve.wait_ge(mx_ready, t + 1)
                    if later(t, 1):
                        dve.wait_ge(e_ready, t)
                    nc.vector.tensor_tensor(low[:, :, :], ps_s[:, :, :], mx[:, :].unsqueeze(2).to_broadcast((P, PR, D)),
                                            ALU.subtract).then_inc(low_ready, 1)
                    dve.wait_ge(e_ready, t + 1)
                    if later(t, 1):
                        dve.wait_ge(rinv_ready, t)
                    nc.vector.reduce_sum(total[:, :], e[:, :, :], axis=AX).then_inc(total_ready, 1)
                    dve.wait_ge(total_ready, t + 1)
                    if later(t, 1):
                        dve.wait_ge(a_ready, t)
                    nc.vector.reciprocal(rinv[:, :], total[:, :]).then_inc(rinv_ready, 1)
                if has(0):
                    dve.wait_ge(k_done, s + 1)
                    if later(s, 1):
                        dve.wait_ge(kt_ready, s)
                    nc.vector.tensor_tensor(kb[:, :], ps_k[:, :], bc[:, DEMOD_K, s // TB, :], ALU.mult).then_inc(kd_ready, 1)
                if has(2):
                    t = s - 2
                    dve.wait_ge(a_ready, t + 1)
                    if later(t, 1):
                        dve.wait_ge(at_diag_ready, t)
                    nc.vector.transpose(at[:, :, :], e[:, :, :]).then_inc(at_ready, 1)
                if has(0):
                    dve.wait_ge(kb_ready, s + 1)
                    if later(s, 2):
                        dve.wait_ge(scores_done, s - 1)
                    nc.vector.transpose(kt[u_][:, :, :].rearrange("p a (h c) -> p h a c", c=2),
                                        kb[:, :].rearrange("p (h a c) -> p h a c", h=H, c=2)).then_inc(kt_ready, 1)

            steps(dve, step, LAST, PEEL, 2)

        @block.gpsimd
        def _(pool):
            pool.wait_ge(consts_in, 16 * 12)

            def step(s, u_, has):
                if has(4):
                    t = s - 4
                    pool.wait_ge(ot_ready, t + 1)
                    nc.gpsimd.tensor_tensor(om[:, :], om[:, :], bc[:, STYLE_O, t // TB, :], ALU.mult).then_inc(om_ready, 1)
                if has(5):
                    t, p = s - 5, (u_ + 1) % 2
                    pool.wait_ge(res_landed, 16 * (t + 1))
                    nc.gpsimd.tensor_tensor(xb[:, :], xb[:, :], bias_o[:, :], ALU.add).then_inc(xb_ready, 1)
                if has(-1):
                    t = s + 1
                    pool.wait_ge(x_landed, 16 * (t + 1))
                    if later(t, 1):
                        pool.wait_ge(x_turned, t)
                    nc.gpsimd.tensor_tensor(xm[:, :], x_in[:, :], bc[:, STYLE_K, t // TB, :], ALU.mult).then_inc(xm_ready, 1)
                if has(5):
                    t, p = s - 5, (u_ + 1) % 2
                    pool.wait_ge(od_ready, t + 1)
                    pool.wait_ge(xb_ready, t + 1)
                    if later(t, 2):
                        pool.wait_ge(x1_stored[p], 8 * (t - p))
                    nc.gpsimd.tensor_tensor(x1[p][:, :], od[:, :], xb[:, :], ALU.add).then_inc(x1_ready, 1)
                if has(2):
                    t = s - 2
                    pool.wait_ge(rinv_ready, t + 1)
                    nc.gpsimd.tensor_tensor(e[:, :, :], e[:, :, :], rinv[:, :].unsqueeze(2).to_broadcast((P, PR, D)),
                                            ALU.mult).then_inc(a_ready, 1)
                if has(0):
                    pool.wait_ge(kd_ready, s + 1)
                    nc.gpsimd.tensor_tensor(kb[:, :], kb[:, :], bias_k[:, :], ALU.add).then_inc(kb_ready, 1)

            steps(pool, step, LAST, PEEL, 2, first=-1, end=T - 2)


def conditions(nc, sems, I, rows, ident, cond, u_dram, w1, w2, wv, table_t, u_hi_lo, v_hi, v_lo):
    with ExitStack() as ctx:
        sb, ps, sem = allocator(nc, ctx, sems)
        c64 = sb("c64", [64, B])
        c32 = sb("c32", [32, B])
        aw = sb("aw", [P, 6])
        aw_max = sb("aw_max", [P, 1])
        aw_low = sb("aw_low", [P, 6])
        aw_exp = sb("aw_exp", [P, 6])
        aw_sum = sb("aw_sum", [P, 1])
        aw_inv = sb("aw_inv", [P, 1])
        vec = sb("vec", [B, 4, 3, F])
        hb = sb("hb", [B, 3, F])
        hs = sb("hs", [B, 3, F])
        hs_t = sb("hs_t", [P, 3, C, B])
        h2 = sb("h2", [B, 3, F])
        stats = sb("c_stats", [B, 3, 6])
        mean_var = sb("c_mean_var", [B, 3, 2])
        var_eps = sb("c_var_eps", [B, 3])
        half = sb("c_half", [B, 3])
        rstd = sb("c_rstd", [B, 3])
        hn = sb("c_hn", [B, 3, F])
        table = sb("table", [TABLE, 6, F])
        last_w = sb("last_w", [P, S // P, RANK])
        last_b = sb("last_b", [RANK, 1])
        last_u = sb("last_u", [RANK, B])
        v = sb("v_rows", [P, F])
        bias1 = sb("bias1", [B, F])
        u_rows = sb("u_rows", [RANK * B, F])
        dec_b = sb("dec_b", [P, C, RANK])
        u = sb("u", [P, C, RANK, B])

        ps_h = ps("ps_h", [B, 3, 512])
        ps_turn = ps("c_ps_turn", [P, 3, C, B])
        ps_table = ps("ps_table_t", [P, 6, C, TABLE])
        ps_last = ps("ps_last", [RANK, B])
        ps_bias = ps("ps_bias", [B, F])
        ps_u = ps("c_ps_u", [P, C, RANK, B])

        in_first = sem("in_first")
        in_mlp = sem("in_mlp")
        in_u = sem("in_u")
        u_turned = sem("u_turned")
        u_ready = sem("u_ready")
        in_table = sem("in_table")
        in_v = sem("in_v")
        zeroed = sem("zeroed")
        aw_step = sem("aw_step")
        aw_exp_ready = sem("aw_exp_ready")
        wv_ready = sem("wv_ready")
        h_mm = sem("h_mm")
        hb_ready = sem("hb_ready")
        hs_ready = sem("hs_ready")
        hs_turned = sem("hs_turned")
        hs_t_ready = sem("hs_t_ready")
        h2_mm = sem("h2_mm")
        h2_ready = sem("h2_ready")
        stats_ready = sem("c_stats_ready")
        mv_ready = sem("c_mv_ready")
        var_ready = sem("c_var_ready")
        rstd_ready = sem("c_rstd_ready")
        ln_step = sem("ln_step")
        table_ready = sem("table_ready")
        table_turned = sem("table_turned")
        last_mm = sem("last_mm")
        last_ready = sem("last_ready")
        bias_mm = sem("bias_mm")
        bias_ready = sem("bias_ready")
        bias_out = sem("bias_out")
        u_hi_ready = sem("u_hi_ready")
        v_hi_ready = sem("v_hi_ready")
        block = ctx.enter_context(nc.Block())

        @block.sync
        def _(sp):
            sp.dma_start(aw[:, :], I["aw"].rearrange("(a f) -> a f", a=1).to_broadcast((P, 6))).then_inc(in_first, 16)
            sp.dma_start(last_w[:, :, :], I["dec_last_w"].rearrange("(c p) k -> p c k", p=P)).then_inc(in_first, 16)
            sp.dma_start(last_b[:, :], I["dec_last_b"]).then_inc(in_first, 16)
            sp.dma_start(u_rows[:, :], u_dram.rearrange("k b f -> (k b) f")).then_inc(in_u, 16)
            sp.dma_start(dec_b[:, :, :], I["dec_b"].rearrange("(c p) k -> p c k", p=P)).then_inc(in_u, 16)
            sp.dma_start(c64[:, :], I["cond64_t"]).then_inc(in_mlp, 16)
            sp.dma_start(c32[:, :], I["fside_t"]).then_inc(in_mlp, 16)
            for j, n in enumerate(MLPS):
                for i, m in enumerate(("b1", "b2", "g", "be")):
                    sp.dma_start(vec[:, i, j, :], I[f"{n}_{m}"].rearrange("(a f) -> a f", a=1).to_broadcast((B, F))).then_inc(in_mlp, 16)
            sp.wait_ge(zeroed, 2)
            sp.dma_start(table[TABLE_COMP:TABLE_COMP + 5, 0, :], I["cp_b"]).then_inc(in_table, 16)
            sp.dma_start(table[TABLE_COMP:TABLE_COMP + 5, 1, :], I["tm_b"]).then_inc(in_table, 16)
            sp.dma_start(table[TABLE_SCALE:TABLE_SCALE + 3, 5, :], I["ms_b"]).then_inc(in_table, 16)
            for q in range(Q):
                sp.dma_start(v[32 * q:32 * q + RANK, :], I["V"]).then_inc(in_v, 16)
            sp.wait_ge(bias_ready, 1)
            sp.dma_start(rows[BIAS_1], bias1[:, :]).then_inc(bias_out, 16)
            sp.wait_ge(bias_out, 16)

        @block.tensor
        def _(pe):
            pe.wait_ge(in_first, 16 * 3)
            for c in range(S // P):
                mm = nc.tensor.matmul(ps_last[:, :], last_w[:, c, :], cond[:, c, :], start=c == 0, stop=c == S // P - 1)
            mm.then_inc(last_mm, 1)
            pe.wait_ge(in_u, 16 * 2)
            for c in range(C):
                mm = nc.tensor.transpose(ps_u[:, c, :, :].rearrange("p k b -> p (k b)"), u_rows[:, c * P:(c + 1) * P],
                                         ident[0:RANK * B, 0:RANK * B])
            mm.then_inc(u_turned, 1)
            pe.wait_ge(in_mlp, 16 * 14)
            for c in range(S // P):
                nc.tensor.matmul(ps_h[:, 0, :], cond[:, c, :], w1[0][:, c, :], start=c == 0, stop=c == S // P - 1)
            nc.tensor.matmul(ps_h[:, 1, :], c64[:, :], w1[1][:, 0, :], start=True, stop=True)
            nc.tensor.matmul(ps_h[:, 2, :], c32[:, :], w1[2][:, 0, :], start=True, stop=True).then_inc(h_mm, 1)
            pe.wait_ge(hs_ready, 1)
            for j in range(3):
                for c in range(C):
                    mm = nc.tensor.transpose(ps_turn[:, j, c, :], hs[:, j, c * P:(c + 1) * P], ident[0:B, 0:B])
            mm.then_inc(hs_turned, 1)
            pe.wait_ge(hs_t_ready, 1)
            for j in range(3):
                for c in range(C):
                    mm = nc.tensor.matmul(ps_h[:, j, :], hs_t[:, j, c, :], w2[j][:, c, :], start=c == 0, stop=c == C - 1)
            mm.then_inc(h2_mm, 1)
            pe.wait_ge(last_ready, 1)
            pe.wait_ge(in_v, 16 * Q)
            nc.tensor.matmul(ps_bias[:, :], last_u[:, :], v[0:RANK, :], start=True, stop=True).then_inc(bias_mm, 1)
            pe.wait_ge(table_ready, 1)
            pe.wait_ge(in_table, 16 * 3)
            for j in range(6):
                for c in range(C):
                    mm = nc.tensor.transpose(ps_table[:, j, c, :], table[:, j, c * P:(c + 1) * P], ident[0:TABLE, 0:TABLE])
            mm.then_inc(table_turned, 1)

        @block.scalar
        def _(act):
            act.wait_ge(aw_step, 2)
            nc.scalar.activation(aw_exp[:, :], aw_low[:, :], ACT.Exp).then_inc(aw_exp_ready, 1)
            act.wait_ge(hb_ready, 1)
            nc.scalar.activation(hs[:, :, :], hb[:, :, :], ACT.Silu).then_inc(hs_ready, 1)

        @block.vector
        def _(dve):
            nc.vector.memset(table[:, :, :], 0.0).then_inc(zeroed, 1)
            nc.vector.memset(v[:, :], 0.0).then_inc(zeroed, 1)
            nc.vector.memset(u_hi_lo[:, :, :, :].bitcast(F32), 0.0).then_inc(zeroed, 1)
            nc.vector.memset(half[:, :], -0.5).then_inc(zeroed, 1)
            dve.wait_ge(in_first, 16 * 3)
            nc.vector.reduce_max(aw_max[:, :], aw[:, :], axis=AX).then_inc(aw_step, 1)
            dve.wait_ge(aw_step, 1)
            nc.vector.tensor_scalar(aw_low[:, :], aw[:, :], aw_max[:, 0:1], None, ALU.subtract).then_inc(aw_step, 1)
            dve.wait_ge(aw_exp_ready, 1)
            nc.vector.reduce_sum(aw_sum[:, :], aw_exp[:, :], axis=AX).then_inc(aw_step, 1)
            dve.wait_ge(aw_step, 3)
            nc.vector.reciprocal(aw_inv[:, :], aw_sum[:, :]).then_inc(aw_step, 1)
            dve.wait_ge(aw_step, 4)
            nc.vector.tensor_scalar(wv[:, :], aw_exp[:, :], aw_inv[:, 0:1], None, ALU.mult).then_inc(wv_ready, 1)
            dve.wait_ge(last_mm, 1)
            nc.vector.tensor_scalar(last_u[:, :], ps_last[:, :], last_b[:, 0:1], None, ALU.add).then_inc(last_ready, 1)
            dve.wait_ge(u_turned, 1)
            nc.vector.tensor_tensor(u[:, :, :, :], ps_u[:, :, :, :], dec_b[:, :, :].unsqueeze(3).to_broadcast((P, C, RANK, B)),
                                    ALU.add).then_inc(u_ready, 1)
            dve.wait_ge(h_mm, 1)
            nc.vector.tensor_tensor(hb[:, :, :], ps_h[:, :, :], vec[:, 0, :, :], ALU.add).then_inc(hb_ready, 1)
            dve.wait_ge(hs_turned, 1)
            nc.vector.tensor_copy(hs_t[:, :, :, :], ps_turn[:, :, :, :]).then_inc(hs_t_ready, 1)
            dve.wait_ge(h2_mm, 1)
            nc.vector.tensor_tensor(h2[:, :, :], ps_h[:, :, :], vec[:, 1, :, :], ALU.add).then_inc(h2_ready, 1)
            dve.wait_ge(h2_ready, 1)
            for j in range(3):
                nc.vector.bn_stats(stats[:, j, :], h2[:, j, :]).then_inc(stats_ready, 1)
            dve.wait_ge(stats_ready, 3)
            for j in range(3):
                nc.vector.bn_aggr(mean_var[:, j, :], stats[:, j, :]).then_inc(mv_ready, 1)
            dve.wait_ge(mv_ready, 3)
            nc.vector.tensor_scalar(var_eps[:, :], mean_var[:, :, 1], 1e-5, None, ALU.add).then_inc(var_ready, 1)
            dve.wait_ge(rstd_ready, 1)
            for j in range(3):
                nc.vector.tensor_scalar(hn[:, j, :], h2[:, j, :], mean_var[:, j, 0:1], rstd[:, j:j + 1],
                                        ALU.subtract, ALU.mult).then_inc(ln_step, 1)
            dve.wait_ge(ln_step, 3)
            nc.vector.tensor_tensor(h2[:, :, :], hn[:, :, :], vec[:, 2, :, :], ALU.mult).then_inc(ln_step, 1)
            dve.wait_ge(ln_step, 4)
            nc.vector.tensor_tensor(table[0:B, 2:5, :], h2[:, :, :], vec[:, 3, :, :], ALU.add).then_inc(table_ready, 1)
            dve.wait_ge(bias_mm, 1)
            nc.vector.tensor_copy(bias1[:, :], ps_bias[:, :]).then_inc(bias_ready, 1)
            dve.wait_ge(in_v, 16 * Q)
            nc.vector.tensor_copy(v_hi[:, :], v[:, :]).then_inc(v_hi_ready, 1)
            dve.wait_ge(v_hi_ready, 1)
            nc.vector.tensor_tensor(v_lo[:, :], v[:, :], v_hi[:, :].bitcast(F32), ALU.subtract)
            dve.wait_ge(zeroed, 4)
            dve.wait_ge(u_ready, 1)
            for b in range(B):
                for k in (0, 64):
                    nc.vector.tensor_copy(u_hi_lo[:, b, :, k:k + RANK], u[:, :, :, b]).then_inc(u_hi_ready, 1)
            dve.wait_ge(u_hi_ready, 2 * B)
            for b in range(B):
                for k in (0, 64):
                    nc.vector.tensor_tensor(u_hi_lo[:, b, :, k + 32:k + 32 + RANK], u[:, :, :, b],
                                            u_hi_lo[:, b, :, k:k + RANK].bitcast(F32), ALU.subtract)
            dve.wait_ge(table_turned, 1)
            dve.wait_ge(wv_ready, 1)
            for j in range(6):
                nc.vector.tensor_scalar(table_t[:, j, :, :], ps_table[:, j, :, :], wv[:, j:j + 1], None, ALU.mult)

        @block.gpsimd
        def _(pool):
            pool.wait_ge(var_ready, 1)
            pool.wait_ge(zeroed, 4)
            nc.gpsimd.tensor_tensor(rstd[:, :], var_eps[:, :], half[:, :], ALU.pow).then_inc(rstd_ready, 1)


LOADS = ("w_2_t", "int_W2", 2, 3, 4, 0, 1, 5)
PARTS = ("2", "out", "h", "t", "x", "s")


def weights(nc, sems, I, raw, wv, table_t, Wt, tab):
    raw_n = len(raw)
    with ExitStack() as ctx:
        sb, ps, sem = allocator(nc, ctx, sems)
        acc = [sb(f"acc{i}", [P, C, F]) for i in range(2)]
        tab_bias = sb("tab_bias", [TABLE, F])
        tab_sum = sb("tab_sum", [TABLE, F])
        ps_tab = ps("ps_tab", [TABLE, F])
        raw_in = [sem(f"raw_in{i}") for i in range(raw_n)]
        hi_ready = sem("w_hi_ready")
        item_done = sem("item_done")
        tab_used = sem("tab_used")
        acc_ready = sem("acc_ready")
        acc_hi = sem("acc_hi")
        bias_zero = sem("bias_zero")
        bias_in = sem("bias_in")
        tab_sum_ready = sem("tab_sum_ready")
        tab_hi_ready = sem("tab_hi_ready")
        tab_zero = sem("tab_zero")
        block = ctx.enter_context(nc.Block())
        dest = {"w_2_t": "2", "int_W2": "out", 0: "h", 1: "t", 5: "s"}

        @block.sync
        def _(sp):
            for i, item in enumerate(LOADS):
                if i >= raw_n:
                    sp.wait_ge(item_done, i - raw_n + 1)
                    if i - raw_n >= 2:
                        sp.wait_ge(tab_used, i - raw_n - 1)
                src = I[item] if isinstance(item, str) else I["int_W1"][item * F:(item + 1) * F, :]
                sp.dma_start(raw[i % raw_n][:, :, :], src.rearrange("(c p) f -> p c f", p=P)).then_inc(raw_in[i % raw_n], 16)
                if i == 1:
                    sp.wait_ge(bias_zero, 1)
                    sp.dma_start(tab_bias[0:B, :], I["int_b1"].rearrange("(a f) -> a f", a=1).to_broadcast((B, F))).then_inc(bias_in, 16)

        @block.tensor
        def _(pe):
            for i, item in enumerate(LOADS[2:]):
                pe.wait_ge(raw_in[(i + 2) % raw_n], 16 * ((i + 2) // raw_n + 1))
                for c in range(C):
                    mm = nc.tensor.matmul(ps_tab[:, :], table_t[:, item, c, :], raw[(i + 2) % raw_n][:, c, :],
                                          start=i == 0 and c == 0, stop=i == 5 and c == C - 1)
                mm.then_inc(tab_used, 1)

        @block.scalar
        def _(act):
            n = 0
            for i, item in enumerate(LOADS):
                if item in dest:
                    act.wait_ge(raw_in[i % raw_n], 16 * (i // raw_n + 1))
                    scale = wv[:, item:item + 1] if isinstance(item, int) else 1.0
                    nc.scalar.activation(Wt[dest[item]][0][:, :, :], raw[i % raw_n][:, :, :], ACT.Copy, scale=scale).then_inc(hi_ready, 1)
                elif item == 4:
                    act.wait_ge(acc_ready, 3)
                    nc.scalar.activation(Wt["x"][0][:, :, :], acc[0][:, :, :], ACT.Copy).then_inc(hi_ready, 1)

        @block.vector
        def _(dve):
            nc.vector.memset(tab_bias[:, :], 0.0).then_inc(bias_zero, 1)
            nc.vector.memset(tab[:, :].bitcast(F32), 0.0).then_inc(tab_zero, 1)
            hi = 0
            for i, item in enumerate(LOADS):
                r = raw[i % raw_n]
                dve.wait_ge(raw_in[i % raw_n], 16 * (i // raw_n + 1))
                if item in dest:
                    hi += 1
                    dve.wait_ge(hi_ready, hi)
                    w_hi, w_lo = Wt[dest[item]]
                    if isinstance(item, str):
                        nc.vector.tensor_tensor(w_lo[:, :, :], r[:, :, :], w_hi[:, :, :].bitcast(F32), ALU.subtract).then_inc(item_done, 1)
                    else:
                        nc.vector.scalar_tensor_tensor(w_lo[:, :, :].rearrange("p c f -> p (c f)"), r[:, :, :].rearrange("p c f -> p (c f)"), wv[:, item:item + 1],
                                                       w_hi[:, :, :].bitcast(F32).rearrange("p c f -> p (c f)"), ALU.mult, ALU.subtract).then_inc(item_done, 1)
                elif item == 2:
                    nc.vector.tensor_scalar(acc[0][:, :, :], r[:, :, :], wv[:, 2:3], None, ALU.mult).then_inc(item_done, 1)
                    dve.wait_ge(item_done, 3)
                    nc.vector.tensor_copy(tab_sum[:, :], tab_bias[:, :]).then_inc(acc_ready, 1)
                elif item == 3:
                    nc.vector.scalar_tensor_tensor(acc[1][:, :, :], r[:, :, :], wv[:, 3:4], acc[0][:, :, :], ALU.mult, ALU.add).then_inc(item_done, 1)
                    dve.wait_ge(item_done, 4)
                else:
                    nc.vector.scalar_tensor_tensor(acc[0][:, :, :], r[:, :, :], wv[:, 4:5], acc[1][:, :, :], ALU.mult, ALU.add).then_inc(item_done, 1)
                    dve.wait_ge(item_done, 5)
                    nc.vector.engine_nop().then_inc(acc_ready, 2)
                    hi += 1
                    dve.wait_ge(hi_ready, hi)
                    nc.vector.tensor_tensor(Wt["x"][1][:, :, :], acc[0][:, :, :], Wt["x"][0][:, :, :].bitcast(F32), ALU.subtract)
            dve.wait_ge(tab_used, 6)
            dve.wait_ge(bias_in, 16)
            nc.vector.tensor_tensor(tab_sum[:, :], ps_tab[:, :], tab_bias[:, :], ALU.add).then_inc(tab_sum_ready, 1)
            dve.wait_ge(tab_sum_ready, 1)
            dve.wait_ge(tab_zero, 1)
            nc.vector.tensor_copy(tab[0:TABLE, :], tab_sum[:, :]).then_inc(tab_hi_ready, 1)
            dve.wait_ge(tab_hi_ready, 1)
            nc.vector.tensor_tensor(tab[LOW:LOW + TABLE, :], tab_sum[:, :], tab[0:TABLE, :].bitcast(F32), ALU.subtract)


def cascade(nc, sems, I, rows, ident, Wt, tab, u_hi_lo, v_hi, v_lo, x1_dram, out):
    x1_tiles = x1_dram.rearrange("(t p) f -> t p f", p=P)
    out_tiles = out.rearrange("(t p) f -> t p f", p=P)
    with ExitStack() as ctx:
        sb, ps, sem = allocator(nc, ctx, sems)
        style2 = sb("style2", [P, B, F])
        demod2 = sb("demod2", [P, B, F])
        bias1 = sb("bias1_bc", [P, B, F])
        bias2 = sb("bias2", [P, F])
        b2 = sb("b2", [P, F])
        gain = sb("gain", [P, F])
        shift = sb("shift", [P, F])
        half = sb("half", [P, 1])
        codes = sb("codes", [2 * LOW, 1])
        ids = sb("ids", [P, 3, T], I32)
        x1 = sb("x1", [P, F])
        x1b = sb("x1b", [P, F])
        u_now = sb("u_now", [P, C, P], F32R)
        z = sb("z", [P, P], F32R)
        x2 = sb("x2", [P, 2, F])
        xm2 = sb("xm2", [P, F])
        yd = sb("yd", [P, F])
        x3 = sb("x3", [P, F])
        x3s = sb("x3s", [P, 4, F])
        stats = sb("stats", [P, 3, 6])
        mean_var = sb("mean_var", [P, 3, 2])
        var_eps = sb("var_eps", [P, 3])
        rstd = sb("rstd", [P, 3])
        shift_n = sb("shift_n", [P, 3])
        xn = sb("xn", [P, F])
        tt = sb("tt", [P, F])
        ss = sb("ss", [P, F])
        h1 = sb("h1", [P, F])
        h = sb("h", [P, F])
        g = sb("act_g", [P, F])
        f2 = sb("f2", [P, F])
        o = sb("o", [P, F])
        names = ("x1", "x2", "x3", "t", "s", "h", "g")
        own = ("x1", "x2", "x3", "t", "g")
        hi = {n: sb(f"{n}_hi", [P, C, P], F32R) for n in own}
        lo = {n: sb(f"{n}_lo", [P, C, P], F32R) for n in own}
        for n, m in (("s", "x1"), ("h", "x2")):
            hi[n], lo[n] = hi[m], lo[m]
        pid = sb("pid", [P, 3], I32)
        path = sb("path", [P, 2 * F])
        comp = sb("comp", [P, 2 * F])
        scal = sb("scal", [P, F])
        id_rows = sb("id_rows", [2 * LOW, P], I32)
        one_hot = sb("one_hot", [2 * LOW, P], F32R)

        tp = [ps(f"tp{i}", [P, C, P]) for i in range(3)]
        ps_z = ps("ps_z", [P, P])
        ps_1 = ps("ps_1", [P, F])
        ps_2 = ps("ps_2", [P, F])
        ps_3 = ps("ps_3", [P, F])
        ps_4 = ps("ps_4", [P, F])

        consts_in = sem("c2_in")
        half_ready = sem("half_ready2")
        x1_in = sem("x1_in")
        rows_in = sem("id_rows_in")
        pid_ready = sem("pid_ready")
        path_in = sem("path_in")
        comp_in = sem("comp_in")
        scal_in = sem("scal_in")
        u_now_ready = sem("u_now_ready")
        x1b_ready = sem("x1b_ready")
        turned = {n: sem(f"{n}_turned") for n in names}
        hi_ready = {n: sem(f"{n}_hi_ready") for n in names}
        lo_ready = {n: sem(f"{n}_lo_ready") for n in names}
        u_done = sem("u_done")
        z_hi_ready = sem("z_hi_ready")
        z_ready = sem("z_ready")
        v_done = sem("v_done")
        x2_ready = sem("x2_ready")
        xm2_ready = sem("xm2_ready")
        l2_done = sem("l2_done")
        yd_ready = sem("yd_ready")
        yb_ready = sem("yb_ready")
        yc_ready = sem("yc_ready")
        x3_ready = sem("x3_ready")
        x3s_ready = sem("x3s_ready")
        st_ready = [sem(f"st_ready{i}") for i in range(3)]
        mv_ready = [sem(f"mv_ready{i}") for i in range(3)]
        var_ready = [sem(f"var_ready{i}") for i in range(3)]
        rstd_ready = [sem(f"rstd_ready{i}") for i in range(3)]
        shift_ready = [sem(f"shift_ready{i}") for i in range(3)]
        xn_ready = sem("xn_ready")
        t_ready = sem("t_ready")
        s_ready = sem("s_ready")
        h1_ready = sem("h1_ready")
        h1b_ready = sem("h1b_ready")
        hn_ready = sem("hn_ready")
        h_ready = sem("h_ready")
        hot_ready = sem("hot_ready")
        l3x_done = sem("l3x_done")
        l3t_done = sem("l3t_done")
        l3s_done = sem("l3s_done")
        l3_done = sem("l3_done")
        g_ready = sem("act_g_ready")
        l4_done = sem("l4_done")
        f2_ready = sem("f2_ready")
        fn_ready = sem("fn_ready")
        fg_ready = sem("fg_ready")
        o_ready = sem("o_ready")
        stored = sem("stored")
        dve_passed = sem("dve_passed")
        pool_passed = sem("pool_passed")
        block = ctx.enter_context(nc.Block())
        LN1, LN2, LN3 = range(3)

        def row(name):
            return I[name].rearrange("(a f) -> a f", a=1).to_broadcast((P, F))

        @block.sync
        def _(sp):
            for b in range(B):
                sp.dma_start(style2[:, b, :], rows[STYLE_2, b:b + 1, :].to_broadcast((P, F))).then_inc(consts_in, 16)
                sp.dma_start(demod2[:, b, :], rows[DEMOD_2, b:b + 1, :].to_broadcast((P, F))).then_inc(consts_in, 16)
                sp.dma_start(bias1[:, b, :], rows[BIAS_1, b:b + 1, :].to_broadcast((P, F))).then_inc(consts_in, 16)
            for dst, name in ((bias2, "bias_2"), (b2, "int_b2"), (gain, "int_g"), (shift, "int_be")):
                sp.dma_start(dst[:, :], row(name)).then_inc(consts_in, 16)
            sp.dma_start(codes[:, :], I["codes"]).then_inc(consts_in, 16)
            sp.dma_start(ids[:, :, :], I["ids"]).then_inc(consts_in, 16)

            def step(s, u, has):
                if has(5):
                    t = s - 5
                    sp.wait_ge(o_ready, t + 1)
                    sp.dma_start(out_tiles[t], o[:, :]).then_inc(stored, 16)
                if has(-1):
                    n = s + 1
                    if later(n, 1):
                        sp.wait_ge(turned["x1"], n)
                        sp.wait_ge(x1b_ready, n)
                    sp.dma_start(x1[:, :], x1_tiles[n]).then_inc(x1_in, 16)
                if has(2):
                    t = s - 2
                    if later(t, 1):
                        sp.wait_ge(hot_ready, t)
                    sp.dma_start(id_rows[:, :], I["id_rows"][t]).then_inc(rows_in, 16)

            steps(sp, step, T + 5, 5, 1, first=-1, end=T - 1)
            sp.wait_ge(stored, 16 * T)

        def product(out_ps, a, w, first=True, last=True):
            terms = [(x, y, c) for c in range(C) for x, y in ((hi[a], w[0]), (hi[a], w[1]), (lo[a], w[0]))]
            for n, (x, y, c) in enumerate(terms):
                mm = nc.tensor.matmul(out_ps[:, :], x[:, c, :], y[:, c, :], start=first and n == 0, stop=last and n == len(terms) - 1)
            return mm

        def turn(src, bank):
            for c in range(C):
                mm = nc.tensor.transpose(bank[:, c, :], src[:, c * P:(c + 1) * P], ident[:, :])
            return mm

        @block.tensor
        def _(pe):
            def step(s, u, has):
                a, b, c, d = s, s - 1, s - 2, s - 3
                if has(1):
                    pe.wait_ge(xm2_ready, b + 1)
                    if later(b, 2):
                        pe.wait_ge(lo_ready["h"], b - 1)
                    turn(xm2, tp[0]).then_inc(turned["x2"], 1)
                if has(2):
                    pe.wait_ge(x3_ready, c + 1)
                    if later(c, 2):
                        pe.wait_ge(lo_ready["g"], c - 1)
                    turn(x3, tp[2]).then_inc(turned["x3"], 1)
                    pe.wait_ge(t_ready, c + 1)
                    if has(0):
                        pe.wait_ge(lo_ready["x1"], a + 1)
                    turn(tt, tp[1]).then_inc(turned["t"], 1)
                if has(0):
                    pe.wait_ge(lo_ready["x1"], a + 1)
                    pe.wait_ge(u_now_ready, a + 1)
                    if later(a, 1):
                        pe.wait_ge(z_ready, a)
                    for n, x in enumerate((hi["x1"], lo["x1"])):
                        for k in range(C):
                            mm = nc.tensor.matmul(ps_z[:, :], u_now[:, k, :], x[:, k, :], start=n == 0 and k == 0, stop=n == 1 and k == C - 1)
                    mm.then_inc(u_done, 1)
                if has(1):
                    pe.wait_ge(lo_ready["x2"], b + 1)
                    if later(b, 1):
                        pe.wait_ge(yd_ready, b)
                    product(ps_2, "x2", Wt["2"]).then_inc(l2_done, 1)
                if has(3):
                    pe.wait_ge(g_ready, d + 1)
                    if has(2):
                        pe.wait_ge(lo_ready["x3"], c + 1)
                    turn(g, tp[2]).then_inc(turned["g"], 1)
                if has(0):
                    pe.wait_ge(z_ready, a + 1)
                    if later(a, 1):
                        pe.wait_ge(x2_ready, a)
                    nc.tensor.matmul(ps_1[:, :], z[:, :], v_hi[:, :], start=True, stop=False)
                    nc.tensor.matmul(ps_1[:, :], z[:, :], v_lo[:, :], start=False, stop=True).then_inc(v_done, 1)
                if has(2):
                    pe.wait_ge(lo_ready["x3"], c + 1)
                    if later(c, 1):
                        pe.wait_ge(g_ready, c)
                    product(ps_3, "x3", Wt["x"], last=False).then_inc(l3x_done, 1)
                    pe.wait_ge(s_ready, c + 1)
                    pe.wait_ge(lo_ready["t"], c + 1)
                    turn(ss, tp[1]).then_inc(turned["s"], 1)
                    product(ps_3, "t", Wt["t"], first=False, last=False).then_inc(l3t_done, 1)
                if has(3):
                    pe.wait_ge(lo_ready["g"], d + 1)
                    if later(d, 1):
                        pe.wait_ge(f2_ready, d)
                    product(ps_4, "g", Wt["out"]).then_inc(l4_done, 1)
                if has(2):
                    pe.wait_ge(h_ready, c + 1)
                    if has(1):
                        pe.wait_ge(lo_ready["x2"], b + 1)
                    turn(h, tp[0]).then_inc(turned["h"], 1)
                    pe.wait_ge(lo_ready["s"], c + 1)
                    product(ps_3, "s", Wt["s"], first=False, last=False).then_inc(l3s_done, 1)
                if has(-1):
                    pe.wait_ge(x1_in, 16 * (a + 2))
                    if has(0) and not has(2):
                        pe.wait_ge(lo_ready["x1"], a + 1)
                    turn(x1, tp[1]).then_inc(turned["x1"], 1)
                if has(2):
                    pe.wait_ge(lo_ready["h"], c + 1)
                    pe.wait_ge(hot_ready, c + 1)
                    product(ps_3, "h", Wt["h"], first=False, last=False)
                    nc.tensor.matmul(ps_3[:, :], one_hot[:, :], tab[:, :], start=False, stop=True).then_inc(l3_done, 1)

            steps(pe, step, T + 3, 5, 1, first=-1, end=T - 1)

        @block.scalar
        def _(act):
            def high(n, t, bank, used):
                act.wait_ge(turned[n], t + 1)
                if later(t, 1):
                    act.wait_ge(used, t)
                nc.scalar.activation(hi[n][:, :, :], bank[:, :, :], ACT.Copy).then_inc(hi_ready[n], 1)

            def normalize(k, t, dst, src, ready, used):
                act.wait_ge(shift_ready[k], t + 1)
                if later(t, 1):
                    act.wait_ge(used, t)
                nc.scalar.activation(dst[:, :], src[:, :], ACT.Identity, bias=shift_n[:, k:k + 1], scale=rstd[:, k:k + 1]).then_inc(ready, 1)

            def step(s, u, has):
                a, b, c, d, f = s, s - 1, s - 2, s - 3, s - 4
                if has(1):
                    high("x2", b, tp[0], l2_done)
                if has(2):
                    high("x3", c, tp[2], l3x_done)
                    high("t", c, tp[1], l3t_done)
                if has(0):
                    act.wait_ge(u_done, a + 1)
                    if later(a, 1):
                        act.wait_ge(v_done, a)
                    nc.scalar.activation(z[:, :], ps_z[:, :], ACT.Copy).then_inc(z_hi_ready, 1)
                if has(3):
                    act.wait_ge(l3_done, d + 1)
                    if later(d, 1):
                        act.wait_ge(turned["g"], d)
                    nc.scalar.activation(g[:, :], ps_3[:, :], ACT.Silu).then_inc(g_ready, 1)
                if has(4):
                    normalize(LN3, f, f2, f2, fn_ready, o_ready)
                if has(2):
                    normalize(LN2, c, h1, h1, hn_ready, h_ready)
                if has(3):
                    high("g", d, tp[2], l4_done)
                if has(2):
                    high("s", c, tp[1], l3s_done)
                if has(2):
                    high("h", c, tp[0], l3_done)
                if has(1):
                    normalize(LN1, b, xn, x3, xn_ready, h1_ready)
                if has(-1):
                    high("x1", a + 1, tp[1], u_done)
                    if later(a, 0):
                        act.wait_ge(u_done, a + 1)
                    nc.scalar.activation(u_now[:, :, :], u_hi_lo[:, (a + 1) // TB, :, :].bitcast(F32), ACT.Copy).then_inc(u_now_ready, 1)

            steps(act, step, T + 4, 5, 1, first=-1, end=T - 1)

        @block.vector
        def _(dve):
            nc.vector.memset(half[:, :], -0.5).then_inc(half_ready, 1)
            dve.wait_ge(consts_in, 16 * 12)

            def low(n, t, bank):
                dve.wait_ge(hi_ready[n], t + 1)
                nc.vector.tensor_tensor(lo[n][:, :, :], bank[:, :, :], hi[n][:, :, :].bitcast(F32), ALU.subtract).then_inc(lo_ready[n], 1)

            def moments(k, t, src):
                if later(t, 1):
                    dve.wait_ge(mv_ready[k], t)
                nc.vector.bn_stats(stats[:, k, :], src[:, :]).then_inc(st_ready[k], 1)
                dve.wait_ge(st_ready[k], t + 1)
                if later(t, 1):
                    dve.wait_ge(shift_ready[k], t)
                dve.sem_inc(dve_passed, 1)
                nc.vector.bn_aggr(mean_var[:, k, :], stats[:, k, :]).then_inc(mv_ready[k], 1)
                dve.wait_ge(mv_ready[k], t + 1)
                if later(t, 1):
                    dve.wait_ge(rstd_ready[k], t)
                nc.vector.tensor_scalar(var_eps[:, k:k + 1], mean_var[:, k, 1:2], 1e-5, None, ALU.add).then_inc(var_ready[k], 1)

            def shifts(k, t, applied):
                dve.wait_ge(rstd_ready[k], t + 1)
                if later(t, 1):
                    dve.wait_ge(applied, t)
                nc.vector.tensor_scalar(shift_n[:, k:k + 1], mean_var[:, k, 0:1], rstd[:, k:k + 1], -1.0, ALU.mult, ALU.mult).then_inc(shift_ready[k], 1)

            def step(s, u, has):
                a, b, c, d, f = s, s - 1, s - 2, s - 3, s - 4
                if has(1):
                    low("x2", b, tp[0])
                if has(2):
                    low("x3", c, tp[2])
                    low("t", c, tp[1])
                if has(0):
                    dve.wait_ge(z_hi_ready, a + 1)
                    nc.vector.tensor_tensor(z[64:P, :], ps_z[64:P, :], z[64:P, :].bitcast(F32), ALU.subtract).then_inc(z_ready, 1)
                if has(4):
                    shifts(LN3, f, fn_ready)
                if has(2):
                    dve.wait_ge(h1b_ready, c + 1)
                    moments(LN2, c, h1)
                if has(1):
                    dve.wait_ge(l2_done, b + 1)
                    if later(b, 1):
                        dve.wait_ge(x3_ready, b)
                    nc.vector.tensor_tensor(yd[:, :], ps_2[:, :], demod2[:, b // TB, :], ALU.mult).then_inc(yd_ready, 1)
                    dve.wait_ge(yd_ready, b + 1)
                    nc.vector.tensor_tensor(yd[:, :], yd[:, :], bias2[:, :], ALU.add).then_inc(yb_ready, 1)
                    dve.wait_ge(yb_ready, b + 1)
                    nc.vector.tensor_scalar(yd[:, :], yd[:, :], 256.0, -256.0, ALU.min, ALU.max).then_inc(yc_ready, 1)
                    dve.wait_ge(yc_ready, b + 1)
                    if later(b, 1):
                        dve.wait_ge(xn_ready, b)
                        dve.wait_ge(turned["x3"], b)
                        dve.wait_ge(x3s_ready, b)
                    nc.vector.tensor_tensor(x3[:, :], yd[:, :], x2[:, b % 2, :], ALU.add).then_inc(x3_ready, 1)
                if has(2):
                    shifts(LN2, c, hn_ready)
                if has(3):
                    low("g", d, tp[2])
                if has(0):
                    dve.wait_ge(v_done, a + 1)
                    dve.wait_ge(x1b_ready, a + 1)
                    if later(a, 2):
                        dve.wait_ge(x3_ready, a - 1)
                        dve.wait_ge(xm2_ready, a - 1)
                    nc.vector.tensor_tensor(x2[:, a % 2, :], ps_1[:, :], x1b[:, :], ALU.add).then_inc(x2_ready, 1)
                if has(2):
                    low("s", c, tp[1])
                    dve.wait_ge(rows_in, 16 * (c + 1))
                    if later(c, 1):
                        dve.wait_ge(l3_done, c)
                    nc.vector.tensor_scalar(one_hot[:, :], id_rows[:, :], codes[:, 0:1], None, ALU.is_equal).then_inc(hot_ready, 1)
                if has(1):
                    dve.wait_ge(x3_ready, b + 1)
                    moments(LN1, b, x3)
                if has(2):
                    low("h", c, tp[0])
                if has(1):
                    shifts(LN1, b, xn_ready)
                if has(3):
                    dve.wait_ge(l4_done, d + 1)
                    if later(d, 1):
                        dve.wait_ge(o_ready, d)
                    nc.vector.tensor_tensor(f2[:, :], ps_4[:, :], b2[:, :], ALU.add).then_inc(f2_ready, 1)
                    dve.wait_ge(f2_ready, d + 1)
                    moments(LN3, d, f2)
                if has(-1):
                    low("x1", a + 1, tp[1])

            steps(dve, step, T + 4, 5, 1, first=-1, end=T - 1)

        @block.gpsimd
        def _(pool):
            pool.wait_ge(consts_in, 16 * 12)
            pool.wait_ge(half_ready, 1)

            def power(k, t):
                pool.wait_ge(var_ready[k], t + 1)
                if later(t, 1):
                    pool.wait_ge(shift_ready[k], t)
                nc.gpsimd.tensor_tensor(rstd[:, k:k + 1], var_eps[:, k:k + 1], half[:, :], ALU.pow).then_inc(rstd_ready[k], 1)

            def step(s, u, has):
                a, b, c, d, f = s, s - 1, s - 2, s - 3, s - 4
                if has(2):
                    pool.wait_ge(xn_ready, c + 1)
                    pool.wait_ge(path_in, 16 * (c + 1))
                    if later(c, 1):
                        pool.wait_ge(h_ready, c)
                    nc.gpsimd.tensor_tensor(h1[:, :], xn[:, :], path[:, 0:F], ALU.mult).then_inc(h1_ready, 1)
                    pool.wait_ge(h1_ready, c + 1)
                    nc.gpsimd.tensor_tensor(h1[:, :], h1[:, :], path[:, F:2 * F], ALU.add).then_inc(h1b_ready, 1)
                if has(0):
                    pool.wait_ge(x1_in, 16 * (a + 1))
                    if later(a, 1):
                        pool.wait_ge(x2_ready, a)
                    nc.gpsimd.tensor_tensor(x1b[:, :], x1[:, :], bias1[:, a // TB, :], ALU.add).then_inc(x1b_ready, 1)
                if has(2):
                    power(LN2, c)
                if has(4):
                    pool.wait_ge(fn_ready, f + 1)
                    nc.gpsimd.tensor_tensor(f2[:, :], f2[:, :], gain[:, :], ALU.mult).then_inc(fg_ready, 1)
                    pool.wait_ge(fg_ready, f + 1)
                    if later(f, 1):
                        pool.wait_ge(stored, 16 * f)
                    nc.gpsimd.tensor_tensor(o[:, :], f2[:, :], x3s[:, f % 4, :], ALU.add).then_inc(o_ready, 1)
                if has(2):
                    pool.wait_ge(hn_ready, c + 1)
                    pool.wait_ge(comp_in, 16 * (c + 1))
                    if later(c, 1):
                        pool.wait_ge(turned["h"], c)
                    nc.gpsimd.tensor_tensor(h[:, :], h1[:, :], comp[:, 0:F], ALU.mult).then_inc(h_ready, 1)
                if has(1):
                    if later(b, 1):
                        pool.wait_ge(path_in, 16 * b)
                        pool.wait_ge(comp_in, 16 * b)
                        pool.wait_ge(scal_in, 16 * b)
                    nc.gpsimd.tensor_copy(pid[:, :], ids[:, :, b]).then_inc(pid_ready, 1)
                    pool.wait_ge(pid_ready, b + 1)
                    if later(b, 1):
                        pool.wait_ge(h1b_ready, b)
                        pool.wait_ge(h_ready, b)
                        pool.wait_ge(t_ready, b)
                        pool.wait_ge(s_ready, b)
                    pool.sem_inc(pool_passed, 1)
                    for dst, table, k, landed in ((path, "path", 0, path_in), (comp, "comp", 1, comp_in), (scal, "scale", 2, scal_in)):
                        nc.gpsimd.indirect_dma_start(dst[:, :], None, I[table], bass.IndirectOffsetOnAxis(pid[:, k:k + 1], 0)).then_inc(landed, 16)
                if has(0):
                    pool.wait_ge(x2_ready, a + 1)
                    if later(a, 1):
                        pool.wait_ge(turned["x2"], a)
                    nc.gpsimd.tensor_tensor(xm2[:, :], x2[:, a % 2, :], style2[:, a // TB, :], ALU.mult).then_inc(xm2_ready, 1)
                if has(1):
                    power(LN1, b)
                    pool.wait_ge(x3_ready, b + 1)
                    if later(b, 4):
                        pool.wait_ge(o_ready, b - 3)
                    nc.gpsimd.tensor_tensor(x3s[:, b % 4, :], x3[:, :], shift[:, :], ALU.add).then_inc(x3s_ready, 1)
                    pool.wait_ge(xn_ready, b + 1)
                    pool.wait_ge(comp_in, 16 * (b + 1))
                    if later(b, 1):
                        pool.wait_ge(turned["t"], b)
                    nc.gpsimd.tensor_tensor(tt[:, :], xn[:, :], comp[:, F:2 * F], ALU.mult).then_inc(t_ready, 1)
                    pool.wait_ge(scal_in, 16 * (b + 1))
                    if later(b, 1):
                        pool.wait_ge(turned["s"], b)
                    nc.gpsimd.tensor_tensor(ss[:, :], xn[:, :], scal[:, :], ALU.mult).then_inc(s_ready, 1)
                if has(3):
                    power(LN3, d)

            steps(pool, step, T + 4, 5, 1)


def program(nc, I, out):
    rows = nc.dram_tensor("rows", (ROWS, B, F), F32, kind="Internal").ap()
    x1_dram = nc.dram_tensor("x1_dram", (B * N, F), F32, kind="Internal").ap()
    u_dram = nc.dram_tensor("u_dram", (RANK, B, F), F32, kind="Internal").ap()
    with ExitStack() as ctx:
        sb, _, _ = allocator(nc, ctx, [])
        ident = sb("ident", [P, P])
        cond = sb("cond", [P, S // P, B])
        wv = sb("wv", [P, 6])
        table_t = sb("table_t", [P, 6, C, TABLE])
        u_hi_lo = sb("u_hi_lo", [P, B, C, P], F32R)
        v_hi = sb("v_hi", [P, F], F32R)
        v_lo = sb("v_lo", [P, F], F32R)
        tab = sb("tab", [2 * LOW, F], F32R)
        with ExitStack() as second:
            sb2, _, _ = allocator(nc, second, [])
            w1 = [sb2("w1_mem", [P, S // P, F]), sb2("w1_noi", [64, 1, F]), sb2("w1_res", [32, 1, F])]
            w2 = [sb2(f"w2_{n}", [P, C, F]) for n in MLPS]
            with ExitStack() as first:
                sb1, _, _ = allocator(nc, first, [])
                W = [[sb1(f"w{n}_{part}", [P, C, F], F32R) for part in ("hi", "lo")] for n in "ko"]
                staged(nc, modulation, I, rows, W, ident, cond)
                prefetch = [(w1[0][:, :, :], I["mem_W1"].rearrange("(c p) f -> p c f", p=P)),
                            (w1[1][:, 0, :], I["noi_W1"]), (w1[2][:, 0, :], I["res_W1"])]
                prefetch += [(w2[j][:, :, :], I[f"{n}_W2"].rearrange("(c p) f -> p c f", p=P)) for j, n in enumerate(MLPS)]
                staged(nc, attention, I, rows, W, ident, cond, u_dram, prefetch, x1_dram)
            staged(nc, conditions, I, rows, ident, cond, u_dram, w1, w2, wv, table_t, u_hi_lo, v_hi, v_lo)
        Wt = {n: [sb(f"w{n}_{part}", [P, C, F], F32R) for part in ("high", "low")] for n in PARTS}
        with ExitStack() as third:
            sb3, _, _ = allocator(nc, third, [])
            raw = [sb3(f"raw{i}", [P, C, F]) for i in range(4)]
            staged(nc, weights, I, raw, wv, table_t, Wt, tab)
        staged(nc, cascade, I, rows, ident, Wt, tab, u_hi_lo, v_hi, v_lo, x1_dram, out)


def kernel(x, cond_512, itok_BxS_0_999, itok_BxS_0_4, cond_64, fside_Bx32_0, mask_BxS_ik0, **w):
    import concourse.bacc as bacc
    from concourse.bass_utils import run_bass_kernel_spmd as run

    token = np.arange(P) % 2
    sign = np.where(token, 1.0, -1.0).astype(np.float32)
    columns = np.tile(sign, F // P)
    paths, comps, scales = (np.asarray(a).reshape(T, P) for a in (itok_BxS_0_999, itok_BxS_0_4, mask_BxS_ik0))
    batch = np.repeat(np.arange(B, dtype=np.int32), TB * P).reshape(T, P)
    id_rows = np.zeros((T, 2 * LOW, P), np.int32)
    codes = np.full((2 * LOW, 1), -1.0, np.float32)
    for at in (0, LOW):
        for first, count, what in ((TABLE_BATCH, B, batch), (TABLE_COMP, 5, comps), (TABLE_SCALE, 3, scales)):
            id_rows[:, at + first:at + first + count, :] = what[:, None, :]
            codes[at + first:at + first + count, 0] = np.arange(count)
    dec = np.asarray(w["L1_cond_W_dec"])
    dec_b = np.asarray(w["L1_cond_b_dec"])
    arrays = {
        "x": np.asarray(x).reshape(B * N, F),
        "cond_t": np.asarray(cond_512).T,
        "cond64_t": np.asarray(cond_64).T,
        "fside_t": np.asarray(fside_Bx32_0).T,
        "ids": np.stack([paths, comps, scales]).transpose(2, 0, 1),
        "id_rows": id_rows,
        "aff_k_t": np.asarray(w["L0_cond_k_aff_w"]).T, "aff_k_b": w["L0_cond_k_aff_b"],
        "aff_o_t": np.asarray(w["L0_cond_o_aff_w"]).T, "aff_o_b": w["L0_cond_o_aff_b"],
        "aff_2_t": np.asarray(w["L2_cond_affine_w"]).T, "aff_2_b": w["L2_cond_affine_b"],
        "w_k_t": np.asarray(w["L0_cond_k_w"]).T, "k_b": w["L0_cond_k_b"],
        "w_o_t": np.asarray(w["L0_cond_o_w"]).T, "o_b": w["L0_cond_o_b"],
        "w_2_t": np.asarray(w["L2_cond_weight"]).T, "bias_2": w["L2_cond_bias"],
        "dec_w": dec[:, :F * RANK].reshape(S, F, RANK).transpose(2, 0, 1),
        "dec_b": dec_b[:F * RANK].reshape(F, RANK),
        "dec_last_w": dec[:, F * RANK:], "dec_last_b": dec_b[F * RANK:].reshape(RANK, 1),
        "V": w["L1_cond_V"],
        "path": np.concatenate([w["L3_cond_pw_g"], w["L3_cond_pw_b"]], axis=1),
        "comp": np.concatenate([w["L3_cond_cp_g"], w["L3_cond_tm_g"]], axis=1),
        "scale": w["L3_cond_ms_g"],
        "codes": codes,
        "ident": np.eye(P, dtype=np.float32),
        "mask_l": np.stack([np.ones(P, np.float32), sign]),
        "mask_r": np.stack([np.full(F, -BIG, np.float32), (BIG * columns).astype(np.float32)]),
    }
    for name in ("cp_b", "tm_b", "ms_b", "int_W1", "int_b1", "int_W2", "int_b2", "int_g", "int_be", "aw",
                 *(f"{m}_{v}" for m in MLPS for v in ("W1", "b1", "W2", "b2", "g", "be"))):
        arrays[name] = w[f"L3_cond_{name}"]
    arrays = {k: np.ascontiguousarray(a) for k, a in arrays.items()}
    nc = bacc.Bacc("TRN2", target_bir_lowering=False, num_devices=1)
    I = {k: nc.dram_tensor(f"in_{k}", a.shape, mybir.dt.from_np(a.dtype), kind="ExternalInput").ap() for k, a in arrays.items()}
    out = nc.dram_tensor("out", (B * N, F), F32, kind="ExternalOutput").ap()
    program(nc, I, out)
    got = run(nc, [{f"in_{k}": a for k, a in arrays.items()}], core_ids=[0]).results[0]["out"]
    return got.reshape(B, N, F)
```

```python
import numpy as np
import concourse.bass as bass
from concourse import mybir
from contextlib import ExitStack

F32 = mybir.dt.float32
F32R = mybir.dt.float32r
I32 = mybir.dt.int32
ALU = mybir.AluOpType
ACT = mybir.ActivationFunctionType
AX = mybir.AxisListType.X

B, N, F = 2, 2048, 512
P = 128
T = B * N // P
TB = N // P
C = F // P
H = 16
D = F // H
Q = P // D
PR = D // 2
S = 256
BIG = 2.0 ** 98

DEMOD_K, STYLE_O, DEMOD_O = range(3)


TABLE_BATCH, TABLE_COMP, TABLE_SCALE = 0, B, B + 5
TABLE = B + 5 + 3
LOW = 32
RANK = 30
MLPS = ("mem", "noi", "res")
BLOCKS = ("h", "t", "m", "n", "r", "s")


def allocator(nc, ctx, sems):
    def sb(name, shape, dt=F32):
        return ctx.enter_context(nc.sbuf_tensor(name, shape, dt))

    def ps(name, shape):
        return ctx.enter_context(nc.psum_tensor(name, shape, F32))

    def sem(name):
        sems.append(nc.alloc_semaphore(name=name))
        return sems[-1]

    return sb, ps, sem


def staged(nc, stage, *args):
    sems = []
    stage(nc, sems, *args)
    nc.clear_and_free_semaphores(sems)
    nc.all_engine_barrier()


def later(t, n):
    return not isinstance(t, int) or t >= n


def steps(engine, body, last, peel, by, first=0, end=T):
    for s in range(first, peel):
        body(s, s % 2, lambda o, s=s: 0 <= s - o < T)
    with engine.Fori(peel // by, end // by) as i:
        for u in range(by):
            body(i * by + u, u % 2, lambda o: True)
    for s in range(end, last):
        body(s, s % 2, lambda o, s=s: 0 <= s - o < T)


def row(vector, partitions):
    return vector.rearrange("(a f) -> a f", a=1).to_broadcast((partitions, vector.shape[0]))


def styles_turned(nc, out, aff, cond):
    for i in range(C):
        for c in range(S // P):
            mm = nc.tensor.matmul(out[:, i, :], aff[:, c, i * P:(i + 1) * P], cond[:, c, :], start=c == 0, stop=c == S // P - 1)
    return mm


def square_sums(nc, out, wsq, stsq):
    for o in range(C):
        for c in range(C):
            mm = nc.tensor.matmul(out[:, o, :], wsq[:, c, o * P:(o + 1) * P], stsq[:, c, :], start=c == 0, stop=c == C - 1)
    return mm


def diagonals(nc, diag, ident, column):
    for c in range(C):
        last = nc.vector.tensor_scalar(diag[:, c, :], ident[:, :], column[:, c:c + 1], None, ALU.mult)
    return last


def opening(nc, sems, I, W, bc, raw, ident, ones, cond, cond_bc, style_t, wv, table_t):
    NAMES = ("k", "o")
    L = len(NAMES)
    with ExitStack() as ctx:
        sb, ps, sem = allocator(nc, ctx, sems)
        aff = sb("aff", [P, L, S // P, F])
        aff_b = sb("aff_b", [P, F])
        aff_bt = sb("aff_bt", [P, L, C])
        w = sb("w", [P, L, C, F])
        wsq = sb("wsq", [P, L, C, F])
        stsq = sb("stsq", [P, L, C, B])
        vareps = sb("vareps", [P, L, C, B])
        minus_half = sb("minus_half", [P, L, C, B])
        demod_t = sb("demod_t", [P, L, C, B])
        diag = [sb(f"diag{i}", [P, C, P]) for i in range(2)]
        aw = sb("aw", [P, 6])
        aw_max = sb("aw_max", [P, 1])
        aw_low = sb("aw_low", [P, 6])
        aw_exp = sb("aw_exp", [P, 6])
        aw_sum = sb("aw_sum", [P, 1])
        aw_inv = sb("aw_inv", [P, 1])
        c64 = sb("c64", [64, B])
        c32 = sb("c32", [32, B])
        w2 = raw[0:3]
        w1 = [raw[3][:, 0:2, :], raw[3][0:64, 2:3, :], raw[3][0:32, 3:4, :]]
        vec = sb("vec", [B, 4, 3, F])
        h1 = sb("mlp_h1", [B, 3, F])
        h1_t = sb("mlp_h1_t", [P, 3, C, B])
        h2 = sb("mlp_h2", [B, 3, F])
        stats = sb("mlp_stats", [B, 3, 6])
        mean_var = sb("mlp_mean_var", [B, 3, 2])
        var_eps = sb("mlp_var_eps", [B, 3])
        rstd = sb("mlp_rstd", [B, 3])
        table = sb("table", [TABLE, 6, F])

        ps_wide = [ps(f"ps_wide{i}", [P, F]) for i in range(2)]
        ps_style = ps("ps_style", [P, L, C, B])
        ps_demod = ps("ps_demod", [P, L, C, B])
        ps_h = ps("ps_h", [B, 3, 512])
        ps_small = ps("ps_small", [P, 512])
        ps_turn = ps_small[:, 0:3 * C * B].rearrange("p (j c b) -> p j c b", j=3, c=C)
        ps_table = ps_small[:, 3 * C * B:3 * C * B + 6 * C * TABLE].rearrange("p (j c r) -> p j c r", j=6, c=C)

        cond_in = sem("cond_in")
        aff_in = [sem(f"aff_in{j}") for j in range(L)]
        aff_b_in = sem("aff_b_in")
        w_in = [sem(f"w_in{j}") for j in range(L)]
        aw_in = sem("aw_in")
        mlp1_in = sem("mlp1_in")
        vec_in = sem("vec_in")
        mlp2_in = sem("mlp2_in")
        table_in = sem("table_in")
        ident_in = sem("ident_in")
        ones_ready = sem("ones_ready")
        cond_bc_ready = sem("cond_bc_ready")
        half_ready = sem("half_ready")
        style_mm = sem("style_mm")
        style_t_ready = sem("style_t_ready")
        stsq_ready = sem("stsq_ready")
        wsq_ready = sem("wsq_ready")
        wide_mm = sem("wide_mm")
        style_bc_ready = sem("style_bc_ready")
        demod_mm = sem("demod_mm")
        vareps_ready = sem("vareps_ready")
        demod_t_ready = sem("demod_t_ready")
        diag_ready = sem("diag_ready")
        demod_bc_ready = sem("demod_bc_ready")
        w_hi_ready = sem("prep_hi_ready")
        aw_step = sem("aw_step")
        aw_exp_ready = sem("aw_exp_ready")
        wv_ready = sem("wv_ready")
        h1_mm = sem("h1_mm")
        h1_biased = sem("h1_biased")
        h1_ready = sem("mlp_h1_ready")
        h1_turned = sem("h1_turned")
        h1_t_ready = sem("h1_t_ready")
        h2_mm = sem("h2_mm")
        h2_ready = sem("h2_ready")
        stats_ready = sem("mlp_stats_ready")
        mv_ready = sem("mlp_mv_ready")
        var_ready = sem("mlp_var_ready")
        rstd_ready = sem("mlp_rstd_ready")
        ln_step = sem("ln_step")
        table_ready = sem("table_ready")
        table_turned = sem("table_turned")
        block = ctx.enter_context(nc.Block())

        @block.sync
        def _(sp):
            sp.dma_start(cond[:, :, :], I["cond_t"].rearrange("(c p) b -> p c b", p=P)).then_inc(cond_in, 16)
            for j, n in enumerate(NAMES):
                sp.dma_start(aff[:, j, :, :], I[f"aff_{n}_t"].rearrange("(c p) f -> p c f", p=P)).then_inc(aff_in[j], 16)
            sp.dma_start(aff_bt[:, :, :], I["aff_bt"]).then_inc(aff_b_in, 16)
            sp.dma_start(c64[:, :], I["cond64_t"]).then_inc(mlp1_in, 16)
            sp.dma_start(c32[:, :], I["fside_t"]).then_inc(mlp1_in, 16)
            sp.dma_start(w1[0], I["mem_W1"].rearrange("(c p) f -> p c f", p=P)).then_inc(mlp1_in, 16)
            sp.dma_start(w1[1][:, 0, :], I["noi_W1"]).then_inc(mlp1_in, 16)
            sp.dma_start(w1[2][:, 0, :], I["res_W1"]).then_inc(mlp1_in, 16)
            sp.dma_start(vec[:, :, :, :], I["mlp_vectors"].rearrange("(a i) j f -> a i j f", a=1).to_broadcast((B, 4, 3, F))).then_inc(vec_in, 16)
            sp.dma_start(aff_b[:, :], row(I["aff_o_b"], P)).then_inc(aff_b_in, 16)
            sp.dma_start(w[:, 0, :, :], I["w_k_t"].rearrange("(c p) f -> p c f", p=P)).then_inc(w_in[0], 16)
            sp.dma_start(ident[:, :], I["ident"]).then_inc(ident_in, 16)
            sp.dma_start(aw[:, :], row(I["aw"], P)).then_inc(aw_in, 16)
            for j, n in enumerate(MLPS):
                sp.dma_start(w2[j][:, :, :], I[f"{n}_W2"].rearrange("(c p) f -> p c f", p=P)).then_inc(mlp2_in, 16)
            sp.dma_start(w[:, 1, :, :], I["w_o_t"].rearrange("(c p) f -> p c f", p=P)).then_inc(w_in[1], 16)
            sp.dma_start(table[:, :, :], I["table_rows"]).then_inc(table_in, 16)

        @block.tensor
        def _(pe):
            pe.wait_ge(cond_in, 16)
            for j in range(L):
                pe.wait_ge(aff_in[j], 16)
                styles_turned(nc, ps_style[:, j, :, :], aff[:, j, :, :], cond).then_inc(style_mm, 1)
            pe.wait_ge(mlp1_in, 16 * 5)
            for c in range(S // P):
                nc.tensor.matmul(ps_h[:, 0, :], cond[:, c, :], w1[0][:, c, :], start=c == 0, stop=c == S // P - 1)
            nc.tensor.matmul(ps_h[:, 1, :], c64[:, :], w1[1][:, 0, :], start=True, stop=True)
            nc.tensor.matmul(ps_h[:, 2, :], c32[:, :], w1[2][:, 0, :], start=True, stop=True).then_inc(h1_mm, 1)
            pe.wait_ge(cond_bc_ready, 2 * B)
            for b in range(B):
                for c in range(S // P):
                    mm = nc.tensor.matmul(ps_wide[b][:, :], cond_bc[:, c, b, :], aff[:, 1, c, :], start=c == 0, stop=c == S // P - 1)
                mm.then_inc(wide_mm, 1)
            pe.wait_ge(ident_in, 16)
            pe.wait_ge(h1_ready, 1)
            for j in range(3):
                for c in range(C):
                    mm = nc.tensor.transpose(ps_turn[:, j, c, :], h1[:, j, c * P:(c + 1) * P], ident[0:B, 0:B])
            mm.then_inc(h1_turned, 1)
            pe.wait_ge(h1_t_ready, 1)
            pe.wait_ge(h1_biased, 1)
            pe.wait_ge(mlp2_in, 16 * 3)
            for j in range(3):
                for c in range(C):
                    mm = nc.tensor.matmul(ps_h[:, j, :], h1_t[:, j, c, :], w2[j][:, c, :], start=c == 0, stop=c == C - 1)
            mm.then_inc(h2_mm, 1)
            pe.wait_ge(stsq_ready, 1)
            for j in range(L):
                pe.wait_ge(wsq_ready, j + 1)
                mm = square_sums(nc, ps_demod[:, j, :, :], wsq[:, j, :, :], stsq[:, j, :, :])
            mm.then_inc(demod_mm, 1)
            pe.wait_ge(table_ready, 1)
            for j in range(6):
                for c in range(C):
                    mm = nc.tensor.transpose(ps_table[:, j, c, :], table[:, j, c * P:(c + 1) * P], ident[0:TABLE, 0:TABLE])
            mm.then_inc(table_turned, 1)
            for n in range(L * B):
                pe.wait_ge(diag_ready, n + 1)
                if n < 2:
                    pe.wait_ge(style_bc_ready, B)
                else:
                    pe.wait_ge(demod_bc_ready, n - 1)
                nc.tensor.matmul(ps_wide[n % 2][:, :], ones[:, :], diag[n % 2][:, :, :], start=True, stop=True).then_inc(wide_mm, 1)

        @block.scalar
        def _(act):
            act.wait_ge(h1_biased, 1)
            nc.scalar.activation(h1[:, :, :], h1[:, :, :], ACT.Silu).then_inc(h1_ready, 1)
            act.wait_ge(aw_step, 2)
            nc.scalar.activation(aw_exp[:, :], aw_low[:, :], ACT.Exp).then_inc(aw_exp_ready, 1)
            for j in range(L):
                act.wait_ge(w_in[j], 16)
                nc.scalar.activation(W[j][0][:, :, :], w[:, j, :, :], ACT.Copy).then_inc(w_hi_ready, 1)
            for n in range(L * B):
                j, b = divmod(n, B)
                act.wait_ge(wide_mm, B + n + 1)
                nc.scalar.activation(bc[:, DEMOD_K if j == 0 else DEMOD_O, b, :], ps_wide[n % 2][:, :], ACT.Copy).then_inc(demod_bc_ready, 1)

        @block.vector
        def _(dve):
            nc.vector.memset(ones[:, :], 1.0).then_inc(ones_ready, 1)
            nc.vector.memset(minus_half[:, :, :, :], -0.5).then_inc(half_ready, 1)
            dve.wait_ge(ones_ready, 1)
            dve.wait_ge(cond_in, 16)
            for c in range(S // P):
                for b in range(B):
                    nc.vector.tensor_scalar(cond_bc[:, c, b, :], ones[:, :], cond[:, c, b:b + 1], None, ALU.mult).then_inc(cond_bc_ready, 1)
            dve.wait_ge(style_mm, L)
            dve.wait_ge(aff_b_in, 16 * 2)
            nc.vector.tensor_tensor(style_t[:, :, :, :], ps_style[:, :, :, :], aff_bt[:, :, :].unsqueeze(3).to_broadcast((P, L, C, B)),
                                    ALU.add).then_inc(style_t_ready, 1)
            dve.wait_ge(style_t_ready, 1)
            nc.vector.tensor_tensor(stsq[:, :, :, :], style_t[:, :, :, :], style_t[:, :, :, :], ALU.mult).then_inc(stsq_ready, 1)
            dve.wait_ge(h1_mm, 1)
            dve.wait_ge(vec_in, 16)
            nc.vector.tensor_tensor(h1[:, :, :], ps_h[:, :, :], vec[:, 0, :, :], ALU.add).then_inc(h1_biased, 1)
            dve.wait_ge(aff_b_in, 16 * 2)
            for b in range(B):
                dve.wait_ge(wide_mm, b + 1)
                nc.vector.tensor_tensor(bc[:, STYLE_O, b, :], ps_wide[b][:, :], aff_b[:, :], ALU.add).then_inc(style_bc_ready, 1)
                if b == 0:
                    dve.wait_ge(aw_in, 16)
                    nc.vector.reduce_max(aw_max[:, :], aw[:, :], axis=AX).then_inc(aw_step, 1)
                    dve.wait_ge(aw_step, 1)
                    nc.vector.tensor_scalar(aw_low[:, :], aw[:, :], aw_max[:, 0:1], None, ALU.subtract).then_inc(aw_step, 1)
            dve.wait_ge(h1_turned, 1)
            nc.vector.tensor_copy(h1_t[:, :, :, :], ps_turn).then_inc(h1_t_ready, 1)
            dve.wait_ge(aw_exp_ready, 1)
            nc.vector.reduce_sum(aw_sum[:, :], aw_exp[:, :], axis=AX).then_inc(aw_step, 1)
            dve.wait_ge(aw_step, 3)
            nc.vector.reciprocal(aw_inv[:, :], aw_sum[:, :]).then_inc(aw_step, 1)
            dve.wait_ge(aw_step, 4)
            nc.vector.tensor_scalar(wv[:, :], aw_exp[:, :], aw_inv[:, 0:1], None, ALU.mult).then_inc(wv_ready, 1)
            dve.wait_ge(w_hi_ready, 1)
            nc.vector.tensor_tensor(W[0][1][:, :, :], w[:, 0, :, :], W[0][0][:, :, :].bitcast(F32), ALU.subtract)
            dve.wait_ge(h2_mm, 1)
            nc.vector.tensor_tensor(h2[:, :, :], ps_h[:, :, :], vec[:, 1, :, :], ALU.add).then_inc(h2_ready, 1)
            dve.wait_ge(h2_ready, 1)
            for j in range(3):
                nc.vector.bn_stats(stats[:, j, :], h2[:, j, :]).then_inc(stats_ready, 1)
            dve.wait_ge(stats_ready, 3)
            for j in range(3):
                nc.vector.bn_aggr(mean_var[:, j, :], stats[:, j, :]).then_inc(mv_ready, 1)
            dve.wait_ge(mv_ready, 3)
            nc.vector.tensor_scalar(var_eps[:, :], mean_var[:, :, 1], 1e-5, None, ALU.add).then_inc(var_ready, 1)
            dve.wait_ge(rstd_ready, 1)
            for j in range(3):
                nc.vector.tensor_scalar(h1[:, j, :], h2[:, j, :], mean_var[:, j, 0:1], rstd[:, j:j + 1],
                                        ALU.subtract, ALU.mult).then_inc(ln_step, 1)
            dve.wait_ge(ln_step, 3)
            nc.vector.tensor_tensor(h2[:, :, :], h1[:, :, :], vec[:, 2, :, :], ALU.mult).then_inc(ln_step, 1)
            dve.wait_ge(demod_mm, 1)
            nc.vector.tensor_scalar(vareps[:, :, :, :], ps_demod[:, :, :, :], 1e-8, None, ALU.add).then_inc(vareps_ready, 1)
            dve.wait_ge(ln_step, 4)
            dve.wait_ge(table_in, 16)
            nc.vector.tensor_tensor(table[0:B, 2:5, :], h2[:, :, :], vec[:, 3, :, :], ALU.add).then_inc(table_ready, 1)
            dve.wait_ge(w_hi_ready, 2)
            nc.vector.tensor_tensor(W[1][1][:, :, :], w[:, 1, :, :], W[1][0][:, :, :].bitcast(F32), ALU.subtract)
            dve.wait_ge(demod_t_ready, 1)
            for n in range(L * B):
                j, b = divmod(n, B)
                if n >= 2:
                    dve.wait_ge(wide_mm, B + n - 1)
                last = diagonals(nc, diag[n % 2], ident, demod_t[:, j, :, b])
                last.then_inc(diag_ready, 1)
            dve.wait_ge(table_turned, 1)
            dve.wait_ge(wv_ready, 1)
            for j in range(6):
                nc.vector.tensor_scalar(table_t[:, j, :, :], ps_table[:, j, :, :], wv[:, j:j + 1], None, ALU.mult)

        @block.gpsimd
        def _(pool):
            for j in range(L):
                pool.wait_ge(w_in[j], 16)
                nc.gpsimd.tensor_tensor(wsq[:, j, :, :], w[:, j, :, :], w[:, j, :, :], ALU.mult).then_inc(wsq_ready, 1)
            pool.wait_ge(half_ready, 1)
            pool.wait_ge(var_ready, 1)
            nc.gpsimd.tensor_tensor(rstd[:, :], var_eps[:, :], minus_half[0:B, 0, 0:3, 0], ALU.pow).then_inc(rstd_ready, 1)
            pool.wait_ge(vareps_ready, 1)
            nc.gpsimd.tensor_tensor(demod_t[:, :, :, :], vareps[:, :, :, :], minus_half[:, :, :, :], ALU.pow).then_inc(demod_t_ready, 1)


def attention(nc, sems, I, W, style_t, bc, ident, cond, u_dram, prefetch, x1_dram):
    (wk_hi, wk_lo), (wo_hi, wo_lo) = W[0], W[1]
    x_dram = I["x"].rearrange("(t p) f -> t p f", p=P)
    x1_tiles = x1_dram.rearrange("(t p) f -> t p f", p=P)
    U_AT = 4
    PEEL, LAST = 8, T + 5
    with ExitStack() as ctx:
        sb, ps, sem = allocator(nc, ctx, sems)
        bias_k = sb("bias_k", [P, F])
        bias_o = sb("bias_o", [P, F])
        mask_l = sb("mask_l", [2, P])
        mask_r = sb("mask_r", [2, F])
        mask_lr = sb("mask_lr", [2, P], F32R)
        mask_rr = sb("mask_rr", [2, F], F32R)
        x_in = sb("x_in", [P, C, P])
        xm = sb("xm", [P, C, P])
        xh = sb("xh", [P, C, P], F32R)
        xl = sb("xl", [P, C, P], F32R)
        kb = sb("kb", [P, F])
        kt = [sb(f"kt{i}", [P, PR, H * 2]) for i in range(2)]
        k_diag = [sb(f"k_diag{i}", [P, PR, Q, H * 2]) for i in range(2)]
        v = [sb(f"v{i}", [P, PR // Q, P]) for i in range(2)]
        mx = sb("mx", [P, PR])
        low = sb("low", [P, PR, D])
        e = sb("e", [P, PR, D])
        total = sb("total", [P, PR])
        rinv = sb("rinv", [P, PR])
        at = sb("at", [P, PR, D])
        at_diag = sb("at_diag", [P, PR, Q, D])
        om = sb("om", [P, F])
        oh = sb("oh", [P, C, P], F32R)
        ol = sb("ol", [P, C, P], F32R)
        od = sb("od", [P, F])
        xb = sb("xb", [P, F])
        x1 = [sb(f"x1o{i}", [P, F]) for i in range(2)]
        dec = sb("dec", [P, S // P, F])
        dec_hi = sb("dec_hi", [P, S // P, F], F32R)
        dec_lo = sb("dec_lo", [P, S // P, F], F32R)
        cond_parts = sb("cond_parts", [P, S // P, 2 * B], F32R)
        u_row = sb("u_row", [2 * B, F])

        ps_k = ps("ps_k", [P, F])
        ps_s = ps("ps_s", [P, PR, D])
        ps_vt = ps("ps_vt", [P, PR // Q, P])
        ps_v = ps("ps_v", [P, PR, H, 2])
        ps_t = ps("ps_t", [P, C, P])
        ps_o = ps("ps_o", [P, F])
        ps_u = ps("ps_u", [2 * B, F])

        consts_in = sem("consts_in")
        bias_in = sem("attn_bias_in")
        mask_ready = sem("mask_ready")
        diag_zero = sem("diag_zero")
        x_landed = sem("x_landed")
        xm_ready = sem("xm_ready")
        xh_ready = sem("xh_ready")
        xl_ready = sem("xl_ready")
        k_done = sem("k_done")
        kd_ready = sem("kd_ready")
        kb_ready = sem("kb_ready")
        kt_ready = sem("kt_ready")
        k_diag_ready = sem("k_diag_ready")
        v_ready = sem("v_ready")
        v_turned = sem("v_turned")
        at_diag_ready = sem("at_diag_ready")
        scores_done = sem("scores_done")
        mx_ready = sem("mx_ready")
        low_ready = sem("low_ready")
        e_ready = sem("e_ready")
        total_ready = sem("total_ready")
        rinv_ready = sem("rinv_ready")
        a_ready = sem("a_ready")
        at_ready = sem("at_ready")
        mixed = sem("mixed")
        ot_ready = sem("ot_ready")
        om_ready = sem("om_ready")
        o_turned = sem("o_turned")
        oh_ready = sem("oh_ready")
        ol_ready = sem("ol_ready")
        o_done = sem("o_done")
        od_ready = sem("od_ready")
        res_landed = sem("res_landed")
        xb_ready = sem("xb_ready")
        x1_ready = sem("x1_ready")
        x1_stored = [sem(f"x1_stored{i}") for i in range(2)]
        ahead = sem("ahead")
        dec_in = sem("dec_in")
        dec_hi_ready = sem("dec_hi_ready")
        dec_lo_ready = sem("dec_lo_ready")
        dec_used = sem("dec_used")
        cond_hi_ready = sem("cond_hi_ready")
        cond_lo_ready = sem("cond_lo_ready")
        u_row_ready = sem("u_row_ready")
        u_stored = sem("u_stored")
        block = ctx.enter_context(nc.Block())

        def has_u(s):
            return not isinstance(s, int) or 0 <= s - U_AT < RANK

        @block.sync
        def _(sp):
            sp.dma_start(x_in[:, :, :], I["x_turned"][0]).then_inc(x_landed, 16)
            sp.dma_start(mask_l[:, :], I["mask_l"]).then_inc(consts_in, 16)
            sp.dma_start(mask_r[:, :], I["mask_r"]).then_inc(consts_in, 16)
            sp.dma_start(bias_k[:, :], row(I["k_b"], P)).then_inc(bias_in, 16)
            sp.dma_start(bias_o[:, :], row(I["o_b"], P)).then_inc(bias_in, 16)

            def step(s, u_, has):
                if has_u(s - 2):
                    k = s - 2 - U_AT
                    sp.wait_ge(u_row_ready, k + 1)
                    sp.dma_start(u_dram[k], u_row[:, :]).then_inc(u_stored, 16)
                if has(6):
                    t, p = s - 6, u_
                    sp.wait_ge(x1_ready, t + 1)
                    sp.dma_start(x1_tiles[t], x1[p][:, :]).then_inc(x1_stored[p], 16)
                if has(-1):
                    t = s + 1
                    if later(t, 1):
                        sp.wait_ge(xm_ready, t)
                    sp.dma_start(x_in[:, :, :], I["x_turned"][t]).then_inc(x_landed, 16)
                if has_u(s + 1):
                    k = s + 1 - U_AT
                    if later(k, 1):
                        sp.wait_ge(dec_lo_ready, k)
                    sp.dma_start(dec[:, :, :], I["dec_w"][k].rearrange("(c p) f -> p c f", p=P)).then_inc(dec_in, 16)
                if has(4):
                    t = s - 4
                    if later(t, 1):
                        sp.wait_ge(x1_ready, t)
                    sp.dma_start(xb[:, :], x_dram[t]).then_inc(res_landed, 16)
                if isinstance(s, int) and s >= 4 and prefetch:
                    dst, src = prefetch.pop(0)
                    sp.dma_start(dst, src).then_inc(ahead, 16)

            count = len(prefetch)
            steps(sp, step, T + 6, PEEL, 2, end=T - 2)
            assert not prefetch
            sp.wait_ge(ahead, 16 * count)
            sp.wait_ge(u_stored, 16 * RANK)
            for p in range(2):
                sp.wait_ge(x1_stored[p], 16 * (T // 2))

        @block.tensor
        def _(pe):
            pe.wait_ge(mask_ready, 2)
            pe.wait_ge(diag_zero, 3)
            pe.wait_ge(cond_lo_ready, 1)

            def project(out_ps, hi, lo, w_hi, w_lo):
                terms = [(x, w, c) for c in range(C) for x, w in ((hi, w_hi), (hi, w_lo), (lo, w_hi))]
                for n, (x, w, c) in enumerate(terms):
                    mm = nc.tensor.matmul(out_ps[:, :], x[:, c, :], w[:, c, :], start=n == 0, stop=n == len(terms) - 1)
                return mm

            def step(s, u_, has):
                if has(2):
                    t, p = s - 2, u_
                    pe.wait_ge(kt_ready, t + 1)
                    if later(t, 1):
                        pe.wait_ge(v_ready, t)
                    for m in range(PR // Q):
                        mm = nc.tensor.transpose(ps_vt[:, m, :], kt[p][:, Q * m:Q * m + Q, :].rearrange("p g h -> p (g h)"), ident[:, :])
                    mm.then_inc(v_turned, 1)
                    pe.wait_ge(k_diag_ready, t + 1)
                    if later(t, 1):
                        pe.wait_ge(low_ready, t)
                    nc.tensor.matmul(ps_s[:, :, :], mask_lr[:, :], mask_rr[:, :], start=True, stop=False, skip_group_check=True)
                    for j in range(PR):
                        m, g = divmod(j, Q)
                        mm = nc.tensor.matmul(ps_s[D * g:D * g + D, Q * m:Q * m + Q, :], kt[p][:, j, :], k_diag[p][:, j, :, :],
                                              start=False, stop=True, skip_group_check=True)
                    mm.then_inc(scores_done, 1)
                if has(0):
                    pe.wait_ge(xl_ready, s + 1)
                    if later(s, 1):
                        pe.wait_ge(kd_ready, s)
                    project(ps_k, xh, xl, wk_hi, wk_lo).then_inc(k_done, 1)
                if has(5):
                    t = s - 5
                    pe.wait_ge(ol_ready, t + 1)
                    if later(t, 1):
                        pe.wait_ge(od_ready, t)
                    project(ps_o, oh, ol, wo_hi, wo_lo).then_inc(o_done, 1)
                if has_u(s):
                    pe.wait_ge(dec_lo_ready, s - U_AT + 1)
                    if later(s, U_AT + 1):
                        pe.wait_ge(u_row_ready, s - U_AT)
                    terms = [(part, c) for part in (dec_hi, dec_lo) for c in range(S // P)]
                    for n, (part, c) in enumerate(terms):
                        mm = nc.tensor.matmul(ps_u[:, :], cond_parts[:, c, :], part[:, c, :], start=n == 0, stop=n == len(terms) - 1)
                    mm.then_inc(dec_used, 1)
                if has(3):
                    t, p = s - 3, (u_ + 1) % 2
                    pe.wait_ge(at_diag_ready, t + 1)
                    pe.wait_ge(v_ready, t + 1)
                    if later(t, 1):
                        pe.wait_ge(ot_ready, t)
                    for j in range(PR):
                        m, q = divmod(j, Q)
                        mm = nc.tensor.matmul(ps_v[D * q:D * q + D, Q * m:Q * m + Q, :, :], v[p][:, m, D * q:D * q + D], at_diag[:, j, :, :],
                                              start=True, stop=True)
                    mm.then_inc(mixed, 1)
                if has(4):
                    t = s - 4
                    pe.wait_ge(om_ready, t + 1)
                    if later(t, 1):
                        pe.wait_ge(ol_ready, t)
                    for c in range(C):
                        mm = nc.tensor.transpose(ps_t[:, c, :], om[:, c * P:(c + 1) * P], ident[:, :])
                    mm.then_inc(o_turned, 1)

            steps(pe, step, LAST, PEEL, 2)

        @block.scalar
        def _(act):
            act.wait_ge(diag_zero, 3)

            def diagonal(dst, src):
                for q in range(Q):
                    g = slice(D * q, D * q + D)
                    last = nc.scalar.activation(dst[g, :, q, :], src[g, :, :], ACT.Copy)
                return last

            def step(s, u_, has):
                if has_u(s):
                    k = s - U_AT
                    act.wait_ge(dec_in, 16 * (k + 1))
                    if later(k, 1):
                        act.wait_ge(dec_used, k)
                    nc.scalar.activation(dec_hi[:, :, :], dec[:, :, :], ACT.Copy).then_inc(dec_hi_ready, 1)
                if has(3):
                    t = s - 3
                    act.wait_ge(at_ready, t + 1)
                    if later(t, 1):
                        act.wait_ge(mixed, t)
                    diagonal(at_diag, at).then_inc(at_diag_ready, 1)
                if has_u(s - 1):
                    k = s - 1 - U_AT
                    act.wait_ge(dec_used, k + 1)
                    if later(k, 1):
                        act.wait_ge(u_stored, 16 * k)
                    nc.scalar.activation(u_row[:, :], ps_u[:, :], ACT.Copy).then_inc(u_row_ready, 1)
                if has(2):
                    t, p = s - 2, u_
                    act.wait_ge(v_turned, t + 1)
                    if later(t, 2):
                        act.wait_ge(mixed, t - 1)
                    nc.scalar.activation(v[p][:, :, :], ps_vt[:, :, :], ACT.Copy).then_inc(v_ready, 1)
                if has(1):
                    t, p = s - 1, (u_ + 1) % 2
                    act.wait_ge(kt_ready, t + 1)
                    if later(t, 2):
                        act.wait_ge(scores_done, t - 1)
                    diagonal(k_diag[p], kt[p]).then_inc(k_diag_ready, 1)
                if has(-1):
                    t = s + 1
                    act.wait_ge(xm_ready, t + 1)
                    if later(t, 1):
                        act.wait_ge(k_done, t)
                    nc.scalar.activation(xh[:, :, :], xm[:, :, :], ACT.Copy).then_inc(xh_ready, 1)
                if has(2):
                    t = s - 2
                    act.wait_ge(low_ready, t + 1)
                    if later(t, 1):
                        act.wait_ge(at_ready, t)
                    nc.scalar.activation(e[:, :, :], low[:, :, :], ACT.Exp, scale=float(D) ** -0.5).then_inc(e_ready, 1)
                if has(4):
                    t = s - 4
                    act.wait_ge(o_turned, t + 1)
                    if later(t, 1):
                        act.wait_ge(o_done, t)
                    nc.scalar.activation(oh[:, :, :], ps_t[:, :, :], ACT.Copy).then_inc(oh_ready, 1)

            steps(act, step, LAST, PEEL, 2, first=-1, end=T - 2)

        @block.vector
        def _(dve):
            for d in k_diag:
                nc.vector.memset(d[:, :, :, :], 0.0).then_inc(diag_zero, 1)
            nc.vector.tensor_copy(cond_parts[:, :, 0:B], cond[:, :, :]).then_inc(cond_hi_ready, 1)
            dve.wait_ge(cond_hi_ready, 1)
            nc.vector.tensor_tensor(cond_parts[:, :, B:2 * B], cond[:, :, :], cond_parts[:, :, 0:B].bitcast(F32),
                                    ALU.subtract).then_inc(cond_lo_ready, 1)
            dve.wait_ge(consts_in, 16 * 2)
            nc.vector.tensor_copy(mask_lr[:, :], mask_l[:, :]).then_inc(mask_ready, 1)
            nc.vector.tensor_copy(mask_rr[:, :], mask_r[:, :]).then_inc(mask_ready, 1)

            def step(s, u_, has):
                if has(4):
                    t = s - 4
                    dve.wait_ge(mixed, t + 1)
                    if later(t, 1):
                        dve.wait_ge(o_turned, t)
                    nc.vector.transpose(om[:, :].rearrange("p (h a c) -> p h a c", h=H, c=2),
                                        ps_v[:, :, :, :].rearrange("p a h c -> p h a c")).then_inc(ot_ready, 1)
                if has_u(s):
                    k = s - U_AT
                    dve.wait_ge(dec_hi_ready, k + 1)
                    if later(k, 1):
                        dve.wait_ge(dec_used, k)
                    nc.vector.tensor_tensor(dec_lo[:, :, :], dec[:, :, :], dec_hi[:, :, :].bitcast(F32), ALU.subtract).then_inc(dec_lo_ready, 1)
                if has(2):
                    t = s - 2
                    dve.wait_ge(scores_done, t + 1)
                    if later(t, 1):
                        dve.wait_ge(low_ready, t)
                    nc.vector.reduce_max(mx[:, :], ps_s[:, :, :], axis=AX).then_inc(mx_ready, 1)
                    dve.wait_ge(mx_ready, t + 1)
                    if later(t, 1):
                        dve.wait_ge(e_ready, t)
                    nc.vector.tensor_tensor(low[:, :, :], ps_s[:, :, :], mx[:, :].unsqueeze(2).to_broadcast((P, PR, D)),
                                            ALU.subtract).then_inc(low_ready, 1)
                if has(0):
                    dve.wait_ge(k_done, s + 1)
                    if later(s, 1):
                        dve.wait_ge(kt_ready, s)
                    nc.vector.tensor_tensor(kb[:, :], ps_k[:, :], bc[:, DEMOD_K, s // TB, :], ALU.mult).then_inc(kd_ready, 1)
                if has(5):
                    t = s - 5
                    dve.wait_ge(o_done, t + 1)
                    if later(t, 1):
                        dve.wait_ge(x1_ready, t)
                    nc.vector.tensor_tensor(od[:, :], ps_o[:, :], bc[:, DEMOD_O, t // TB, :], ALU.mult).then_inc(od_ready, 1)
                if has(-1):
                    t = s + 1
                    dve.wait_ge(xh_ready, t + 1)
                    nc.vector.tensor_tensor(xl[:, :, :], xm[:, :, :], xh[:, :, :].bitcast(F32), ALU.subtract).then_inc(xl_ready, 1)
                if has(2):
                    t = s - 2
                    dve.wait_ge(e_ready, t + 1)
                    if later(t, 1):
                        dve.wait_ge(rinv_ready, t)
                    nc.vector.reduce_sum(total[:, :], e[:, :, :], axis=AX).then_inc(total_ready, 1)
                    dve.wait_ge(total_ready, t + 1)
                    if later(t, 1):
                        dve.wait_ge(a_ready, t)
                    nc.vector.reciprocal(rinv[:, :], total[:, :]).then_inc(rinv_ready, 1)
                if has(4):
                    t = s - 4
                    dve.wait_ge(oh_ready, t + 1)
                    nc.vector.tensor_tensor(ol[:, :, :], ps_t[:, :, :], oh[:, :, :].bitcast(F32), ALU.subtract).then_inc(ol_ready, 1)
                if has(2):
                    t = s - 2
                    dve.wait_ge(a_ready, t + 1)
                    if later(t, 1):
                        dve.wait_ge(at_diag_ready, t)
                    nc.vector.transpose(at[:, :, :], e[:, :, :]).then_inc(at_ready, 1)
                if has(0):
                    dve.wait_ge(kb_ready, s + 1)
                    if later(s, 2):
                        dve.wait_ge(scores_done, s - 1)
                    nc.vector.transpose(kt[u_][:, :, :].rearrange("p a (h c) -> p h a c", c=2),
                                        kb[:, :].rearrange("p (h a c) -> p h a c", h=H, c=2)).then_inc(kt_ready, 1)

            steps(dve, step, LAST, PEEL, 2, first=-1, end=T - 2)

        @block.gpsimd
        def _(pool):
            nc.gpsimd.memset(at_diag[:, :, :, :], 0.0).then_inc(diag_zero, 1)

            def step(s, u_, has):
                if has(4):
                    t = s - 4
                    pool.wait_ge(ot_ready, t + 1)
                    nc.gpsimd.tensor_tensor(om[:, :], om[:, :], bc[:, STYLE_O, t // TB, :], ALU.mult).then_inc(om_ready, 1)
                if has(5):
                    t, p = s - 5, (u_ + 1) % 2
                    pool.wait_ge(res_landed, 16 * (t + 1))
                    nc.gpsimd.tensor_tensor(xb[:, :], xb[:, :], bias_o[:, :], ALU.add).then_inc(xb_ready, 1)
                if has(-1):
                    t = s + 1
                    pool.wait_ge(x_landed, 16 * (t + 1))
                    if later(t, 1):
                        pool.wait_ge(xl_ready, t)
                    nc.gpsimd.tensor_tensor(xm[:, :, :], x_in[:, :, :], style_t[:, 0, :, t // TB].unsqueeze(2).to_broadcast((P, C, P)), ALU.mult).then_inc(xm_ready, 1)
                if has(5):
                    t, p = s - 5, (u_ + 1) % 2
                    pool.wait_ge(od_ready, t + 1)
                    pool.wait_ge(xb_ready, t + 1)
                    if later(t, 2):
                        pool.wait_ge(x1_stored[p], 8 * (t - p))
                    nc.gpsimd.tensor_tensor(x1[p][:, :], od[:, :], xb[:, :], ALU.add).then_inc(x1_ready, 1)
                if has(2):
                    t = s - 2
                    pool.wait_ge(rinv_ready, t + 1)
                    nc.gpsimd.tensor_tensor(e[:, :, :], e[:, :, :], rinv[:, :].unsqueeze(2).to_broadcast((P, PR, D)),
                                            ALU.mult).then_inc(a_ready, 1)
                if has(0):
                    if isinstance(s, int) and s == 0:
                        pool.wait_ge(bias_in, 16 * 2)
                    pool.wait_ge(kd_ready, s + 1)
                    nc.gpsimd.tensor_tensor(kb[:, :], kb[:, :], bias_k[:, :], ALU.add).then_inc(kb_ready, 1)

            steps(pool, step, LAST, PEEL, 2, first=-1, end=T - 2)


LOADS = ("w_2_t", "int_W2", 2, 3, 4, 0, 1, 5)


def raw_source(I, item):
    weight = I[item] if isinstance(item, str) else I["int_W1"][item * F:(item + 1) * F, :]
    return weight.rearrange("(c p) f -> p c f", p=P)


PARTS = ("2", "out", "h", "t", "x", "s")


def interlude(nc, sems, I, raw, ident, ones, cond, cond_bc, u_dram, wv, table_t, Wt, tab, u_parts, v_parts, tables):
    raw_n = len(raw)
    style2, demod2, bias1 = tables["style2"], tables["demod2"], tables["bias1"]
    with ExitStack() as ctx:
        sb, ps, sem = allocator(nc, ctx, sems)
        acc = [sb(f"acc{i}", [P, C, F]) for i in range(2)]
        tab_bias = sb("tab_bias", [TABLE, F])
        tab_sum = sb("tab_sum", [TABLE, F])
        aff = sb("aff2", [P, S // P, F])
        aff_b = sb("aff2_b", [P, F])
        aff_bt = sb("aff2_bt", [P, C])
        wsq = sb("wsq2", [P, C, F])
        style_t = sb("style2_t", [P, C, B])
        stsq = sb("stsq2", [P, C, B])
        vareps = sb("vareps2", [P, C, B])
        minus_half = sb("minus_half2", [P, C, B])
        demod_t = sb("demod2_t", [P, C, B])
        diag = [sb(f"diag2_{b}", [P, C, P]) for b in range(B)]
        u_rows = sb("u_rows", [RANK * 2 * B, F])
        dec_b = sb("dec_b", [P, C, RANK])
        u = sb("u", [P, C, RANK, B])
        v = sb("v_rows", [P, F])
        last_w = sb("last_w", [P, S // P, RANK])
        last_b = sb("last_b", [RANK, 1])
        last_u = sb("last_u", [RANK, B])
        last_bc = sb("last_bc", [RANK, B, P])

        ps_tab = ps("ps_tab", [TABLE, F])
        ps_wide = [ps(f"ps_wide2_{i}", [P, F]) for i in range(2)]
        ps_style = ps("ps_style2", [P, C, B])
        ps_demod = ps("ps_demod2", [P, C, B])
        ps_u = ps("ps_u_t", [P, C, RANK, 2, B])
        ps_last = ps("ps_last", [RANK, B])

        raw_in = [sem(f"raw_in{i}") for i in range(raw_n)]
        hi_ready = sem("w_hi_ready")
        item_done = sem("item_done")
        tab_used = sem("tab_used")
        bias_zero = sem("bias_zero")
        bias_in = sem("bias_in")
        tab_sum_ready = sem("tab_sum_ready")
        tab_hi_ready = sem("tab_hi_ready")
        tab_zero = sem("tab_zero")
        u_in = sem("u_in")
        last_in = sem("last_in")
        aff_in = sem("aff2_in")
        aff_b_in = sem("aff2_b_in")
        v_in = sem("v_in")
        v_zero = sem("v_zero")
        u_zero = sem("u_zero")
        half_ready = sem("half2_ready")
        tables_in = sem("tables_in")
        last_mm = sem("last_mm")
        last_ready = sem("last_ready")
        last_bc_ready = sem("last_bc_ready")
        u_turned = sem("u_turned")
        u_ready = sem("u_ready")
        u_hi_ready = sem("u_hi_ready")
        v_hi_ready = sem("v_hi_ready")
        style_mm = sem("style2_mm")
        style_t_ready = sem("style2_t_ready")
        stsq_ready = sem("stsq2_ready")
        wsq_ready = sem("wsq2_ready")
        demod_mm = sem("demod2_mm")
        vareps_ready = sem("vareps2_ready")
        demod_t_ready = sem("demod2_t_ready")
        diag_ready = sem("diag2_ready")
        wide_mm = sem("wide2_mm")
        wide_read = sem("wide2_read")
        block = ctx.enter_context(nc.Block())
        dest = {"w_2_t": "2", "int_W2": "out", 0: "h", 1: "t", 5: "s"}

        def wait_raw(engine, i):
            if i >= raw_n:
                engine.wait_ge(raw_in[i % raw_n], 16 * (i // raw_n))

        @block.sync
        def _(sp):
            sp.dma_start(aff[:, :, :], I["aff_2_t"].rearrange("(c p) f -> p c f", p=P)).then_inc(aff_in, 16)
            sp.dma_start(aff_bt[:, :], I["aff_2_bt"]).then_inc(aff_in, 16)
            sp.dma_start(aff_b[:, :], row(I["aff_2_b"], P)).then_inc(aff_b_in, 16)
            sp.dma_start(last_w[:, :, :], I["dec_last_w"].rearrange("(c p) k -> p c k", p=P)).then_inc(last_in, 16)
            sp.dma_start(last_b[:, :], I["dec_last_b"]).then_inc(last_in, 16)
            sp.dma_start(u_rows[:, :], u_dram.rearrange("k b f -> (k b) f")).then_inc(u_in, 16)
            sp.dma_start(dec_b[:, :, :], I["dec_b"].rearrange("(c p) k -> p c k", p=P)).then_inc(u_in, 16)
            sp.wait_ge(v_zero, 1)
            for q in range(Q):
                sp.dma_start(v[32 * q:32 * q + RANK, :], I["V"]).then_inc(v_in, 16)
            sp.wait_ge(bias_zero, 1)
            sp.dma_start(tab_bias[0:B, :], row(I["int_b1"], B)).then_inc(bias_in, 16)
            for i, item in enumerate(LOADS):
                if i >= raw_n:
                    sp.wait_ge(item_done, i - raw_n + 1)
                    if i == raw_n:
                        sp.wait_ge(wsq_ready, 1)
                    if i - raw_n >= 2:
                        sp.wait_ge(tab_used, i - raw_n - 1)
                    sp.dma_start(raw[i % raw_n][:, :, :], raw_source(I, item)).then_inc(raw_in[i % raw_n], 16)
            for name, src in (("bias2", "bias_2"), ("b2", "int_b2"), ("gain", "int_g"), ("shift", "int_be")):
                sp.dma_start(tables[name][:, :], row(I[src], P)).then_inc(tables_in, 16)
            sp.dma_start(tables["codes"][:, :], I["codes"]).then_inc(tables_in, 16)
            sp.dma_start(tables["ids"][:, :, :], I["ids"]).then_inc(tables_in, 16)
            sp.wait_ge(tables_in, 16 * 6)

        @block.tensor
        def _(pe):
            def table_product(n):
                i = n + 2
                wait_raw(pe, i)
                for c in range(C):
                    mm = nc.tensor.matmul(ps_tab[:, :], table_t[:, LOADS[i], c, :], raw[i % raw_n][:, c, :],
                                          start=n == 0 and c == 0, stop=n == 5 and c == C - 1)
                mm.then_inc(tab_used, 1)

            table_product(0)
            table_product(1)
            pe.wait_ge(aff_in, 16 * 2)
            styles_turned(nc, ps_style, aff, cond).then_inc(style_mm, 1)
            for b in range(B):
                for c in range(S // P):
                    mm = nc.tensor.matmul(ps_wide[b][:, :], cond_bc[:, c, b, :], aff[:, c, :], start=c == 0, stop=c == S // P - 1)
                mm.then_inc(wide_mm, 1)
            pe.wait_ge(last_in, 16 * 2)
            for c in range(S // P):
                mm = nc.tensor.matmul(ps_last[:, :], last_w[:, c, :], cond[:, c, :], start=c == 0, stop=c == S // P - 1)
            mm.then_inc(last_mm, 1)
            pe.wait_ge(u_in, 16 * 2)
            for c in range(C):
                mm = nc.tensor.transpose(ps_u[:, c, :, :, :].rearrange("p k h b -> p (k h b)"), u_rows[:, c * P:(c + 1) * P],
                                         ident[0:RANK * 2 * B, 0:RANK * 2 * B])
            mm.then_inc(u_turned, 1)
            table_product(2)
            pe.wait_ge(stsq_ready, 1)
            pe.wait_ge(wsq_ready, 1)
            square_sums(nc, ps_demod, wsq, stsq).then_inc(demod_mm, 1)
            pe.wait_ge(last_bc_ready, B)
            pe.wait_ge(v_in, 16 * Q)
            for b in range(B):
                pe.wait_ge(wide_read, b + 1)
                nc.tensor.matmul(ps_wide[b][:, :], last_bc[:, b, :], v[0:RANK, :], start=True, stop=True).then_inc(wide_mm, 1)
            table_product(3)
            table_product(4)
            for b in range(B):
                pe.wait_ge(diag_ready, b + 1)
                pe.wait_ge(wide_read, B + b + 1)
                nc.tensor.matmul(ps_wide[b][:, :], ones[:, :], diag[b][:, :, :], start=True, stop=True).then_inc(wide_mm, 1)
            table_product(5)

        @block.scalar
        def _(act):
            for i, item in enumerate(LOADS):
                if item in dest:
                    wait_raw(act, i)
                    scale = wv[:, item:item + 1] if isinstance(item, int) else 1.0
                    nc.scalar.activation(Wt[dest[item]][0][:, :, :], raw[i % raw_n][:, :, :], ACT.Copy, scale=scale).then_inc(hi_ready, 1)
                elif item == 4:
                    act.wait_ge(item_done, i + 1)
                    nc.scalar.activation(Wt["x"][0][:, :, :], acc[0][:, :, :], ACT.Copy).then_inc(hi_ready, 1)
                if i == 1:
                    for b in range(B):
                        act.wait_ge(wide_mm, B + b + 1)
                        nc.scalar.activation(bias1[:, b, :], ps_wide[b][:, :], ACT.Copy).then_inc(wide_read, 1)
            for b in range(B):
                act.wait_ge(wide_mm, 2 * B + b + 1)
                nc.scalar.activation(demod2[:, b, :], ps_wide[b][:, :], ACT.Copy).then_inc(wide_read, 1)

        @block.vector
        def _(dve):
            def split(i):
                item, r = LOADS[i], raw[i % raw_n]
                wait_raw(dve, i)
                if item in dest:
                    w_hi, w_lo = Wt[dest[item]]
                    dve.wait_ge(hi_ready, i + 1 if i < 2 else i - 1)
                    if isinstance(item, str):
                        nc.vector.tensor_tensor(w_lo[:, :, :], r[:, :, :], w_hi[:, :, :].bitcast(F32), ALU.subtract).then_inc(item_done, 1)
                    else:
                        nc.vector.scalar_tensor_tensor(w_lo[:, :, :].rearrange("p c f -> p (c f)"), r[:, :, :].rearrange("p c f -> p (c f)"), wv[:, item:item + 1],
                                                       w_hi[:, :, :].bitcast(F32).rearrange("p c f -> p (c f)"), ALU.mult, ALU.subtract).then_inc(item_done, 1)
                elif item == 2:
                    nc.vector.tensor_scalar(acc[0][:, :, :], r[:, :, :], wv[:, 2:3], None, ALU.mult).then_inc(item_done, 1)
                elif item == 3:
                    dve.wait_ge(item_done, i)
                    nc.vector.scalar_tensor_tensor(acc[1][:, :, :], r[:, :, :], wv[:, 3:4], acc[0][:, :, :], ALU.mult, ALU.add).then_inc(item_done, 1)
                else:
                    dve.wait_ge(item_done, i)
                    nc.vector.scalar_tensor_tensor(acc[0][:, :, :], r[:, :, :], wv[:, 4:5], acc[1][:, :, :], ALU.mult, ALU.add).then_inc(item_done, 1)
                    dve.wait_ge(hi_ready, i - 1)
                    nc.vector.tensor_tensor(Wt["x"][1][:, :, :], acc[0][:, :, :], Wt["x"][0][:, :, :].bitcast(F32), ALU.subtract)

            nc.vector.memset(v[:, :], 0.0).then_inc(v_zero, 1)
            nc.vector.memset(tab_bias[:, :], 0.0).then_inc(bias_zero, 1)
            nc.vector.memset(minus_half[:, :, :], -0.5).then_inc(half_ready, 1)
            nc.vector.memset(u_parts[:, :, :, :].bitcast(F32), 0.0).then_inc(u_zero, 1)
            nc.vector.memset(tab[:, :].bitcast(F32), 0.0).then_inc(tab_zero, 1)
            split(0)
            split(1)
            gain = 1.0 / float(np.sqrt(S))
            dve.wait_ge(style_mm, 1)
            nc.vector.scalar_tensor_tensor(style_t[:, :, :], ps_style[:, :, :], gain, aff_bt[:, :].unsqueeze(2).to_broadcast((P, C, B)),
                                           ALU.mult, ALU.add).then_inc(style_t_ready, 1)
            dve.wait_ge(style_t_ready, 1)
            nc.vector.tensor_tensor(stsq[:, :, :], style_t[:, :, :], style_t[:, :, :], ALU.mult).then_inc(stsq_ready, 1)
            dve.wait_ge(aff_b_in, 16)
            for b in range(B):
                dve.wait_ge(wide_mm, b + 1)
                nc.vector.scalar_tensor_tensor(style2[:, b, :], ps_wide[b][:, :], gain, aff_b[:, :], ALU.mult, ALU.add).then_inc(wide_read, 1)
            split(2)
            dve.wait_ge(last_mm, 1)
            nc.vector.tensor_scalar(last_u[:, :], ps_last[:, :], last_b[:, 0:1], None, ALU.add).then_inc(last_ready, 1)
            dve.wait_ge(last_ready, 1)
            for b in range(B):
                nc.vector.tensor_scalar(last_bc[:, b, :], ones[0:RANK, :], last_u[:, b:b + 1], None, ALU.mult).then_inc(last_bc_ready, 1)
            dve.wait_ge(u_turned, 1)
            nc.vector.tensor_tensor(u[:, :, :, :], ps_u[:, :, :, 0, :], dec_b[:, :, :].unsqueeze(3).to_broadcast((P, C, RANK, B)),
                                    ALU.add).then_inc(u_ready, 1)
            dve.wait_ge(u_ready, 1)
            nc.vector.tensor_tensor(u[:, :, :, :], ps_u[:, :, :, 1, :], u[:, :, :, :], ALU.add).then_inc(u_ready, 1)
            dve.wait_ge(u_zero, 1)
            dve.wait_ge(u_ready, 2)
            for b in range(B):
                for k in (0, 32, 64):
                    nc.vector.tensor_copy(u_parts[:, b, :, k:k + RANK], u[:, :, :, b]).then_inc(u_hi_ready, 1)
            dve.wait_ge(u_hi_ready, 3 * B)
            for b in range(B):
                nc.vector.tensor_tensor(u_parts[:, b, :, 96:96 + RANK], u[:, :, :, b], u_parts[:, b, :, 0:RANK].bitcast(F32), ALU.subtract)
            split(3)
            dve.wait_ge(demod_mm, 1)
            nc.vector.tensor_scalar(vareps[:, :, :], ps_demod[:, :, :], 1e-8, None, ALU.add).then_inc(vareps_ready, 1)
            dve.wait_ge(v_in, 16 * Q)
            nc.vector.tensor_copy(v_parts[:, :], v[:, :]).then_inc(v_hi_ready, 1)
            dve.wait_ge(v_hi_ready, 1)
            nc.vector.tensor_tensor(v_parts[64:96, :], v[64:96, :], v_parts[64:96, :].bitcast(F32), ALU.subtract)
            split(4)
            dve.wait_ge(demod_t_ready, 1)
            for b in range(B):
                diagonals(nc, diag[b], ident, demod_t[:, :, b]).then_inc(diag_ready, 1)
            for i in range(5, len(LOADS)):
                split(i)
            dve.wait_ge(tab_used, 6)
            dve.wait_ge(bias_in, 16)
            nc.vector.tensor_tensor(tab_sum[:, :], ps_tab[:, :], tab_bias[:, :], ALU.add).then_inc(tab_sum_ready, 1)
            dve.wait_ge(tab_sum_ready, 1)
            dve.wait_ge(tab_zero, 1)
            nc.vector.tensor_copy(tab[0:TABLE, :], tab_sum[:, :]).then_inc(tab_hi_ready, 1)
            dve.wait_ge(tab_hi_ready, 1)
            nc.vector.tensor_tensor(tab[LOW:LOW + TABLE, :], tab_sum[:, :], tab[0:TABLE, :].bitcast(F32), ALU.subtract)

        @block.gpsimd
        def _(pool):
            nc.gpsimd.tensor_tensor(wsq[:, :, :], raw[0][:, :, :], raw[0][:, :, :], ALU.mult).then_inc(wsq_ready, 1)
            pool.wait_ge(half_ready, 1)
            pool.wait_ge(vareps_ready, 1)
            nc.gpsimd.tensor_tensor(demod_t[:, :, :], vareps[:, :, :], minus_half[:, :, :], ALU.pow).then_inc(demod_t_ready, 1)


def cascade(nc, sems, I, room, ident, Wt, tab, u_parts, v_parts, tables, x1_dram, out):
    x1_tiles = x1_dram.rearrange("(t p) f -> t p f", p=P)
    out_tiles = out.rearrange("(t p) f -> t p f", p=P)
    with ExitStack() as ctx:
        sb, ps, sem = allocator(nc, ctx, sems)
        style2, demod2, bias1, bias2, b2, gain, shift, codes, ids = (
            tables[n] for n in ("style2", "demod2", "bias1", "bias2", "b2", "gain", "shift", "codes", "ids"))
        half = sb("half", [P, 1])
        x1 = sb("x1", [P, F])
        x1b = sb("x1b", [P, F])
        u_now = sb("u_now", [P, C, P], F32R)
        z = sb("z", [P, P], F32R)
        x2 = sb("x2", [P, 2, F])
        xm2 = sb("xm2", [P, F])
        yd = sb("yd", [P, F])
        x3 = sb("x3", [P, F])
        x3s = room[0]
        stats = sb("stats", [P, 3, 6])
        mean_var = sb("mean_var", [P, 3, 2])
        var_eps = sb("var_eps", [P, 3])
        rstd = sb("rstd", [P, 3])
        shift_n = sb("shift_n", [P, 3])
        xn = sb("xn", [P, F])
        tt, ss, h1, h = (room[2][:, i, :] for i in range(4))
        g, f2, o = (room[3][:, i, :] for i in range(3))
        names = ("x1", "x2", "x3", "t", "s", "h", "g")
        own = ("x1", "x2", "x3", "t", "g")
        hi = {n: sb(f"{n}_hi", [P, C, P], F32R) for n in own}
        lo = {n: sb(f"{n}_lo", [P, C, P], F32R) for n in own}
        for n, m in (("s", "x1"), ("h", "x2")):
            hi[n], lo[n] = hi[m], lo[m]
        pid = sb("pid", [P, 3], I32)
        path = room[1][:, 0:2, :].rearrange("p a f -> p (a f)")
        comp = room[1][:, 2:4, :].rearrange("p a f -> p (a f)")
        scal = sb("scal", [P, F])
        id_rows = sb("id_rows", [2 * LOW, P], I32)
        one_hot = sb("one_hot", [2 * LOW, P], F32R)

        tp = [ps(f"tp{i}", [P, C, P]) for i in range(3)]
        ps_z = ps("ps_z", [P, P])
        ps_1 = ps("ps_1", [P, F])
        ps_2 = ps("ps_2", [P, F])
        ps_3 = ps("ps_3", [P, F])
        ps_4 = ps("ps_4", [P, F])

        half_ready = sem("half_ready2")
        x1_in = sem("x1_in")
        rows_in = sem("id_rows_in")
        pid_ready = sem("pid_ready")
        path_in = sem("path_in")
        comp_in = sem("comp_in")
        scal_in = sem("scal_in")
        u_now_ready = sem("u_now_ready")
        x1b_ready = sem("x1b_ready")
        turned = {n: sem(f"{n}_turned") for n in names}
        hi_ready = {n: sem(f"{n}_hi_ready") for n in names}
        lo_ready = {n: sem(f"{n}_lo_ready") for n in names}
        u_done = sem("u_done")
        z_hi_ready = sem("z_hi_ready")
        z_ready = sem("z_ready")
        v_done = sem("v_done")
        x2_ready = sem("x2_ready")
        xm2_ready = sem("xm2_ready")
        l2_done = sem("l2_done")
        yd_ready = sem("yd_ready")
        yb_ready = sem("yb_ready")
        yc_ready = sem("yc_ready")
        x3_ready = sem("x3_ready")
        x3s_ready = sem("x3s_ready")
        st_ready = [sem(f"st_ready{i}") for i in range(3)]
        mv_ready = [sem(f"mv_ready{i}") for i in range(3)]
        var_ready = [sem(f"var_ready{i}") for i in range(3)]
        rstd_ready = [sem(f"rstd_ready{i}") for i in range(3)]
        shift_ready = [sem(f"shift_ready{i}") for i in range(3)]
        xn_ready = sem("xn_ready")
        t_ready = sem("t_ready")
        s_ready = sem("s_ready")
        h1_ready = sem("h1_ready")
        h1b_ready = sem("h1b_ready")
        hn_ready = sem("hn_ready")
        h_ready = sem("h_ready")
        hot_ready = sem("hot_ready")
        l3x_done = sem("l3x_done")
        l3t_done = sem("l3t_done")
        l3s_done = sem("l3s_done")
        l3_done = sem("l3_done")
        g_ready = sem("act_g_ready")
        l4_done = sem("l4_done")
        f2_ready = sem("f2_ready")
        fn_ready = sem("fn_ready")
        fg_ready = sem("fg_ready")
        o_ready = sem("o_ready")
        stored = sem("stored")
        dve_passed = sem("dve_passed")
        pool_passed = sem("pool_passed")
        block = ctx.enter_context(nc.Block())
        LN1, LN2, LN3 = range(3)

        @block.sync
        def _(sp):
            def step(s, u, has):
                if has(5):
                    t = s - 5
                    sp.wait_ge(o_ready, t + 1)
                    sp.dma_start(out_tiles[t], o[:, :]).then_inc(stored, 16)
                if has(-1):
                    n = s + 1
                    if later(n, 1):
                        sp.wait_ge(turned["x1"], n)
                        sp.wait_ge(x1b_ready, n)
                    sp.dma_start(x1[:, :], x1_tiles[n]).then_inc(x1_in, 16)
                if has(2):
                    t = s - 2
                    if later(t, 1):
                        sp.wait_ge(hot_ready, t)
                    sp.dma_start(id_rows[:, :], I["id_rows"][t]).then_inc(rows_in, 16)

            steps(sp, step, T + 5, 5, 1, first=-1, end=T - 1)
            sp.wait_ge(stored, 16 * T)

        def product(out_ps, a, w, first=True, last=True):
            terms = [(x, y, c) for c in range(C) for x, y in ((hi[a], w[0]), (hi[a], w[1]), (lo[a], w[0]))]
            for n, (x, y, c) in enumerate(terms):
                mm = nc.tensor.matmul(out_ps[:, :], x[:, c, :], y[:, c, :], start=first and n == 0, stop=last and n == len(terms) - 1)
            return mm

        def turn(src, bank):
            for c in range(C):
                mm = nc.tensor.transpose(bank[:, c, :], src[:, c * P:(c + 1) * P], ident[:, :])
            return mm

        @block.tensor
        def _(pe):
            def step(s, u, has):
                a, b, c, d = s, s - 1, s - 2, s - 3
                if has(1):
                    pe.wait_ge(xm2_ready, b + 1)
                    if later(b, 2):
                        pe.wait_ge(lo_ready["h"], b - 1)
                    turn(xm2, tp[0]).then_inc(turned["x2"], 1)
                if has(2):
                    pe.wait_ge(x3_ready, c + 1)
                    if later(c, 2):
                        pe.wait_ge(lo_ready["g"], c - 1)
                    turn(x3, tp[2]).then_inc(turned["x3"], 1)
                    pe.wait_ge(t_ready, c + 1)
                    if has(0):
                        pe.wait_ge(lo_ready["x1"], a + 1)
                    turn(tt, tp[1]).then_inc(turned["t"], 1)
                if has(0):
                    pe.wait_ge(lo_ready["x1"], a + 1)
                    pe.wait_ge(u_now_ready, a + 1)
                    if later(a, 1):
                        pe.wait_ge(z_ready, a)
                    for n, x in enumerate((hi["x1"], lo["x1"])):
                        for k in range(C):
                            mm = nc.tensor.matmul(ps_z[:, :], u_now[:, k, :], x[:, k, :], start=n == 0 and k == 0, stop=n == 1 and k == C - 1)
                    mm.then_inc(u_done, 1)
                if has(1):
                    pe.wait_ge(lo_ready["x2"], b + 1)
                    if later(b, 1):
                        pe.wait_ge(yd_ready, b)
                    product(ps_2, "x2", Wt["2"]).then_inc(l2_done, 1)
                if has(3):
                    pe.wait_ge(g_ready, d + 1)
                    if has(2):
                        pe.wait_ge(lo_ready["x3"], c + 1)
                    turn(g, tp[2]).then_inc(turned["g"], 1)
                if has(0):
                    pe.wait_ge(z_ready, a + 1)
                    if later(a, 1):
                        pe.wait_ge(x2_ready, a)
                    nc.tensor.matmul(ps_1[:, :], z[:, :], v_parts[:, :], start=True, stop=True).then_inc(v_done, 1)
                if has(2):
                    pe.wait_ge(lo_ready["x3"], c + 1)
                    if later(c, 1):
                        pe.wait_ge(g_ready, c)
                    product(ps_3, "x3", Wt["x"], last=False).then_inc(l3x_done, 1)
                    pe.wait_ge(s_ready, c + 1)
                    pe.wait_ge(lo_ready["t"], c + 1)
                    turn(ss, tp[1]).then_inc(turned["s"], 1)
                    product(ps_3, "t", Wt["t"], first=False, last=False).then_inc(l3t_done, 1)
                if has(3):
                    pe.wait_ge(lo_ready["g"], d + 1)
                    if later(d, 1):
                        pe.wait_ge(f2_ready, d)
                    product(ps_4, "g", Wt["out"]).then_inc(l4_done, 1)
                if has(2):
                    pe.wait_ge(h_ready, c + 1)
                    if has(1):
                        pe.wait_ge(lo_ready["x2"], b + 1)
                    turn(h, tp[0]).then_inc(turned["h"], 1)
                    pe.wait_ge(lo_ready["s"], c + 1)
                    product(ps_3, "s", Wt["s"], first=False, last=False).then_inc(l3s_done, 1)
                if has(-1):
                    pe.wait_ge(x1_in, 16 * (a + 2))
                    if has(0) and not has(2):
                        pe.wait_ge(lo_ready["x1"], a + 1)
                    turn(x1, tp[1]).then_inc(turned["x1"], 1)
                if has(2):
                    pe.wait_ge(lo_ready["h"], c + 1)
                    pe.wait_ge(hot_ready, c + 1)
                    product(ps_3, "h", Wt["h"], first=False, last=False)
                    nc.tensor.matmul(ps_3[:, :], one_hot[:, :], tab[:, :], start=False, stop=True).then_inc(l3_done, 1)

            steps(pe, step, T + 3, 5, 1, first=-1, end=T - 1)

        @block.scalar
        def _(act):
            def high(n, t, bank, used):
                act.wait_ge(turned[n], t + 1)
                if later(t, 1):
                    act.wait_ge(used, t)
                nc.scalar.activation(hi[n][:, :, :], bank[:, :, :], ACT.Copy).then_inc(hi_ready[n], 1)

            def normalize(k, t, dst, src, ready, used):
                act.wait_ge(shift_ready[k], t + 1)
                if later(t, 1):
                    act.wait_ge(used, t)
                nc.scalar.activation(dst[:, :], src[:, :], ACT.Identity, bias=shift_n[:, k:k + 1], scale=rstd[:, k:k + 1]).then_inc(ready, 1)

            def step(s, u, has):
                a, b, c, d, f = s, s - 1, s - 2, s - 3, s - 4
                if has(1):
                    high("x2", b, tp[0], l2_done)
                if has(2):
                    high("x3", c, tp[2], l3x_done)
                    high("t", c, tp[1], l3t_done)
                if has(0):
                    act.wait_ge(u_done, a + 1)
                    if later(a, 1):
                        act.wait_ge(v_done, a)
                    nc.scalar.activation(z[:, :], ps_z[:, :], ACT.Copy).then_inc(z_hi_ready, 1)
                if has(3):
                    act.wait_ge(l3_done, d + 1)
                    if later(d, 1):
                        act.wait_ge(turned["g"], d)
                    nc.scalar.activation(g[:, :], ps_3[:, :], ACT.Silu).then_inc(g_ready, 1)
                if has(4):
                    normalize(LN3, f, f2, f2, fn_ready, o_ready)
                if has(2):
                    normalize(LN2, c, h1, h1, hn_ready, h_ready)
                if has(3):
                    high("g", d, tp[2], l4_done)
                if has(2):
                    high("s", c, tp[1], l3s_done)
                if has(2):
                    high("h", c, tp[0], l3_done)
                if has(1):
                    normalize(LN1, b, xn, x3, xn_ready, h1_ready)
                if has(-1):
                    high("x1", a + 1, tp[1], u_done)
                    if later(a, 0):
                        act.wait_ge(u_done, a + 1)
                    nc.scalar.activation(u_now[:, :, :], u_parts[:, (a + 1) // TB, :, :].bitcast(F32), ACT.Copy).then_inc(u_now_ready, 1)

            steps(act, step, T + 4, 5, 1, first=-1, end=T - 1)

        @block.vector
        def _(dve):
            nc.vector.memset(half[:, :], -0.5).then_inc(half_ready, 1)

            def low(n, t, bank):
                dve.wait_ge(hi_ready[n], t + 1)
                nc.vector.tensor_tensor(lo[n][:, :, :], bank[:, :, :], hi[n][:, :, :].bitcast(F32), ALU.subtract).then_inc(lo_ready[n], 1)

            def moments(k, t, src):
                if later(t, 1):
                    dve.wait_ge(mv_ready[k], t)
                nc.vector.bn_stats(stats[:, k, :], src[:, :]).then_inc(st_ready[k], 1)
                dve.wait_ge(st_ready[k], t + 1)
                if later(t, 1):
                    dve.wait_ge(shift_ready[k], t)
                dve.sem_inc(dve_passed, 1)
                nc.vector.bn_aggr(mean_var[:, k, :], stats[:, k, :]).then_inc(mv_ready[k], 1)
                dve.wait_ge(mv_ready[k], t + 1)
                if later(t, 1):
                    dve.wait_ge(rstd_ready[k], t)
                nc.vector.tensor_scalar(var_eps[:, k:k + 1], mean_var[:, k, 1:2], 1e-5, None, ALU.add).then_inc(var_ready[k], 1)

            def shifts(k, t, applied):
                dve.wait_ge(rstd_ready[k], t + 1)
                if later(t, 1):
                    dve.wait_ge(applied, t)
                nc.vector.tensor_scalar(shift_n[:, k:k + 1], mean_var[:, k, 0:1], rstd[:, k:k + 1], -1.0, ALU.mult, ALU.mult).then_inc(shift_ready[k], 1)

            def step(s, u, has):
                a, b, c, d, f = s, s - 1, s - 2, s - 3, s - 4
                if has(1):
                    low("x2", b, tp[0])
                if has(2):
                    low("x3", c, tp[2])
                    low("t", c, tp[1])
                if has(0):
                    dve.wait_ge(z_hi_ready, a + 1)
                    nc.vector.tensor_tensor(z[32:64, :], ps_z[32:64, :], z[32:64, :].bitcast(F32), ALU.subtract).then_inc(z_ready, 1)
                if has(4):
                    shifts(LN3, f, fn_ready)
                if has(2):
                    dve.wait_ge(h1b_ready, c + 1)
                    moments(LN2, c, h1)
                if has(1):
                    dve.wait_ge(l2_done, b + 1)
                    if later(b, 1):
                        dve.wait_ge(x3_ready, b)
                    nc.vector.tensor_tensor(yd[:, :], ps_2[:, :], demod2[:, b // TB, :], ALU.mult).then_inc(yd_ready, 1)
                    dve.wait_ge(yd_ready, b + 1)
                    nc.vector.tensor_tensor(yd[:, :], yd[:, :], bias2[:, :], ALU.add).then_inc(yb_ready, 1)
                    dve.wait_ge(yb_ready, b + 1)
                    nc.vector.tensor_scalar(yd[:, :], yd[:, :], 256.0, -256.0, ALU.min, ALU.max).then_inc(yc_ready, 1)
                    dve.wait_ge(yc_ready, b + 1)
                    if later(b, 1):
                        dve.wait_ge(xn_ready, b)
                        dve.wait_ge(turned["x3"], b)
                        dve.wait_ge(x3s_ready, b)
                    nc.vector.tensor_tensor(x3[:, :], yd[:, :], x2[:, b % 2, :], ALU.add).then_inc(x3_ready, 1)
                if has(2):
                    shifts(LN2, c, hn_ready)
                if has(3):
                    low("g", d, tp[2])
                if has(0):
                    dve.wait_ge(v_done, a + 1)
                    dve.wait_ge(x1b_ready, a + 1)
                    if later(a, 2):
                        dve.wait_ge(x3_ready, a - 1)
                        dve.wait_ge(xm2_ready, a - 1)
                    nc.vector.tensor_tensor(x2[:, a % 2, :], ps_1[:, :], x1b[:, :], ALU.add).then_inc(x2_ready, 1)
                if has(2):
                    low("s", c, tp[1])
                    dve.wait_ge(rows_in, 16 * (c + 1))
                    if later(c, 1):
                        dve.wait_ge(l3_done, c)
                    nc.vector.tensor_scalar(one_hot[:, :], id_rows[:, :], codes[:, 0:1], None, ALU.is_equal).then_inc(hot_ready, 1)
                if has(1):
                    dve.wait_ge(x3_ready, b + 1)
                    moments(LN1, b, x3)
                if has(2):
                    low("h", c, tp[0])
                if has(1):
                    shifts(LN1, b, xn_ready)
                if has(3):
                    dve.wait_ge(l4_done, d + 1)
                    if later(d, 1):
                        dve.wait_ge(o_ready, d)
                    nc.vector.tensor_tensor(f2[:, :], ps_4[:, :], b2[:, :], ALU.add).then_inc(f2_ready, 1)
                    dve.wait_ge(f2_ready, d + 1)
                    moments(LN3, d, f2)
                if has(-1):
                    low("x1", a + 1, tp[1])

            steps(dve, step, T + 4, 5, 1, first=-1, end=T - 1)

        @block.gpsimd
        def _(pool):
            pool.wait_ge(half_ready, 1)

            def power(k, t):
                pool.wait_ge(var_ready[k], t + 1)
                if later(t, 1):
                    pool.wait_ge(shift_ready[k], t)
                nc.gpsimd.tensor_tensor(rstd[:, k:k + 1], var_eps[:, k:k + 1], half[:, :], ALU.pow).then_inc(rstd_ready[k], 1)

            def step(s, u, has):
                a, b, c, d, f = s, s - 1, s - 2, s - 3, s - 4
                if has(2):
                    pool.wait_ge(xn_ready, c + 1)
                    pool.wait_ge(path_in, 16 * (c + 1))
                    if later(c, 1):
                        pool.wait_ge(h_ready, c)
                    nc.gpsimd.tensor_tensor(h1[:, :], xn[:, :], path[:, 0:F], ALU.mult).then_inc(h1_ready, 1)
                    pool.wait_ge(h1_ready, c + 1)
                    nc.gpsimd.tensor_tensor(h1[:, :], h1[:, :], path[:, F:2 * F], ALU.add).then_inc(h1b_ready, 1)
                if has(0):
                    pool.wait_ge(x1_in, 16 * (a + 1))
                    if later(a, 1):
                        pool.wait_ge(x2_ready, a)
                    nc.gpsimd.tensor_tensor(x1b[:, :], x1[:, :], bias1[:, a // TB, :], ALU.add).then_inc(x1b_ready, 1)
                if has(2):
                    power(LN2, c)
                if has(4):
                    pool.wait_ge(fn_ready, f + 1)
                    nc.gpsimd.tensor_tensor(f2[:, :], f2[:, :], gain[:, :], ALU.mult).then_inc(fg_ready, 1)
                    pool.wait_ge(fg_ready, f + 1)
                    if later(f, 1):
                        pool.wait_ge(stored, 16 * f)
                    nc.gpsimd.tensor_tensor(o[:, :], f2[:, :], x3s[:, f % 4, :], ALU.add).then_inc(o_ready, 1)
                if has(2):
                    pool.wait_ge(hn_ready, c + 1)
                    pool.wait_ge(comp_in, 16 * (c + 1))
                    if later(c, 1):
                        pool.wait_ge(turned["h"], c)
                    nc.gpsimd.tensor_tensor(h[:, :], h1[:, :], comp[:, 0:F], ALU.mult).then_inc(h_ready, 1)
                if has(1):
                    if later(b, 1):
                        pool.wait_ge(path_in, 16 * b)
                        pool.wait_ge(comp_in, 16 * b)
                        pool.wait_ge(scal_in, 16 * b)
                    nc.gpsimd.tensor_copy(pid[:, :], ids[:, :, b]).then_inc(pid_ready, 1)
                    pool.wait_ge(pid_ready, b + 1)
                    if later(b, 1):
                        pool.wait_ge(h1b_ready, b)
                        pool.wait_ge(h_ready, b)
                        pool.wait_ge(t_ready, b)
                        pool.wait_ge(s_ready, b)
                    pool.sem_inc(pool_passed, 1)
                    for dst, table, k, landed in ((path, "path", 0, path_in), (comp, "comp", 1, comp_in), (scal, "scale", 2, scal_in)):
                        nc.gpsimd.indirect_dma_start(dst[:, :], None, I[table], bass.IndirectOffsetOnAxis(pid[:, k:k + 1], 0)).then_inc(landed, 16)
                if has(0):
                    pool.wait_ge(x2_ready, a + 1)
                    if later(a, 1):
                        pool.wait_ge(turned["x2"], a)
                    nc.gpsimd.tensor_tensor(xm2[:, :], x2[:, a % 2, :], style2[:, a // TB, :], ALU.mult).then_inc(xm2_ready, 1)
                if has(1):
                    power(LN1, b)
                    pool.wait_ge(x3_ready, b + 1)
                    if later(b, 4):
                        pool.wait_ge(o_ready, b - 3)
                    nc.gpsimd.tensor_tensor(x3s[:, b % 4, :], x3[:, :], shift[:, :], ALU.add).then_inc(x3s_ready, 1)
                    pool.wait_ge(xn_ready, b + 1)
                    pool.wait_ge(comp_in, 16 * (b + 1))
                    if later(b, 1):
                        pool.wait_ge(turned["t"], b)
                    nc.gpsimd.tensor_tensor(tt[:, :], xn[:, :], comp[:, F:2 * F], ALU.mult).then_inc(t_ready, 1)
                    pool.wait_ge(scal_in, 16 * (b + 1))
                    if later(b, 1):
                        pool.wait_ge(turned["s"], b)
                    nc.gpsimd.tensor_tensor(ss[:, :], xn[:, :], scal[:, :], ALU.mult).then_inc(s_ready, 1)
                if has(3):
                    power(LN3, d)

            steps(pool, step, T + 4, 5, 1)


def program(nc, I, out):
    x1_dram = nc.dram_tensor("x1_dram", (B * N, F), F32, kind="Internal").ap()
    u_dram = nc.dram_tensor("u_dram", (RANK, 2 * B, F), F32, kind="Internal").ap()
    with ExitStack() as ctx:
        sb, _, _ = allocator(nc, ctx, [])
        ident = sb("ident", [P, P])
        ones = sb("ones", [P, P])
        cond = sb("cond", [P, S // P, B])
        cond_bc = sb("cond_bc", [P, S // P, B, P])
        style_t = sb("style_t", [P, 2, C, B])
        wv = sb("wv", [P, 6])
        table_t = sb("table_t", [P, 6, C, TABLE])
        raw = [sb(f"raw{i}", [P, C, F]) for i in range(4)]
        with ExitStack() as first:
            sb1, _, _ = allocator(nc, first, [])
            W = [[sb1(f"w{n}_{part}", [P, C, F], F32R) for part in ("hi", "lo")] for n in "ko"]
            bc = sb1("bc", [P, 3, B, F])
            staged(nc, opening, I, W, bc, raw, ident, ones, cond, cond_bc, style_t, wv, table_t)
            prefetch = [(raw[i][:, :, :], raw_source(I, item)) for i, item in enumerate(LOADS[:len(raw)])]
            staged(nc, attention, I, W, style_t, bc, ident, cond, u_dram, prefetch, x1_dram)
        Wt = {n: [sb(f"w{n}_{part}", [P, C, F], F32R) for part in ("high", "low")] for n in PARTS}
        u_parts = sb("u_parts", [P, B, C, P], F32R)
        v_parts = sb("v_parts", [P, F], F32R)
        tab = sb("tab", [2 * LOW, F], F32R)
        tables = {n: sb(n, [P, B, F]) for n in ("style2", "demod2", "bias1")}
        tables |= {n: sb(n, [P, F]) for n in ("bias2", "b2", "gain", "shift")}
        tables |= {"codes": sb("codes", [2 * LOW, 1]), "ids": sb("ids", [P, 3, T], I32)}
        staged(nc, interlude, I, raw, ident, ones, cond, cond_bc, u_dram, wv, table_t, Wt, tab, u_parts, v_parts, tables)
        staged(nc, cascade, I, raw, ident, Wt, tab, u_parts, v_parts, tables, x1_dram, out)


def kernel(x, cond_512, itok_BxS_0_999, itok_BxS_0_4, cond_64, fside_Bx32_0, mask_BxS_ik0, **w):
    import concourse.bacc as bacc
    from concourse.bass_utils import run_bass_kernel_spmd as run

    token = np.arange(P) % 2
    sign = np.where(token, 1.0, -1.0).astype(np.float32)
    columns = np.tile(sign, F // P)
    paths, comps, scales = (np.asarray(a).reshape(T, P) for a in (itok_BxS_0_999, itok_BxS_0_4, mask_BxS_ik0))
    batch = np.repeat(np.arange(B, dtype=np.int32), TB * P).reshape(T, P)
    id_rows = np.zeros((T, 2 * LOW, P), np.int32)
    codes = np.full((2 * LOW, 1), -1.0, np.float32)
    for at in (0, LOW):
        for first, count, what in ((TABLE_BATCH, B, batch), (TABLE_COMP, 5, comps), (TABLE_SCALE, 3, scales)):
            id_rows[:, at + first:at + first + count, :] = what[:, None, :]
            codes[at + first:at + first + count, 0] = np.arange(count)
    table_rows = np.zeros((TABLE, 6, F), np.float32)
    for at, block, name in ((TABLE_COMP, 0, "cp_b"), (TABLE_COMP, 1, "tm_b"), (TABLE_SCALE, 5, "ms_b")):
        rows = np.asarray(w[f"L3_cond_{name}"])
        table_rows[at:at + len(rows), block] = rows
    dec = np.asarray(w["L1_cond_W_dec"])
    dec_b = np.asarray(w["L1_cond_b_dec"])
    arrays = {
        "x": np.asarray(x).reshape(B * N, F),
        "x_turned": np.asarray(x).reshape(T, P, C, P).transpose(0, 3, 2, 1),
        "cond_t": np.asarray(cond_512).T,
        "cond64_t": np.asarray(cond_64).T,
        "fside_t": np.asarray(fside_Bx32_0).T,
        "ids": np.stack([paths, comps, scales]).transpose(2, 0, 1),
        "id_rows": id_rows,
        "aff_k_t": np.asarray(w["L0_cond_k_aff_w"]).T, 
        "aff_o_t": np.asarray(w["L0_cond_o_aff_w"]).T, 
        "aff_2_t": np.asarray(w["L2_cond_affine_w"]).T, "aff_2_b": w["L2_cond_affine_b"],
        "aff_bt": np.stack([np.asarray(w[f"L0_cond_{n}_aff_b"]).reshape(C, P).T for n in "ko"], axis=1),
        "aff_o_b": w["L0_cond_o_aff_b"],
        "mlp_vectors": np.stack([[w[f"L3_cond_{m}_{v}"] for m in MLPS] for v in ("b1", "b2", "g", "be")]),
        "table_rows": table_rows,
        "aff_2_bt": np.asarray(w["L2_cond_affine_b"]).reshape(C, P).T,
        "w_k_t": np.asarray(w["L0_cond_k_w"]).T, "k_b": w["L0_cond_k_b"],
        "w_o_t": np.asarray(w["L0_cond_o_w"]).T, "o_b": w["L0_cond_o_b"],
        "w_2_t": np.asarray(w["L2_cond_weight"]).T, "bias_2": w["L2_cond_bias"],
        "dec_w": dec[:, :F * RANK].reshape(S, F, RANK).transpose(2, 0, 1),
        "dec_b": dec_b[:F * RANK].reshape(F, RANK),
        "dec_last_w": dec[:, F * RANK:], "dec_last_b": dec_b[F * RANK:].reshape(RANK, 1),
        "V": w["L1_cond_V"],
        "path": np.concatenate([w["L3_cond_pw_g"], w["L3_cond_pw_b"]], axis=1),
        "comp": np.concatenate([w["L3_cond_cp_g"], w["L3_cond_tm_g"]], axis=1),
        "scale": w["L3_cond_ms_g"],
        "codes": codes,
        "ident": np.eye(P, dtype=np.float32),
        "mask_l": np.stack([np.ones(P, np.float32), sign]),
        "mask_r": np.stack([np.full(F, -BIG, np.float32), (BIG * columns).astype(np.float32)]),
    }
    for name in ("int_W1", "int_b1", "int_W2", "int_b2", "int_g", "int_be", "aw",
                 *(f"{m}_{v}" for m in MLPS for v in ("W1", "W2"))):
        arrays[name] = w[f"L3_cond_{name}"]
    arrays = {k: np.ascontiguousarray(a) for k, a in arrays.items()}
    nc = bacc.Bacc("TRN2", target_bir_lowering=False, num_devices=1)
    I = {k: nc.dram_tensor(f"in_{k}", a.shape, mybir.dt.from_np(a.dtype), kind="ExternalInput").ap() for k, a in arrays.items()}
    out = nc.dram_tensor("out", (B * N, F), F32, kind="ExternalOutput").ap()
    program(nc, I, out)
    got = run(nc, [{f"in_{k}": a for k, a in arrays.items()}], core_ids=[0]).results[0]["out"]
    return got.reshape(B, N, F)
```
